# Optimizing a Trainium2 kernel written in Bass

```python
import numpy as np
import jax
import jax.numpy as jnp

def _softmax(x, axis=-1):
    return jax.nn.softmax(x, axis=axis)

def _gelu(x):
    return jax.nn.gelu(x, approximate=True)

def _silu(x):
    return jax.nn.silu(x)

def _sigmoid(x):
    return jax.nn.sigmoid(x)

def _layernorm(x, axis=-1, eps=1e-05):
    m = jnp.mean(x, axis=axis, keepdims=True)
    v = jnp.var(x, axis=axis, keepdims=True)
    return (x - m) / jnp.sqrt(v + eps)

def _scatter_add(tgt, idx, src, axis=0):
    return tgt.at[idx].add(src)

def _segment_sum(src, seg, n):
    return jax.ops.segment_sum(src, seg, n)
kernel_name = 'mk_macaron_d1_jaxref_r4_7d0880'

def setup_inputs(seed: int=0):
    np.random.seed(seed)
    _w = jnp.asarray

    def _L0_attn_setup():
        import jax, jax.numpy as jnp
        import numpy as np
        B, T, D, H = (8, 1024, 256, 16)
        DK = D // H
        CHUNK = 64
        E, TOPK, MULT, CAPF = (8, 2, 4, 1.25)
        HID = D * MULT
        N = B * T
        CAPACITY = int(CAPF * (N / E))

        def rmsnorm(x, scale):
            return x / jnp.sqrt(jnp.mean(x * x, axis=-1, keepdims=True)) * scale

        def apply_rope(x):
            half = x.shape[-1] // 2
            t = x.shape[2]
            inv = 1.0 / 10000.0 ** (jnp.arange(half, dtype=jnp.float32) / half)
            ang = jnp.arange(t, dtype=jnp.float32)[:, None] * inv[None, :]
            sin, cos = (jnp.sin(ang)[None, None], jnp.cos(ang)[None, None])
            x1, x2 = (x[..., :half], x[..., half:])
            return jnp.concatenate([x1 * cos - x2 * sin, x1 * sin + x2 * cos], axis=-1)

        def phi(x):
            return jax.nn.elu(x) + 1.0

        def attention(x, Wq, bq, Wk, bk, Wv, bv, Wg, bg, Wo, bo):
            b, t, c = x.shape
            heads = lambda y: y.reshape(b, t, H, DK).transpose(0, 2, 1, 3)
            q = phi(apply_rope(heads(x @ Wq + bq)))
            k = phi(apply_rope(heads(x @ Wk + bk)))
            v = heads(x @ Wv + bv)
            g = heads(jax.nn.sigmoid(x @ Wg + bg))
            nc = t // CHUNK
            to_chunks = lambda y: y.reshape(b, H, nc, CHUNK, DK).transpose(2, 0, 1, 3, 4)
            qs, ks_, vs, gs = map(to_chunks, (q, k, v, g))
            S0 = jnp.zeros((b, H, DK, DK), x.dtype)
            Z0 = jnp.zeros((b, H, DK), x.dtype)

            def step(carry, inp):
                S, Z = carry
                qc, kc, vc, gc = inp
                S = S + jnp.einsum('bhtd,bhte->bhde', kc, vc)
                Z = Z + kc.sum(axis=2)
                num = jnp.einsum('bhtd,bhde->bhte', qc, S)
                den = jnp.einsum('bhtd,bhd->bht', qc, Z)[..., None] + 1e-06
                return ((S, Z), gc * (num / den))
            _, outs = jax.lax.scan(step, (S0, Z0), (qs, ks_, vs, gs))
            out = outs.transpose(1, 2, 0, 3, 4).reshape(b, H, t, DK)
            out = out.transpose(0, 2, 1, 3).reshape(b, t, c)
            return out @ Wo + bo

        def moe(x, router_W, router_b, W1, b1, W2, b2):
            b, t, c = x.shape
            n = b * t
            xf = x.reshape(n, c)
            probs = jax.nn.softmax(xf @ router_W + router_b, axis=-1)
            topk_probs, topk_idx = jax.lax.top_k(probs, TOPK)
            topk_probs = topk_probs / topk_probs.sum(axis=-1, keepdims=True)
            out = jnp.zeros_like(xf)
            load = []
            for eid in range(E):
                mask = (topk_idx == eid).reshape(-1)
                idx = jnp.nonzero(mask, size=CAPACITY, fill_value=n * TOPK)[0]
                valid = idx < n * TOPK
                idxc = jnp.minimum(idx, n * TOPK - 1)
                tok, choice = (idxc // TOPK, idxc % TOPK)
                h = jax.nn.gelu(xf[tok] @ W1[eid] + b1[eid], approximate=False) @ W2[eid] + b2[eid]
                gate = jnp.where(valid, topk_probs[tok, choice], 0.0)
                out = out.at[tok].add(gate[:, None] * h)
                load.append(jnp.minimum(mask.sum(), CAPACITY).astype(xf.dtype))
            load = jnp.stack(load)
            importance = probs.sum(axis=0)
            importance = importance / importance.sum()
            load = load / load.sum()
            aux = (importance * load).sum() * E ** 2
            return (out.reshape(b, t, c), aux)

        def _reference_tuple_inner(x, norm1_scale, norm2_scale, Wq, bq, Wk, bk, Wv, bv, Wg, bg, Wo, bo, router_W, router_b, W1, b1, W2, b2):
            x = x + attention(rmsnorm(x, norm1_scale), Wq, bq, Wk, bk, Wv, bv, Wg, bg, Wo, bo)
            moe_out, aux = moe(rmsnorm(x, norm2_scale), router_W, router_b, W1, b1, W2, b2)
            return (x + moe_out, aux)
        key = jax.random.key(seed)
        ks = jax.random.split(key, 16)
        s = 0.02
        r = lambda k, shape: jax.random.normal(k, shape, jnp.float32) * s
        return {'x': jax.random.normal(ks[0], (B, T, D), jnp.float32), 'norm1_scale': jnp.ones((D,), jnp.float32), 'norm2_scale': jnp.ones((D,), jnp.float32), 'Wq': r(ks[1], (D, D)), 'bq': jnp.zeros((D,), jnp.float32), 'Wk': r(ks[2], (D, D)), 'bk': jnp.zeros((D,), jnp.float32), 'Wv': r(ks[3], (D, D)), 'bv': jnp.zeros((D,), jnp.float32), 'Wg': r(ks[4], (D, D)), 'bg': jnp.zeros((D,), jnp.float32), 'Wo': r(ks[5], (D, D)), 'bo': jnp.zeros((D,), jnp.float32), 'router_W': r(ks[6], (D, E)), 'router_b': jnp.zeros((E,), jnp.float32), 'W1': r(ks[7], (E, D, HID)), 'b1': jnp.zeros((E, HID), jnp.float32), 'W2': r(ks[8], (E, HID, D)), 'b2': jnp.zeros((E, D), jnp.float32)}
    _L0_attn_in = _L0_attn_setup()

    def _L0_ffn_setup():
        import jax, jax.numpy as jnp
        import numpy as np
        import math
        E = 16
        TOP_K = 2
        D = 256
        F = 1024
        SH = 512
        key = jax.random.key(seed)
        ks = jax.random.split(key, 10)
        s = lambda k, shape, fan: jax.random.normal(k, shape, jnp.float32) / np.sqrt(fan)
        return {'x': jax.random.normal(ks[0], (32, 64, D), jnp.float32), 'gate_w': s(ks[1], (E, D), D), 'up_w': s(ks[2], (E, F, D), D), 'up_b': s(ks[3], (E, F), D), 'gw': s(ks[4], (E, F, D), D), 'gb': s(ks[5], (E, F), D), 'down_w': s(ks[6], (E, D, F), F), 'down_b': s(ks[7], (E, D), F), 'sh_gate_w': s(ks[8], (SH, D), D), 'sh_up_w': s(ks[9], (SH, D), D), 'sh_down_w': s(jax.random.fold_in(key, 11), (D, SH), SH)}
    _L0_ffn_in = _L0_ffn_setup()
    _d = {'L0_attn_x': _L0_attn_in['x'], 'L0_attn_norm1_scale': _L0_attn_in['norm1_scale'], 'L0_attn_norm2_scale': _L0_attn_in['norm2_scale'], 'L0_attn_Wq': _L0_attn_in['Wq'], 'L0_attn_bq': _L0_attn_in['bq'], 'L0_attn_Wk': _L0_attn_in['Wk'], 'L0_attn_bk': _L0_attn_in['bk'], 'L0_attn_Wv': _L0_attn_in['Wv'], 'L0_attn_bv': _L0_attn_in['bv'], 'L0_attn_Wg': _L0_attn_in['Wg'], 'L0_attn_bg': _L0_attn_in['bg'], 'L0_attn_Wo': _L0_attn_in['Wo'], 'L0_attn_bo': _L0_attn_in['bo'], 'L0_attn_router_W': _L0_attn_in['router_W'], 'L0_attn_router_b': _L0_attn_in['router_b'], 'L0_attn_W1': _L0_attn_in['W1'], 'L0_attn_b1': _L0_attn_in['b1'], 'L0_attn_W2': _L0_attn_in['W2'], 'L0_attn_b2': _L0_attn_in['b2'], 'L0_ffn_gate_w': _L0_ffn_in['gate_w'], 'L0_ffn_up_w': _L0_ffn_in['up_w'], 'L0_ffn_up_b': _L0_ffn_in['up_b'], 'L0_ffn_gw': _L0_ffn_in['gw'], 'L0_ffn_gb': _L0_ffn_in['gb'], 'L0_ffn_down_w': _L0_ffn_in['down_w'], 'L0_ffn_down_b': _L0_ffn_in['down_b'], 'L0_ffn_sh_gate_w': _L0_ffn_in['sh_gate_w'], 'L0_ffn_sh_up_w': _L0_ffn_in['sh_up_w'], 'L0_ffn_sh_down_w': _L0_ffn_in['sh_down_w']}
    _x0 = _d['L0_attn_x']
    _d['L0_attn_x'] = jax.random.normal(jax.random.fold_in(jax.random.key(seed), 1), (2, 2048, 256), dtype=_x0.dtype)
    del _x0
    return _d

def reference(L0_attn_x, L0_attn_norm1_scale, L0_attn_norm2_scale, L0_attn_Wq, L0_attn_bq, L0_attn_Wk, L0_attn_bk, L0_attn_Wv, L0_attn_bv, L0_attn_Wg, L0_attn_bg, L0_attn_Wo, L0_attn_bo, L0_attn_router_W, L0_attn_router_b, L0_attn_W1, L0_attn_b1, L0_attn_W2, L0_attn_b2, L0_ffn_gate_w, L0_ffn_up_w, L0_ffn_up_b, L0_ffn_gw, L0_ffn_gb, L0_ffn_down_w, L0_ffn_down_b, L0_ffn_sh_gate_w, L0_ffn_sh_up_w, L0_ffn_sh_down_w):

    def _L0_attn_ref(x, norm1_scale, norm2_scale, Wq, bq, Wk, bk, Wv, bv, Wg, bg, Wo, bo, router_W, router_b, W1, b1, W2, b2):
        import jax, jax.numpy as jnp
        import numpy as np
        B, T, D, H = (8, 1024, 256, 16)
        DK = D // H
        CHUNK = 64
        E, TOPK, MULT, CAPF = (8, 2, 4, 1.25)
        HID = D * MULT
        N = B * T
        CAPACITY = int(CAPF * (N / E))

        def rmsnorm(x, scale):
            return x / jnp.sqrt(jnp.mean(x * x, axis=-1, keepdims=True)) * scale

        def apply_rope(x):
            half = x.shape[-1] // 2
            t = x.shape[2]
            inv = 1.0 / 10000.0 ** (jnp.arange(half, dtype=jnp.float32) / half)
            ang = jnp.arange(t, dtype=jnp.float32)[:, None] * inv[None, :]
            sin, cos = (jnp.sin(ang)[None, None], jnp.cos(ang)[None, None])
            x1, x2 = (x[..., :half], x[..., half:])
            return jnp.concatenate([x1 * cos - x2 * sin, x1 * sin + x2 * cos], axis=-1)

        def phi(x):
            return jax.nn.elu(x) + 1.0

        def attention(x, Wq, bq, Wk, bk, Wv, bv, Wg, bg, Wo, bo):
            b, t, c = x.shape
            heads = lambda y: y.reshape(b, t, H, DK).transpose(0, 2, 1, 3)
            q = phi(apply_rope(heads(x @ Wq + bq)))
            k = phi(apply_rope(heads(x @ Wk + bk)))
            v = heads(x @ Wv + bv)
            g = heads(jax.nn.sigmoid(x @ Wg + bg))
            nc = t // CHUNK
            to_chunks = lambda y: y.reshape(b, H, nc, CHUNK, DK).transpose(2, 0, 1, 3, 4)
            qs, ks_, vs, gs = map(to_chunks, (q, k, v, g))
            S0 = jnp.zeros((b, H, DK, DK), x.dtype)
            Z0 = jnp.zeros((b, H, DK), x.dtype)

            def step(carry, inp):
                S, Z = carry
                qc, kc, vc, gc = inp
                S = S + jnp.einsum('bhtd,bhte->bhde', kc, vc)
                Z = Z + kc.sum(axis=2)
                num = jnp.einsum('bhtd,bhde->bhte', qc, S)
                den = jnp.einsum('bhtd,bhd->bht', qc, Z)[..., None] + 1e-06
                return ((S, Z), gc * (num / den))
            _, outs = jax.lax.scan(step, (S0, Z0), (qs, ks_, vs, gs))
            out = outs.transpose(1, 2, 0, 3, 4).reshape(b, H, t, DK)
            out = out.transpose(0, 2, 1, 3).reshape(b, t, c)
            return out @ Wo + bo

        def moe(x, router_W, router_b, W1, b1, W2, b2):
            b, t, c = x.shape
            n = b * t
            xf = x.reshape(n, c)
            probs = jax.nn.softmax(xf @ router_W + router_b, axis=-1)
            topk_probs, topk_idx = jax.lax.top_k(probs, TOPK)
            topk_probs = topk_probs / topk_probs.sum(axis=-1, keepdims=True)
            out = jnp.zeros_like(xf)
            load = []
            for eid in range(E):
                mask = (topk_idx == eid).reshape(-1)
                idx = jnp.nonzero(mask, size=CAPACITY, fill_value=n * TOPK)[0]
                valid = idx < n * TOPK
                idxc = jnp.minimum(idx, n * TOPK - 1)
                tok, choice = (idxc // TOPK, idxc % TOPK)
                h = jax.nn.gelu(xf[tok] @ W1[eid] + b1[eid], approximate=False) @ W2[eid] + b2[eid]
                gate = jnp.where(valid, topk_probs[tok, choice], 0.0)
                out = out.at[tok].add(gate[:, None] * h)
                load.append(jnp.minimum(mask.sum(), CAPACITY).astype(xf.dtype))
            load = jnp.stack(load)
            importance = probs.sum(axis=0)
            importance = importance / importance.sum()
            load = load / load.sum()
            aux = (importance * load).sum() * E ** 2
            return (out.reshape(b, t, c), aux)

        def _reference_tuple_inner(x, norm1_scale, norm2_scale, Wq, bq, Wk, bk, Wv, bv, Wg, bg, Wo, bo, router_W, router_b, W1, b1, W2, b2):
            x = x + attention(rmsnorm(x, norm1_scale), Wq, bq, Wk, bk, Wv, bv, Wg, bg, Wo, bo)
            moe_out, aux = moe(rmsnorm(x, norm2_scale), router_W, router_b, W1, b1, W2, b2)
            return (x + moe_out, aux)
        return _reference_tuple_inner(x, norm1_scale, norm2_scale, Wq, bq, Wk, bk, Wv, bv, Wg, bg, Wo, bo, router_W, router_b, W1, b1, W2, b2)[0]

    def _L0_ffn_ref(x, gate_w, up_w, up_b, gw, gb, down_w, down_b, sh_gate_w, sh_up_w, sh_down_w):
        import jax, jax.numpy as jnp
        import numpy as np
        import math
        E = 16
        TOP_K = 2
        D = 256
        F = 1024
        SH = 512
        B, S, Dm = x.shape
        h = x.reshape(-1, Dm)
        T = h.shape[0]
        scores = jax.nn.sigmoid(h @ gate_w.T)
        cap = math.ceil(T / E * TOP_K)
        topk_score, topk_ids = jax.lax.top_k(scores.T, cap)
        xin = h[topk_ids]
        up = jnp.einsum('ecd,efd->ecf', xin, up_w) + up_b[:, None, :]
        g = jnp.einsum('ecd,efd->ecf', xin, gw) + gb[:, None, :]
        eo = jax.nn.silu(g) * up
        eo = jnp.einsum('ecf,edf->ecd', eo, down_w) + down_b[:, None, :]
        flat = (eo * topk_score[..., None]).reshape(-1, Dm)
        out = jnp.zeros_like(h).at[topk_ids.reshape(-1)].add(flat)
        out = out.reshape(B, S, Dm)
        shared = jax.nn.silu(jnp.einsum('bsd,fd->bsf', x, sh_gate_w)) * jnp.einsum('bsd,fd->bsf', x, sh_up_w)
        shared = jnp.einsum('bsf,df->bsd', shared, sh_down_w)
        return out + shared
    x = L0_attn_x
    x = x + 0.5 * _L0_ffn_ref(_layernorm(x, axis=-1), L0_ffn_gate_w, L0_ffn_up_w, L0_ffn_up_b, L0_ffn_gw, L0_ffn_gb, L0_ffn_down_w, L0_ffn_down_b, L0_ffn_sh_gate_w, L0_ffn_sh_up_w, L0_ffn_sh_down_w)
    x = x + _L0_attn_ref(_layernorm(x, axis=-1), L0_attn_norm1_scale, L0_attn_norm2_scale, L0_attn_Wq, L0_attn_bq, L0_attn_Wk, L0_attn_bk, L0_attn_Wv, L0_attn_bv, L0_attn_Wg, L0_attn_bg, L0_attn_Wo, L0_attn_bo, L0_attn_router_W, L0_attn_router_b, L0_attn_W1, L0_attn_b1, L0_attn_W2, L0_attn_b2)
    x = x + 0.5 * _L0_ffn_ref(_layernorm(x, axis=-1), L0_ffn_gate_w, L0_ffn_up_w, L0_ffn_up_b, L0_ffn_gw, L0_ffn_gb, L0_ffn_down_w, L0_ffn_down_b, L0_ffn_sh_gate_w, L0_ffn_sh_up_w, L0_ffn_sh_down_w)
    return x

_drawn_inputs = setup_inputs


def setup_inputs(seed=0):
    import zlib

    import numpy as np

    out = dict(_drawn_inputs(seed))
    spreads = {'L0_attn_norm1_scale': (1.0, 0.6),
     'L0_attn_norm2_scale': (1.0, 0.2),
     'L0_attn_bq': (0.0, 2.0),
     'L0_attn_bk': (0.0, 2.0),
     'L0_attn_bv': (0.0, 0.569),
     'L0_attn_bg': (0.0, 0.8),
     'L0_attn_bo': (0.0, 0.1),
     'L0_attn_router_b': (0.0, 0.1),
     'L0_attn_b1': (0.0, 0.423),
     'L0_attn_b2': (0.0, 0.1)}
    factors = {'L0_attn_Wq': 8.0,
     'L0_attn_Wk': 8.0,
     'L0_attn_Wv': 8.0,
     'L0_attn_Wg': 8.0,
     'L0_attn_Wo': 4.945}
    for name, (base, spread) in spreads.items():
        noise = np.random.default_rng([zlib.crc32(name.encode()), seed]).standard_normal(out[name].shape)
        drawn = base * np.exp(spread * noise) if base else spread * noise
        out[name] = jnp.asarray(drawn.astype(out[name].dtype))
    for name, factor in factors.items():
        out[name] = (out[name] * factor).astype(out[name].dtype)
    return out
```

```python
from contextlib import ExitStack

import numpy as np

import concourse.bass as bass
from concourse import mybir

P = 128
ALU = mybir.AluOpType
ACT = mybir.ActivationFunctionType
AX = mybir.AxisListType
F32 = mybir.dt.float32
F32R = mybir.dt.float32r
BF16 = mybir.dt.bfloat16
I32 = mybir.dt.int32
U32 = mybir.dt.uint32
ds = bass.ds

BATCH, SEQ, D = 2, 2048, 256
N = BATCH * SEQ
T = N // P
K = D // P
EPS = 1e-5

FFN_E, FFN_F, FFN_CAP, SHARED_F = 16, 1024, N // 16 * 2, 512
MOE_E, MOE_F, MOE_CAP = 8, 1024, int(1.25 * (8 * 1024 / 8))
HEADS, DK, CHUNK = 16, 16, 64
HALF = P // DK

GT = 4
G = T // GT
W_RING = 4
SEARCH = 4 * G
IDC = 5

C_IDENT, C_TRI, C_IOTA = 0, P, 2 * P
C_TILE = 3 * P
C_SLOTHI = C_TILE + T
C_RESET = C_SLOTHI + 16
C_ROW = C_RESET + T
C_MASK = C_ROW + 1
C_ALL = C_MASK + P + HALF


class Scope(ExitStack):

    def __init__(self, nc, tag):
        super().__init__()
        self.nc, self.tag, self.sems = nc, tag, []
        self.callback(self.clear)

    def sb(self, name, shape, dt=F32):
        return self.enter_context(self.nc.sbuf_tensor(f"{self.tag}_{name}", shape, dt))

    def ps(self, name, shape=(P, 512), dt=F32):
        return self.enter_context(self.nc.psum_tensor(f"{self.tag}_{name}", list(shape), dt))

    def sem(self, name):
        self.sems.append(self.nc.alloc_semaphore(name=f"{self.tag}_{name}"))
        return self.sems[-1]

    def clear(self):
        if self.sems:
            self.nc.clear_and_free_semaphores(self.sems)
            self.nc.all_engine_barrier()


class Chain:

    def __init__(self, eng, sem):
        self.eng, self.sem, self.base, self.n = eng, sem, 0, 0

    def at(self, base):
        self.base, self.n = base, 0

    def step(self, ins, apart=False):
        ins.then_inc(self.sem, 1)
        self.n += 1
        if apart:
            wait_apart(self.eng, self.sem, self.base + self.n)
        else:
            self.eng.wait_ge(self.sem, self.base + self.n)


def wait_apart(eng, sem, value):
    eng.wait_ge(sem, value)
    eng.nop(nofuse=True)


def product(pe, out, left, right, first, last):
    (lh, ll), (rh, rl) = left, right
    pe.matmul(out, lh, rh, start=first, stop=False, skip_group_check=True)
    pe.matmul(out, lh, rl, start=False, stop=False, skip_group_check=True)
    return pe.matmul(out, ll, rh, start=False, stop=last, skip_group_check=True)


def as_f32(ap):
    return ap.bitcast(F32)


def norm_and_score(nc, tag, x_in, gate_w, consts, h_rows, x_all, ht_hi, ht_lo, logits):
    E = gate_w.shape[2]
    with Scope(nc, tag) as s:
        ident = s.sb("ident", [P, P])
        gate = s.sb("gate", [P, K, E])
        neg_half = s.sb("neg_half", [P, GT])
        stats = s.sb("stats", [P, 2, GT, 6])
        mv = s.sb("mv", [P, 2, GT, 2])
        var_eps = s.sb("var_eps", [P, 2, GT])
        rstd = s.sb("rstd", [P, 2, GT])
        h = s.sb("h", [P, 2, GT, D])
        ht = s.sb("ht", [P, 2, K, GT * P])
        turned = [s.ps(f"turned{b}", (P, K, GT * P)) for b in range(2)]
        scored = [s.ps(f"scored{b}", (P, GT, E)) for b in range(2)]
        const_in, x_in_s = s.sem("const_in"), [s.sem(f"x_in{b}") for b in range(2)]
        stat_done, rstd_done, h_done = s.sem("stat_done"), s.sem("rstd_done"), s.sem("h_done")
        h_out = [s.sem(f"h_out{b}") for b in range(2)]
        turn_done, ht_done, hi_done = s.sem("turn_done"), s.sem("ht_done"), s.sem("hi_done")
        lo_done, score_done, logit_done = s.sem("lo_done"), s.sem("score_done"), s.sem("logit_done")
        dve_own, pool_own = s.sem("dve_own"), s.sem("pool_own")
        block = s.enter_context(nc.Block())

        @block.sync
        def _(sp):
            sp.dma_start(ident[:], consts[:, C_IDENT:C_IDENT + P]).then_inc(const_in, 16)
            sp.dma_start(gate[:], gate_w).then_inc(const_in, 16)
            with sp.Fori(0, G // 2) as i:
                for b in range(2):
                    g = i * 2 + b
                    sp.wait_ge(h_done, g + 1)
                    sp.dma_start(x_all[:, ds(g * GT, GT), :],
                                 x_in[ds(g * (GT * P), GT * P), :].rearrange("(t p) d -> p t d", p=P)
                                 ).then_inc(x_in_s[b], 16)

        @block.gpsimd
        def _(pool):
            own = Chain(pool, pool_own)
            own.step(pool.memset(neg_half[:], -0.5))
            with pool.Fori(0, G // 2) as i:
                for b in range(2):
                    g = i * 2 + b
                    own.at(g + 1)
                    wait_apart(pool, stat_done, g + 1)
                    own.step(pool.tensor_scalar(var_eps[:, b], mv[:, b, :, 1], EPS, None, ALU.add))
                    pool.tensor_tensor(rstd[:, b], var_eps[:, b], neg_half[:], ALU.pow).then_inc(rstd_done, 1)

        @block.tensor
        def _(pe):
            pe.wait_ge(const_in, 32)
            with pe.Fori(0, G // 2) as i:
                for b in range(2):
                    g = i * 2 + b
                    pe.wait_ge(h_done, g + 3)
                    pe.wait_ge(lo_done, g + 1)
                    for k in range(K):
                        for t in range(GT):
                            last = pe.transpose(turned[b][:, k, t * P:(t + 1) * P],
                                                h[:, b, t, k * P:(k + 1) * P], ident[:])
                    last.then_inc(turn_done, 1)
                    pe.wait_ge(ht_done, g + 1)
                    pe.wait_ge(logit_done, g + 1)
                    for t in range(GT):
                        for k in range(K):
                            last = pe.matmul(scored[b][:, t, :], ht[:, b, k, t * P:(t + 1) * P],
                                             gate[:, k, :], start=(k == 0), stop=(k == K - 1))
                    last.then_inc(score_done, 1)

        @block.scalar
        def _(act):
            with act.Fori(0, G // 2) as i:
                for b in range(2):
                    g = i * 2 + b
                    act.wait_ge(turn_done, g + 3)
                    act.wait_ge(score_done, g + 1)
                    for k in range(K):
                        last = act.copy(ht[:, b, k, :], turned[b][:, k, :])
                    last.then_inc(ht_done, 1)
                    for k in range(K):
                        last = act.copy(ht_hi[:, k, ds(g * (GT * P), GT * P)], turned[b][:, k, :])
                    last.then_inc(hi_done, 1)
                    act.wait_ge(h_done, g + 3)
                    act.dma_start(h_rows[ds(g * (GT * P), GT * P), :].rearrange("(t p) d -> p t d", p=P),
                                  h[:, b]).then_inc(h_out[b], 16)
            for b in range(2):
                act.wait_ge(h_out[b], 16 * (G // 2) + 16)

        @block.vector
        def _(dve):
            dve.sem_inc(h_done, 2)
            dve.sem_inc(lo_done, 2)
            dve.sem_inc(turn_done, 2)
            dve.sem_inc(logit_done, 2)
            dve.sem_inc(score_done, 2)
            for b in range(2):
                dve.sem_inc(h_out[b], 16)
            own = Chain(dve, dve_own)
            with dve.Fori(0, G // 2) as i:
                for b in range(2):
                    g = i * 2 + b
                    own.at(g)
                    dve.wait_ge(x_in_s[b], i * 16 + 16)
                    for t in range(GT):
                        last = dve.bn_stats(stats[:, b, t], x_all[:, ds(g * GT + t, 1), :].rearrange("p t d -> p (t d)"))
                    own.step(last, apart=True)
                    for t in range(GT):
                        last = dve.bn_aggr(mv[:, b, t], stats[:, b, t])
                    last.then_inc(stat_done, 1)
                    dve.wait_ge(stat_done, g + 1)
                    dve.wait_ge(rstd_done, g + 1)
                    dve.wait_ge(h_out[b], i * 16 + 16)
                    dve.wait_ge(turn_done, g + 1)
                    for t in range(GT):
                        last = dve.tensor_scalar(h[:, b, t], x_all[:, ds(g * GT + t, 1), :].rearrange("p t d -> p (t d)"),
                                                 mv[:, b, t, 0:1], rstd[:, b, t:t + 1], ALU.subtract, ALU.mult)
                    last.then_inc(h_done, 1)
                    dve.wait_ge(hi_done, g + 1)
                    for k in range(K):
                        at = ds(g * (GT * P), GT * P)
                        last = dve.tensor_tensor(ht_lo[:, k, at], turned[b][:, k, :], as_f32(ht_hi[:, k, at]),
                                                 ALU.subtract)
                    last.then_inc(lo_done, 1)
                    dve.wait_ge(score_done, g + 3)
                    dve.tensor_copy(logits[:, :, ds(g * GT, GT)],
                                    scored[b][:].rearrange("p t e -> p e t")).then_inc(logit_done, 1)
            dve.wait_ge(logit_done, G + 2)


def shared_and_search(nc, tag, w_dram, consts, x_all, ht_hi, ht_lo, logits, low, high, acc_out):
    E = FFN_E
    F_T = SHARED_F // P
    W = (2 * K) * P + D
    with Scope(nc, tag) as s:
        raw = s.sb("raw", [P, F_T, W])
        w_hi, w_lo = s.sb("w_hi", [P, F_T, W], F32R), s.sb("w_lo", [P, F_T, W], F32R)
        ones = s.sb("ones", [P, P], BF16)
        at_least = s.sb("at_least", [P, E, T], BF16)
        part = s.sb("part", [P, E])
        part_b = s.sb("part_b", [P, E], BF16)
        ends = s.sb("ends", [P, 2, E])
        ends_all = s.sb("ends_all", [P, 2, E])
        size = s.sb("size", [P, E])
        both = s.sb("both", [P, E])
        mid = s.sb("mid", [P, E])
        enough, short = s.sb("enough", [P, E], I32), s.sb("short", [P, E], I32)
        silu = s.sb("silu", [P, 2, 512])
        act_f = s.sb("act_f", [P, 512])
        act_hi, act_lo = s.sb("act_hi", [P, 2, 512], F32R), s.sb("act_lo", [P, 2, 512], F32R)
        out = s.sb("out", [P, 2, GT, D])
        ps_gate = [s.ps(f"gate{b}") for b in range(2)]
        ps_up = [s.ps(f"up{b}") for b in range(2)]
        ps_down = s.ps("down", (P, GT, D))
        ps_count = s.ps("count", (P, E))
        w_in, w_hi_done, w_lo_done = s.sem("w_in"), s.sem("w_hi_done"), s.sem("w_lo_done")
        ones_done, ends_done, ends_all_done = s.sem("ones_done"), s.sem("ends_done"), s.sem("ends_all_done")
        gu_done, silu_done, act_done, down_done = (s.sem(n) for n in ("gu_done", "silu_done", "act_done", "down_done"))
        part_done, count_done, out_done = s.sem("part_done"), s.sem("count_done"), s.sem("out_done")
        out_stored = [s.sem(f"out_stored{b}") for b in range(2)]
        dve_own = s.sem("dve_own")
        block = s.enter_context(nc.Block())

        @block.sync
        def _(sp):
            sp.dma_start(raw[:], w_dram.rearrange("f p w -> p f w")).then_inc(w_in, 16)
            with sp.Fori(0, G // 2) as i:
                for b in range(2):
                    g = i * 2 + b
                    sp.wait_ge(out_done, g + 2)
                    sp.dma_start(acc_out[ds(g * (GT * P), GT * P), :].rearrange("(t p) d -> p t d", p=P),
                                 out[:, b]).then_inc(out_stored[b], 16)
            for b in range(2):
                sp.wait_ge(out_stored[b], 16 * (G // 2) + 16)

        @block.gpsimd
        def _(pool):
            pool.wait_ge(w_hi_done, 1)
            for f in range(F_T):
                last = pool.tensor_tensor(w_lo[:, f], raw[:, f], as_f32(w_hi[:, f]), ALU.subtract)
            last.then_inc(w_lo_done, 1)
            pool.wait_ge(ends_done, 1)
            pool.partition_all_reduce(ends_all[:].rearrange("p a e -> p (a e)"),
                                      ends[:].rearrange("p a e -> p (a e)"), P,
                                      bass.bass_isa.ReduceOp.max).then_inc(ends_all_done, 1)

        @block.tensor
        def _(pe):
            pe.wait_ge(w_lo_done, 1)
            pe.wait_ge(ones_done, 1)

            def down(g, n, f):
                pe.wait_ge(act_done, n + 3)
                if f == 0:
                    pe.wait_ge(out_done, g + 1)
                for t in range(GT):
                    last = product(pe, ps_down[:, t, :],
                                   [a[:, f % 2, t * P:(t + 1) * P] for a in (act_hi, act_lo)],
                                   [w[:, f, 2 * K * P:] for w in (w_hi, w_lo)],
                                   f == 0 and t % 2 == 0, f == F_T - 1)
                last.then_inc(down_done, 1)

            with pe.Fori(0, G // 2) as i:
                for b in range(2):
                    g = i * 2 + b
                    for f in range(F_T):
                        n = g * F_T + f
                        pe.wait_ge(act_done, n + 1)
                        for j, ps in enumerate((ps_gate, ps_up)):
                            for k in range(K):
                                w0 = (j * K + k) * P
                                last = product(pe, ps[f % 2][:], [w[:, f, w0:w0 + P] for w in (w_hi, w_lo)],
                                               [h[:, k, ds(g * (GT * P), GT * P)] for h in (ht_hi, ht_lo)],
                                               k == 0, k == K - 1)
                        last.then_inc(gu_done, 1)
                        pe.wait_ge(part_done, n + 1)
                        pe.matmul(ps_count[:], ones[:], part_b[:], start=True, stop=True).then_inc(count_done, 1)
                        if f:
                            down(g, n - 1, f - 1)
                    down(g, g * F_T + F_T - 1, F_T - 1)

        @block.scalar
        def _(act):
            act.wait_ge(w_in, 16)
            for f in range(F_T):
                last = act.copy(w_hi[:, f], raw[:, f])
            last.then_inc(w_hi_done, 1)
            with act.Fori(0, G // 2) as i:
                for b in range(2):
                    for f in range(F_T):
                        n = (i * 2 + b) * F_T + f
                        act.wait_ge(gu_done, n + 1)
                        act.wait_ge(act_done, n + 1)
                        act.activation(silu[:, f % 2], ps_gate[f % 2][:], ACT.Silu).then_inc(silu_done, 1)

        @block.vector
        def _(dve):
            own = Chain(dve, dve_own)
            dve.sem_inc(act_done, 2)
            dve.sem_inc(down_done, 2)
            dve.sem_inc(out_done, 1)
            for b in range(2):
                dve.sem_inc(out_stored[b], 16)
            dve.memset(ones[:], 1.0).then_inc(ones_done, 1)
            own.step(dve.tensor_reduce(ends[:, 0], logits[:], AX.X, ALU.max))
            own.step(dve.tensor_reduce(ends[:, 1], logits[:], AX.X, ALU.min))
            dve.tensor_scalar(ends[:, 1], ends[:, 1], -1.0, None, ALU.mult).then_inc(ends_done, 1)
            dve.wait_ge(ends_all_done, 1)
            own.step(dve.tensor_scalar(low[:], ends_all[:, 1], -1.0, None, ALU.mult))
            own.step(dve.scalar_tensor_tensor(size[:], ends_all[:, 0], -1.0, ends_all[:, 0], ALU.mult, ALU.max))
            own.step(dve.tensor_scalar(size[:], size[:], 2.0 ** -10, 1e-30, ALU.mult, ALU.add))
            own.step(dve.tensor_tensor(high[:], ends_all[:, 0], size[:], ALU.add))
            first = own.n

            def compare():
                own.step(dve.tensor_tensor(both[:], low[:], high[:], ALU.add))
                own.step(dve.tensor_scalar(mid[:], both[:], 0.5, None, ALU.mult))
                own.step(dve.tensor_tensor(at_least[:], logits[:], mid[:].unsqueeze(2).to_broadcast([P, E, T]), ALU.is_ge))
                own.step(dve.tensor_reduce(part[:], at_least[:], AX.X, ALU.add))
                dve.tensor_copy(part_b[:], part[:]).then_inc(part_done, 1)

            def halve(n):
                wait_apart(dve, count_done, n + 1)
                dve.tensor_scalar(enough[:], ps_count[:], float(FFN_CAP) - 0.5, None, ALU.is_ge)
                own.step(dve.tensor_scalar(short[:], ps_count[:], float(FFN_CAP) - 0.5, None, ALU.is_lt), apart=True)
                dve.copy_predicated(low[:], enough[:], mid[:])
                own.step(dve.copy_predicated(high[:], short[:], mid[:]))

            STEP = 4 + 2 + 2
            compare()
            with dve.Fori(0, G // 2) as i:
                for b in range(2):
                    g = i * 2 + b
                    own.at(g * (F_T * STEP + 1) + (first + 4))
                    for f in range(F_T):
                        n = g * F_T + f
                        halve(n)
                        compare()
                        dve.wait_ge(silu_done, n + 1)
                        dve.wait_ge(down_done, n + 1)
                        own.step(dve.tensor_tensor(act_f[:], ps_up[f % 2][:], silu[:, f % 2], ALU.mult))
                        own.step(dve.tensor_copy(act_hi[:, f % 2], act_f[:]))
                        dve.tensor_tensor(act_lo[:, f % 2], act_f[:], as_f32(act_hi[:, f % 2]),
                                          ALU.subtract).then_inc(act_done, 1)
                        dve.wait_ge(act_done, n + 3)
                    dve.wait_ge(down_done, g * F_T + (F_T + 2))
                    dve.wait_ge(out_stored[b], i * 16 + 16)
                    own.step(dve.tensor_scalar(out[:, b].rearrange("p t d -> p (t d)"),
                                               ps_down[:].rearrange("p t d -> p (t d)"), 0.5, None, ALU.mult))
                    dve.tensor_tensor(out[:, b], out[:, b], x_all[:, ds(g * GT, GT), :], ALU.add).then_inc(out_done, 1)


def make_lists(nc, tag, E, NT, consts, logits, low, high, gather_ids, scatter_ids, gate_cols):
    ET = E * T
    HB = 8
    NB = T // HB
    expert_chooses = low is not None
    with Scope(nc, tag) as s:
        cst = s.sb("cst", [P, C_ALL])
        tri, ones, iota = (s.sb(n, [P, P], BF16) for n in ("tri", "ones", "iota"))
        reset, sel, tie, gate, totals, summed, pos, row = (
            s.sb(n, [P, E, T]) for n in ("reset", "sel", "tie", "gate", "totals", "summed", "pos", "row"))
        sel_b, lane_b = s.sb("sel_b", [P, E, T], BF16), s.sb("lane_b", [P, E, T], BF16)
        pos_i, part_i = s.sb("pos_i", [P, E, T], I32), s.sb("part_i", [P, E, T], I32)
        row_hot = s.sb("row_hot", [P, E, T, NT], BF16)
        vals = s.sb("vals", [P, E, T, IDC], BF16)
        moved = s.sb("moved", [P, E, T, NT * IDC], BF16)
        hot = s.sb("hot", [P, 2, HB, P], BF16)
        counts = s.sb("counts", [P, E])
        slots = s.sb("slots", [P, E, NT, IDC])
        idf, tmp = s.sb("idf", [P, E, NT]), s.sb("tmp", [P, E, NT])
        if not expert_chooses:
            slot_no = s.sb("slot_no", [P, E, NT])
            best, best_i = s.sb("best", [P, T, 8]), s.sb("best_i", [P, T, 8], U32)
            best_f = s.sb("best_f", [P, 2, T])
            ratio, share = s.sb("ratio", [P, T]), s.sb("share", [P, 2, T])
        ps_before, ps_total = s.ps("before", (P, E, T)), s.ps("total", (P, E, T))
        PER_BANK = 512 // (NT * IDC)
        n_banks = -(-E // PER_BANK)
        ps_slots = [s.ps(f"slots{i}", (P, PER_BANK, NT * IDC)) for i in range(n_banks)]
        const_in, const_done = s.sem("const_in"), s.sem("const_done")
        sel_done, prefix_done, vals_done = s.sem("sel_done"), s.sem("prefix_done"), s.sem("vals_done")
        hot_done, hot_used = s.sem("hot_done"), s.sem("hot_used")
        gate_asked, gate_ready = s.sem("gate_asked"), s.sem("gate_ready")
        dve_own = s.sem("dve_own")
        block = s.enter_context(nc.Block())
        ROUNDS = 3 if expert_chooses else 1

        @block.sync
        def _(sp):
            sp.dma_start(cst[:], consts).then_inc(const_in, 16)

        @block.scalar
        def _(act):
            if expert_chooses:
                act.activation(gate[:], logits[:], ACT.Sigmoid).then_inc(gate_ready, 1)
            else:
                act.wait_ge(gate_asked, 1)
                act.activation(ratio[:], ratio[:], ACT.Exp).then_inc(gate_ready, 1)

        @block.tensor
        def _(pe):
            pe.wait_ge(const_done, 1)
            flat = sel_b[:].rearrange("p e t -> p (e t)")
            for r in range(ROUNDS):
                pe.wait_ge(sel_done, r + 1)
                pe.matmul(ps_before[:].rearrange("p e t -> p (e t)"), tri[:], flat, start=True, stop=True)
                pe.matmul(ps_total[:].rearrange("p e t -> p (e t)"), ones[:], flat,
                          start=True, stop=True).then_inc(prefix_done, 1)
            pe.wait_ge(vals_done, 1)
            for e in range(E):
                for n in range(NB):
                    m = e * NB + n
                    pe.wait_ge(hot_done, m + 1)
                    for t in range(HB):
                        last = pe.matmul(ps_slots[e // PER_BANK][:, e % PER_BANK, :], hot[:, m % 2, t, :],
                                         moved[:, e, n * HB + t, :], start=(n == 0 and t == 0),
                                         stop=(n == NB - 1 and t == HB - 1))
                    last.then_inc(hot_used, 1)

        @block.vector
        def _(dve):
            own = Chain(dve, dve_own)
            by_expert = [P, E, T]
            dve.wait_ge(const_in, 16)
            dve.tensor_copy(tri[:], cst[:, C_TRI:C_TRI + P])
            dve.memset(ones[:], 1.0)
            dve.tensor_copy(iota[:], cst[:, C_IOTA:C_IOTA + P])
            dve.tensor_copy(reset[:], cst[:, C_RESET:C_RESET + T].unsqueeze(1).to_broadcast(by_expert)
                            ).then_inc(const_done, 1)
            dve.wait_ge(const_done, 1)
            rounds = [0]

            def prefix(chosen):
                rounds[0] += 1
                dve.tensor_copy(sel_b[:], chosen[:]).then_inc(sel_done, 1)
                dve.wait_ge(prefix_done, rounds[0])
                own.step(dve.tensor_copy(totals[:], ps_total[:]))
                own.step(dve.tensor_tensor_scan(summed[:].rearrange("p e t -> p (e t)"),
                                                reset[:].rearrange("p e t -> p (e t)"),
                                                totals[:].rearrange("p e t -> p (e t)"), 0.0, ALU.mult, ALU.add))
                own.step(dve.tensor_tensor(pos[:], summed[:], totals[:], ALU.subtract))
                own.step(dve.tensor_tensor(pos[:], ps_before[:], pos[:], ALU.add))

            if expert_chooses:
                own.step(dve.tensor_tensor(sel[:], logits[:], high[:].unsqueeze(2).to_broadcast(by_expert), ALU.is_ge))
                own.step(dve.tensor_tensor(tie[:], logits[:], low[:].unsqueeze(2).to_broadcast(by_expert), ALU.is_ge))
                own.step(dve.tensor_tensor(tie[:], tie[:], sel[:], ALU.subtract))
                prefix(sel)
                own.step(dve.tensor_scalar(counts[:], summed[:, :, T - 1], -1.0, float(FFN_CAP), ALU.mult, ALU.add))
                prefix(tie)
                own.step(dve.tensor_tensor(pos[:], pos[:], counts[:].unsqueeze(2).to_broadcast(by_expert), ALU.is_lt))
                own.step(dve.tensor_tensor(tie[:], tie[:], pos[:], ALU.mult))
                own.step(dve.tensor_tensor(sel[:], sel[:], tie[:], ALU.add))
                prefix(sel)
                dve.wait_ge(gate_ready, 1)
            else:
                for t in range(T):
                    last = dve.max(best[:, t, :], logits[:, t, :])
                own.step(last)
                for t in range(T):
                    last = dve.max_index(best_i[:, t, :], best[:, t, :], logits[:, t, :])
                own.step(last)
                own.step(dve.tensor_copy(best_f[:], best_i[:, :, 0:2].rearrange("p t c -> p c t")))
                dve.tensor_tensor(ratio[:], best[:, :, 1], best[:, :, 0], ALU.subtract).then_inc(gate_asked, 1)
                dve.wait_ge(gate_ready, 1)
                own.step(dve.tensor_scalar(share[:, 1], ratio[:], 1.0, None, ALU.add))
                own.step(dve.reciprocal(share[:, 0], share[:, 1]))
                own.step(dve.tensor_tensor(share[:, 1], share[:, 0], ratio[:], ALU.mult))
                expert_no = cst[:, C_SLOTHI:C_SLOTHI + E].unsqueeze(2).to_broadcast(by_expert)
                for c, (hot_c, gated) in enumerate(((sel, gate), (tie, row))):
                    own.step(dve.tensor_tensor(hot_c[:], expert_no,
                                               best_f[:, c, :].unsqueeze(1).to_broadcast(by_expert), ALU.is_equal))
                    own.step(dve.tensor_tensor(gated[:], hot_c[:],
                                               share[:, c, :].unsqueeze(1).to_broadcast(by_expert), ALU.mult))
                own.step(dve.tensor_tensor(sel[:], sel[:], tie[:], ALU.add))
                own.step(dve.tensor_tensor(gate[:], gate[:], row[:], ALU.add))
                prefix(sel)
                own.step(dve.tensor_scalar(tie[:], pos[:], float(MOE_CAP) - 0.5, None, ALU.is_lt))
                own.step(dve.tensor_tensor(sel[:], sel[:], tie[:], ALU.mult))
                own.step(dve.tensor_scalar(counts[:], summed[:, :, T - 1], float(MOE_CAP), None, ALU.min))
            own.step(dve.tensor_scalar(pos[:], pos[:], 1.0, None, ALU.add))
            own.step(dve.tensor_tensor(pos[:], pos[:], sel[:], ALU.mult))
            own.step(dve.tensor_scalar(pos_i[:], pos[:], -1.0, None, ALU.add))
            own.step(dve.tensor_scalar(part_i[:], pos_i[:], P - 1, None, ALU.bitwise_and))
            own.step(dve.tensor_copy(lane_b[:], part_i[:]))
            own.step(dve.tensor_scalar(part_i[:], pos_i[:], P.bit_length() - 1, None, ALU.arith_shift_right))
            own.step(dve.tensor_copy(row[:], part_i[:]))
            own.step(dve.tensor_copy(vals[:, :, :, 0], cst[:, C_TILE:C_TILE + T].unsqueeze(1).to_broadcast(by_expert)))
            own.step(dve.tensor_copy(vals[:, :, :, 1], cst[:, C_ROW:C_ROW + 1].unsqueeze(2).to_broadcast(by_expert)))
            for c in range(3):
                own.step(dve.tensor_copy(vals[:, :, :, 2 + c], gate[:]))
                if c < 2:
                    own.step(dve.tensor_tensor(gate[:], gate[:], vals[:, :, :, 2 + c], ALU.subtract))
            for j in range(NT):
                last = dve.tensor_scalar(row_hot[:, :, :, j], row[:], float(j), None, ALU.is_equal)
            own.step(last)
            for j in range(NT):
                last = dve.tensor_tensor(moved[:, :, :, j * IDC:(j + 1) * IDC].rearrange("p e t c -> p (e t) c"),
                                         vals[:].rearrange("p e t c -> p (e t) c"),
                                         row_hot[:, :, :, j].rearrange("p e t -> p (e t)").unsqueeze(2)
                                         .to_broadcast([P, ET, IDC]), ALU.mult)
            last.then_inc(vals_done, 1)
            for e in range(E):
                for n in range(NB):
                    m = e * NB + n
                    if m >= 2:
                        dve.wait_ge(hot_used, m - 1)
                    dve.tensor_tensor(hot[:, m % 2], iota[:].unsqueeze(1).to_broadcast([P, HB, P]),
                                      lane_b[:, e, n * HB:(n + 1) * HB].unsqueeze(2).to_broadcast([P, HB, P]),
                                      ALU.is_equal).then_inc(hot_done, 1)
            dve.wait_ge(hot_used, E * NB)
            for i in range(n_banks):
                e0, e1 = i * PER_BANK, min(E, (i + 1) * PER_BANK)
                last = dve.tensor_copy(slots[:, e0:e1].rearrange("p e j c -> p e (j c)"), ps_slots[i][:, 0:e1 - e0])
            own.step(last)
            own.step(dve.scalar_tensor_tensor(idf[:], slots[:, :, :, 0], float(P), slots[:, :, :, 1], ALU.mult, ALU.add))
            own.step(dve.tensor_copy(gather_ids[:], idf[:]))
            own.step(dve.tensor_tensor(tmp[:], slots[:, :, :, 2], slots[:, :, :, 3], ALU.add))
            own.step(dve.tensor_tensor(gate_cols[:], tmp[:], slots[:, :, :, 4], ALU.add))
            if expert_chooses:
                own.step(dve.tensor_scalar(gate_cols[:], gate_cols[:], 0.5, None, ALU.mult))
            else:
                slot_tiles = cst[:, C_SLOTHI:C_SLOTHI + NT].unsqueeze(1).to_broadcast([P, E, NT])
                own.step(dve.tensor_scalar(slot_no[:], slot_tiles, float(P), cst[:, C_ROW:C_ROW + 1], ALU.mult, ALU.add))
                own.step(dve.tensor_tensor(tmp[:], slot_no[:], counts[:].unsqueeze(2).to_broadcast([P, E, NT]), ALU.is_ge))
                own.step(dve.scalar_tensor_tensor(tmp[:], slot_no[:], float(N), tmp[:], ALU.add, ALU.mult))
                own.step(dve.tensor_tensor(idf[:], idf[:], tmp[:], ALU.add))
            own.step(dve.tensor_copy(scatter_ids[:], idf[:]))


def run_experts(nc, tag, E, NT, gated, w_dram, bias_dram, down_bias, consts, h_rows, acc,
                gather_ids, scatter_ids, gate_cols):
    F_T = FFN_F // P
    CH = [(c, min(c + 4, NT)) for c in range(0, NT, 4)]
    S = F_T * len(CH)
    IN = (2 if gated else 1)
    W = IN * K * P + D
    NI = NT // 2
    NMISC = 2 if gated else 1
    ITEM_AT = {5: 0, 7: 1} if gated else {13: 0, 15: 1, 17: 2, 19: 3, 21: 4}
    AHEAD = 2
    assert len(ITEM_AT) == NI and S % 2 == 0 and F_T % W_RING == 0 and NI % NMISC == 0
    with Scope(nc, tag) as s:
        ident = s.sb("ident", [P, P])
        raw = s.sb("raw", [P, W_RING, W])
        w_hi, w_lo = s.sb("w_hi", [P, W_RING, W], F32R), s.sb("w_lo", [P, W_RING, W], F32R)
        bias = s.sb("bias", [P, 2, IN * F_T])
        db = s.sb("db", [P, 2, D])
        rows = s.sb("rows", [P, NT, D])
        xt_hi = s.sb("xt_hi", [P, 2, K, NT * P], F32R)
        xt_lo = s.sb("xt_lo", [P, 2, K, NT * P], F32R)
        silu = s.sb("silu", [P, 2, 512])
        act_f = s.sb("act_f", [P, 2, 512])
        act_hi, act_lo = s.sb("act_hi", [P, 2, 512], F32R), s.sb("act_lo", [P, 2, 512], F32R)
        out = s.sb("out", [P, 2, NT, D])
        gcol = s.sb("gcol", [P, 2, NT])
        gid, sid = s.sb("gid", [P, NT], U32), s.sb("sid", [P, NT], U32)
        ps_in = [[s.ps(f"in{j}{b}") for j in range(IN)] for b in range(2)]
        ps_down = s.ps("down", (P, NT, D))
        ps_turn = [s.ps(f"turn{m}", (P, K, 2 * P)) for m in range(NMISC)]
        const_in = s.sem("const_in")
        raw_in = [s.sem(f"raw_in{r}") for r in range(W_RING)]
        bias_in = [s.sem(f"bias_in{b}") for b in range(2)]
        raw_hi, raw_lo = s.sem("raw_hi"), s.sem("raw_lo")
        rows_in, turned, xt_done = s.sem("rows_in"), s.sem("turned"), s.sem("xt_done")
        in_done, silu_done, act_done, down_done = (s.sem(n) for n in ("in_done", "silu_done", "act_done", "down_done"))
        read_out, out_done, scattered = s.sem("read_out"), s.sem("out_done"), s.sem("scattered")
        landed = s.sem("landed")
        dve_own, pool_own = s.sem("dve_own"), s.sem("pool_own")
        block = s.enter_context(nc.Block())
        ACT0, DOWN0, RAW0, XT0, READ0 = 2, 4 * len(CH), W_RING, NMISC, 2
        L = F_T * E

        def experts(eng, one):
            with eng.Fori(0, E // 2 - 1) as i:
                one(i * 2, 0, False)
                one(i * 2 + 1, 1, False)
            one(E - 2, 0, False)
            one(E - 1, 1, True)

        @block.sync
        def _(sp):
            sp.dma_start(ident[:], consts[:, C_IDENT:C_IDENT + P]).then_inc(const_in, 16)

            def one(e, b, last):
                sp.wait_ge(read_out, e + 1)
                sp.dma_start(bias[:, b], bias_dram[ds(e, 1)].rearrange("e p c -> (e p) c")).then_inc(bias_in[b], 16)
                sp.dma_start(db[:, b], down_bias[ds(e, 1)].to_broadcast([P, D])).then_inc(bias_in[b], 16)
                for f in range(F_T):
                    sp.wait_ge(raw_hi, e * F_T + (f + 1))
                    sp.wait_ge(raw_lo, e * F_T + (f + 1))
                    sp.dma_start(raw[:, f % W_RING], w_dram[ds(e * F_T + f, 1)].rearrange("s p w -> (s p) w")
                                 ).then_inc(raw_in[f % W_RING], 16)

            experts(sp, one)

        @block.gpsimd
        def _(pool):
            own = Chain(pool, pool_own)
            PER = 2

            def gather(e):
                own.step(pool.tensor_copy(gid[:], gather_ids[:, ds(e, 1), :].rearrange("p e j -> p (e j)")), apart=True)
                for j in range(NT):
                    pool.indirect_dma_start(out=rows[:, j, :], out_offset=None, in_=h_rows,
                                            in_offset=bass.IndirectOffsetOnAxis(ap=gid[:, j:j + 1], axis=0)
                                            ).then_inc(rows_in, 16)

            def low_part(e, f):
                n = e * F_T + f
                pool.wait_ge(raw_hi, n + (RAW0 + 1))
                r = f % W_RING
                pool.tensor_tensor(w_lo[:, r], raw[:, r], as_f32(w_hi[:, r]), ALU.subtract).then_inc(raw_lo, 1)

            gather(0)
            for f in range(AHEAD):
                low_part(0, f)

            def one(e, b, last):
                own.at(e * PER + 1)
                for f in range(F_T):
                    if f + AHEAD < F_T:
                        low_part(e, f + AHEAD)
                    elif not last:
                        low_part(e + 1, f + AHEAD - F_T)
                    if f == 1 and not last:
                        pool.wait_ge(turned, e * NI + NI)
                        wait_apart(pool, rows_in, e * (16 * NT) + 16 * NT)
                        gather(e + 1)
                if last:
                    own.at(e * PER + 1)
                own.step(pool.tensor_copy(sid[:], scatter_ids[:, ds(e, 1), :].rearrange("p e j -> p (e j)")))
                wait_apart(pool, out_done, e + 1)
                for j in range(NT):
                    pool.indirect_dma_start(out=acc, out_offset=bass.IndirectOffsetOnAxis(ap=sid[:, j:j + 1], axis=0),
                                            in_=out[:, b, j, :], in_offset=None, compute_op=ALU.add
                                            ).then_inc(scattered, 16)
                pool.wait_ge(scattered, e * (16 * NT) + 16 * NT)
                pool.nop().then_inc(landed, 1)

            experts(pool, one)

        @block.tensor
        def _(pe):
            pe.wait_ge(const_in, 16)

            def turn(e, i, b):
                if i == 0:
                    pe.wait_ge(rows_in, e * (16 * NT) + 16 * NT)
                pe.wait_ge(xt_done, e * NI + (i + 1))
                for k in range(K):
                    for t in range(2):
                        last = pe.transpose(ps_turn[i % NMISC][:, k, t * P:(t + 1) * P],
                                            rows[:, 2 * i + t, k * P:(k + 1) * P], ident[:])
                last.then_inc(turned, 1)

            def down(e, st):
                f, (t0, t1) = st // len(CH), CH[st % len(CH)]
                pe.wait_ge(act_done, e * S + (st + 1 + ACT0))
                if st == 0:
                    pe.wait_ge(read_out, e + READ0)
                for t in range(t0, t1):
                    at = slice((t - t0) * P, (t - t0 + 1) * P)
                    last = product(pe, ps_down[:, t, :], [a[:, st % 2, at] for a in (act_hi, act_lo)],
                                   [w[:, f % W_RING, IN * K * P:] for w in (w_hi, w_lo)],
                                   f == 0 and t % 2 == 0, f == F_T - 1)
                last.then_inc(down_done, 1)

            for i in range(NI):
                turn(0, i, 0)

            def one(e, b, last_e):
                pe.wait_ge(xt_done, e * NI + (NI + XT0))
                for st in range(S):
                    f, (t0, t1) = st // len(CH), CH[st % len(CH)]
                    if st % len(CH) == 0:
                        pe.wait_ge(raw_lo, e * F_T + (f + 1 + RAW0))
                    pe.wait_ge(act_done, e * S + (st + 1))
                    for j in range(IN):
                        for k in range(K):
                            w0 = (j * K + k) * P
                            last = product(pe, ps_in[st % 2][j][:, 0:(t1 - t0) * P],
                                           [w[:, f % W_RING, w0:w0 + P] for w in (w_hi, w_lo)],
                                           [x[:, b, k, t0 * P:t1 * P] for x in (xt_hi, xt_lo)],
                                           k == 0, k == K - 1)
                    last.then_inc(in_done, 1)
                    if st in ITEM_AT and not last_e:
                        turn(e + 1, ITEM_AT[st], 1 - b)
                    if st:
                        down(e, st - 1)
                down(e, S - 1)

            experts(pe, one)

        @block.scalar
        def _(act):
            def high_part(e, f):
                n = e * F_T + f
                act.wait_ge(raw_in[f % W_RING], (e * (F_T // W_RING) + (f // W_RING + 1)) * 16)
                act.wait_ge(down_done, (n + 1) * len(CH))
                act.copy(w_hi[:, f % W_RING], raw[:, f % W_RING]).then_inc(raw_hi, 1)

            for f in range(AHEAD):
                high_part(0, f)

            def one(e, b, last):
                act.wait_ge(bias_in[b], (e - b) * 16 + 32)
                for st in range(S):
                    f, (t0, t1) = st // len(CH), CH[st % len(CH)]
                    n = (t1 - t0) * P
                    act.wait_ge(in_done, e * S + (st + 1))
                    act.wait_ge(act_done, e * S + (st + 1))
                    if gated:
                        act.activation(silu[:, st % 2, 0:n], ps_in[st % 2][0][:, 0:n], ACT.Silu,
                                       bias=bias[:, b, f:f + 1]).then_inc(silu_done, 1)
                    else:
                        act.activation(act_f[:, st % 2, 0:n], ps_in[st % 2][0][:, 0:n], ACT.Gelu,
                                       bias=bias[:, b, f:f + 1]).then_inc(silu_done, 1)
                    if st % len(CH) == 0:
                        if f + AHEAD < F_T:
                            high_part(e, f + AHEAD)
                        elif not last:
                            high_part(e + 1, f + AHEAD - F_T)

            experts(act, one)

        @block.vector
        def _(dve):
            own = Chain(dve, dve_own)
            dve.sem_inc(act_done, ACT0)
            dve.sem_inc(down_done, DOWN0)
            dve.sem_inc(raw_hi, RAW0)
            dve.sem_inc(raw_lo, RAW0)
            dve.sem_inc(xt_done, XT0)
            dve.sem_inc(read_out, READ0)
            dve.sem_inc(landed, 2)

            def split_rows(e, i, b):
                dve.wait_ge(turned, e * NI + (i + 1))
                at = slice(2 * i * P, (2 * i + 2) * P)
                own.step(dve.tensor_copy(xt_hi[:, b, :, at], ps_turn[i % NMISC][:]))
                dve.tensor_tensor(xt_lo[:, b, :, at], ps_turn[i % NMISC][:], as_f32(xt_hi[:, b, :, at]),
                                  ALU.subtract).then_inc(xt_done, 1)

            for i in range(NI):
                split_rows(0, i, 0)
            first = own.n
            PER = 1 + NI + S * (2 if gated else 1) + 1

            def one(e, b, last):
                own.at(e * PER + first)
                dve.wait_ge(bias_in[b], (e - b) * 16 + 32)
                own.step(dve.tensor_copy(gcol[:, b], gate_cols[:, ds(e, 1), :].rearrange("p e j -> p (e j)")))
                for st in range(S):
                    f, (t0, t1) = st // len(CH), CH[st % len(CH)]
                    n = (t1 - t0) * P
                    act_n, hi_n, lo_n = (a[:, st % 2, 0:n] for a in (act_f, act_hi, act_lo))
                    dve.wait_ge(silu_done, e * S + (st + 1))
                    dve.wait_ge(down_done, e * S + (st + DOWN0 - 1))
                    if gated:
                        own.step(dve.scalar_tensor_tensor(act_n, ps_in[st % 2][1][:, 0:n],
                                                          bias[:, b, F_T + f:F_T + f + 1], silu[:, st % 2, 0:n],
                                                          ALU.add, ALU.mult))
                    own.step(dve.tensor_copy(hi_n, act_n))
                    dve.tensor_tensor(lo_n, act_n, as_f32(hi_n), ALU.subtract).then_inc(act_done, 1)
                    if st in ITEM_AT and not last:
                        split_rows(e + 1, ITEM_AT[st], 1 - b)
                dve.wait_ge(down_done, e * S + (S + DOWN0))
                dve.wait_ge(landed, e + 1)
                for j in range(0, NT, 2):
                    ins = dve.tensor_tensor(out[:, b, j:j + 2, :], ps_down[:, j:j + 2, :],
                                            db[:, b:b + 1, :].to_broadcast([P, 2, D]), ALU.add)
                ins.then_inc(read_out, 1)
                dve.wait_ge(read_out, e + (READ0 + 1))
                for j in range(NT):
                    ins = dve.tensor_scalar(out[:, b, j, :], out[:, b, j, :], gcol[:, b, j:j + 1], None, ALU.mult)
                ins.then_inc(out_done, 1)
                if last:
                    return
                own.step(dve.nop())

            experts(dve, one)


def ffn(nc, tag, x_in, acc, gate_w, shared_w, ffn_w, ffn_b, ffn_db, consts):
    NT = FFN_CAP // P
    h_rows = nc.dram_tensor(f"{tag}_h", (N, D), F32, kind="Internal").ap()
    with Scope(nc, tag) as s:
        logits = s.sb("logits", [P, FFN_E, T])
        low, high = s.sb("low", [P, FFN_E]), s.sb("high", [P, FFN_E])
        ids = s.sb("ids", [P, FFN_E, NT], U32)
        ids2 = s.sb("ids2", [P, FFN_E, NT], U32)
        gates = s.sb("gates", [P, FFN_E, NT])
        with Scope(nc, tag) as s2:
            x_all = s2.sb("x_all", [P, T, D])
            ht_hi, ht_lo = s2.sb("ht_hi", [P, K, N], F32R), s2.sb("ht_lo", [P, K, N], F32R)
            norm_and_score(nc, tag + "n", x_in, gate_w, consts, h_rows, x_all, ht_hi, ht_lo, logits)
            shared_and_search(nc, tag + "s", shared_w, consts, x_all, ht_hi, ht_lo, logits, low, high, acc)
        make_lists(nc, tag + "l", FFN_E, NT, consts, logits, low, high, ids, ids2, gates)
        run_experts(nc, tag + "e", FFN_E, NT, True, ffn_w, ffn_b, ffn_db, consts, h_rows, acc, ids, ids2, gates)


def pipelined(eng, tiles, stages):
    deep = -(-max(lag for lag, _ in stages) // 2) * 2
    end = tiles + deep

    def round_(r):
        for lag, step in stages:
            if 0 <= r - lag < tiles:
                step((r - lag) // 2, (r - lag) % 2)

    for r in range(deep):
        round_(r)
    with eng.Fori(0, (tiles - deep) // 2) as i:
        for u in range(2):
            for lag, step in stages:
                step(i + (deep + u - lag) // 2, (u - lag) % 2)
    for r in range(tiles, end):
        round_(r)


def attention(nc, tag, x_in, acc, w, consts, x2_all, sums):
    Q = T // BATCH
    QK, VG = slice(0, 2 * D), slice(2 * D, 4 * D)
    HW = P + HALF
    with Scope(nc, tag) as s:
        ident, mask = s.sb("ident", [P, P]), s.sb("mask", [P, HW])
        w_hi, w_lo = s.sb("w_hi", [P, K, 4 * D], F32R), s.sb("w_lo", [P, K, 4 * D], F32R)
        wo, scale = s.sb("wo", [P, K, D]), s.sb("scale", [P, K])
        bias, bo, rope = s.sb("bias", [P, 4 * D]), s.sb("bo", [P, D]), s.sb("rope", [P, Q, 4, DK // 2])
        zeros = s.sb("zeros", [P, K * HW])
        x_all, v_all, eg_all = (s.sb(n, [P, T, D]) for n in ("x_all", "v_all", "eg_all"))
        w_raw = v_all[:, 0:4 * K, :].rearrange("p (k t) d -> p k (t d)", k=K)
        neg_half = s.sb("neg_half", [P, 1])
        stats, mv = s.sb("stats", [P, 2, 6]), s.sb("mv", [P, 2, 2])
        rs = s.sb("rs", [P, 2, 4])
        a = s.sb("a", [P, 2, D])
        at_hi, at_lo = s.sb("at_hi", [P, 2, K, P], F32R), s.sb("at_lo", [P, 2, K, P], F32R)
        qk, rot_a, rot_b, rot, er, pos_part, phi = (
            s.sb(n, [P, 2, 2 * D]) for n in ("qk", "rot_a", "rot_b", "rot", "er", "pos_part", "phi"))
        gp = s.sb("gp", [P, 2, D])
        v1 = s.sb("v1", [P, 2, 2, HW])
        qt = s.sb("qt", [P, 2, K, P])
        state = s.sb("state", [P, 2, 2, 2, HW])
        den, div, o = s.sb("den", [P, HEADS]), s.sb("div", [P, D]), s.sb("o", [P, 2, D])
        ot = s.sb("ot", [P, K, P])
        square = zeros[:, 0:D]
        total = s.sb("total", [P, 2, D])
        ps_a, ps_qt = s.ps("ps_a", (P, K, P)), s.ps("ps_qt", (P, K, P))
        ps_qk, ps_vg = s.ps("ps_qk"), s.ps("ps_vg")
        ps_state = [s.ps(f"state{u}", (P, 2, HW)) for u in range(2)]
        ps_num, ps_o = s.ps("ps_num", (P, 2, HW)), s.ps("ps_o", (P, 2, D))
        const_in, w_hi_done, w_lo_done, set_up = (s.sem(n) for n in ("const_in", "w_hi_done", "w_lo_done", "set_up"))
        x_in_s = [s.sem(f"x_in{u}") for u in range(2)]
        stored = [s.sem(f"stored{u}") for u in range(2)]
        (stat_done, rs_done, a_done, xtb_done, a_turned, at_hi_done, at_done, proj_done, proj_read, gp_done, eg_done,
         rot_a_done, rot_b_done, rot_done, er_done, phi_done, v1_done, q_turned, qt_done, s0_done, m0_done, s1_done,
         m1_done, num_done, o_done, o_turned, ot_done, wo_done, x2_done, sum_done, total_done) = (
            s.sem(n) for n in (
                "stat_done", "rs_done", "a_done", "xtb_done", "a_turned", "at_hi_done", "at_done", "proj_done",
                "proj_read", "gp_done", "eg_done", "rot_a_done", "rot_b_done", "rot_done", "er_done", "phi_done",
                "v1_done", "q_turned", "qt_done", "s0_done", "m0_done", "s1_done", "m1_done", "num_done", "o_done",
                "o_turned", "ot_done", "wo_done", "x2_done", "sum_done", "total_done"))
        own_aggr, own_xt, own_qk, own_den, own_div, own_rs, own_var, own_sq, own_ratio = (
            s.sem(n) for n in ("own_aggr", "own_xt", "own_qk", "own_den", "own_div", "own_rs", "own_var", "own_sq",
                               "own_ratio"))
        own_inv = s.sem("own_inv")
        block = s.enter_context(nc.Block())
        N_CONST = 8

        def row(arr, q, u):
            return arr[:, ds(q + u * Q, 1), :].rearrange("p t d -> p (t d)")

        def rows_of(dram, q, u):
            return dram[ds(q * P + u * SEQ, P), :]

        @block.sync
        def _(sp):
            for dst, src in ((ident[:], consts[:, C_IDENT:C_IDENT + P]), (mask[:], consts[:, C_MASK:C_MASK + HW]),
                             (w_raw, w["qkvg"]), (wo[:], w["wo"]), (scale[:], w["norm1"]),
                             (bias[:], w["qkvg_b"].to_broadcast([P, 4 * D])), (bo[:], w["bo"].to_broadcast([P, D])),
                             (rope[:].rearrange("p q c j -> p q (c j)"), w["rope"])):
                sp.dma_start(dst, src).then_inc(const_in, 16)

            def load(q, u):
                sp.wait_ge(a_done, q * 2 + (u + 1))
                sp.dma_start(row(x_all, q, u), rows_of(x_in, q, u)).then_inc(x_in_s[u], 16)

            def store(q, u):
                sp.wait_ge(total_done, q * 2 + (u + 3))
                sp.dma_start(rows_of(acc, q, u), total[:, u]).then_inc(stored[u], 16)

            pipelined(sp, T, [(10, store), (0, load)])
            for u in range(2):
                sp.wait_ge(stored[u], 16 * Q + 16)

        @block.gpsimd
        def _(pool):
            pool.memset(neg_half[:], -0.5).then_inc(own_rs, 1)
            pool.wait_ge(own_rs, 1)
            pool.wait_ge(const_in, 16 * N_CONST)
            pool.wait_ge(w_hi_done, 1)
            pool.tensor_tensor(w_lo[:], w_raw, as_f32(w_hi[:]), ALU.subtract).then_inc(w_lo_done, 1)

            def root(q, u):
                h = q * 2 + u
                wait_apart(pool, a_done, h + 1)
                wait_apart(pool, stat_done, h + 1)
                var = mv[:, u, 1:2]
                pool.tensor_scalar(rs[:, u, 0:1], var, EPS, None, ALU.add).then_inc(own_var, 1)
                pool.wait_ge(own_var, h + 1)
                pool.tensor_tensor(rs[:, u, 1:2], rs[:, u, 0:1], neg_half[:], ALU.pow).then_inc(own_inv, 1)
                pool.wait_ge(own_inv, h + 1)
                pool.tensor_tensor(rs[:, u, 2:3], rs[:, u, 1:2], rs[:, u, 1:2], ALU.mult).then_inc(own_sq, 1)
                pool.wait_ge(own_sq, h + 1)
                pool.tensor_tensor(rs[:, u, 2:3], rs[:, u, 2:3], var, ALU.mult).then_inc(own_ratio, 1)
                pool.wait_ge(own_ratio, h + 1)
                pool.tensor_tensor(rs[:, u, 3:4], rs[:, u, 2:3], neg_half[:], ALU.pow).then_inc(rs_done, 1)

            def add_bo(q, u):
                pool.wait_ge(a_done, q * 2 + (u + 3))
                pool.tensor_tensor(row(x2_all, q, u), row(x2_all, q, u), bo[:], ALU.add).then_inc(xtb_done, 1)

            def rotate_b(q, u):
                h = q * 2 + u
                pool.wait_ge(rot_a_done, h + 1)
                pool.wait_ge(rot_done, h + 1)
                src = qk[:, u].rearrange("p (h c j) -> p h c j", c=2, j=DK // 2)
                dst = rot_b[:, u].rearrange("p (h c j) -> p h c j", c=2, j=DK // 2)
                for c in range(2):
                    ins = pool.tensor_tensor(dst[:, :, c, :], src[:, :, 1 - c, :],
                                             rope[:, ds(q, 1), 2 + c, :].to_broadcast([P, 2 * HEADS, DK // 2]), ALU.mult)
                ins.then_inc(rot_b_done, 1)

            def residual(q, u):
                h = q * 2 + u
                pool.wait_ge(x2_done, h + 2)
                pool.wait_ge(stored[u], q * 16 + 16)
                pool.tensor_tensor(total[:, u], row(x_all, q, u), row(x2_all, q, u), ALU.add).then_inc(total_done, 1)

            pipelined(pool, T, [(10, residual), (3, rotate_b), (1, add_bo), (0, root)])

        @block.tensor
        def _(pe):
            pe.wait_ge(w_lo_done, 1)
            pe.wait_ge(set_up, 1)
            for u in range(2):
                pe.matmul(ps_state[u][:].rearrange("p k c -> p (k c)"), zeros[:, 0:P], zeros[:], start=True, stop=False,
                          skip_group_check=True)

            def turn_a(q, u):
                h = q * 2 + u
                pe.wait_ge(a_done, h + 3)
                pe.wait_ge(at_done, h + 1)
                for k in range(K):
                    ins = pe.transpose(ps_a[:, k, :], a[:, u, k * P:(k + 1) * P], ident[:])
                ins.then_inc(a_turned, 1)

            def project(q, u):
                h = q * 2 + u
                pe.wait_ge(at_done, h + 2)
                pe.wait_ge(proj_read, h + 1)
                for ps, cols in ((ps_qk, QK), (ps_vg, VG)):
                    for k in range(K):
                        ins = product(pe, ps[:], [x[:, u, k, :] for x in (at_hi, at_lo)],
                                      [x[:, k, cols] for x in (w_hi, w_lo)], k == 0, k == K - 1)
                ins.then_inc(proj_done, 1)

            def add_chunk(c, u):
                at = slice(c * CHUNK, (c + 1) * CHUNK)
                for k in range(2):
                    ins = pe.matmul(ps_state[u][:, k, :], phi[at, u, D + k * P:D + (k + 1) * P], v1[at, u, k, :],
                                    start=False, stop=True, skip_group_check=True)
                return ins

            def chunk0(q, u):
                h = q * 2 + u
                pe.wait_ge(phi_done, h + 1)
                pe.wait_ge(v1_done, h + 3)
                pe.wait_ge(qt_done, h + 1)
                for k in range(K):
                    ins = pe.transpose(ps_qt[:, k, :], phi[:, u, k * P:(k + 1) * P], ident[:])
                ins.then_inc(q_turned, 1)
                pe.wait_ge(m1_done, h + 1)
                add_chunk(0, u).then_inc(s0_done, 1)

            def chunk1(q, u):
                pe.wait_ge(m0_done, q * 2 + (u + 1))
                add_chunk(1, u).then_inc(s1_done, 1)

            def numerators(q, u):
                h = q * 2 + u
                pe.wait_ge(m1_done, h + 3)
                pe.wait_ge(qt_done, h + 2)
                pe.wait_ge(o_done, h + 1)
                for c in range(2):
                    at = slice(c * CHUNK, (c + 1) * CHUNK)
                    for k in range(2):
                        ins = pe.matmul(ps_num[at, k, :], qt[:, u, k, at], state[:, u, c, k, :], start=(k == 0), stop=True,
                                        skip_group_check=True)
                ins.then_inc(num_done, 1)

            def turn_o(q, u):
                h = q * 2 + u
                pe.wait_ge(o_done, h + 2)
                pe.wait_ge(x2_done, h + 1)
                for k in range(K):
                    ins = pe.transpose(ps_o[:, 0, k * P:(k + 1) * P], o[:, u, k * P:(k + 1) * P], ident[:])
                ins.then_inc(o_turned, 1)

            def project_o(q, u):
                pe.wait_ge(ot_done, q * 2 + (u + 1))
                for k in range(K):
                    ins = pe.matmul(ps_o[:, 1, :], ot[:, k, :], wo[:, k, :], start=(k == 0), stop=(k == K - 1))
                ins.then_inc(wo_done, 1)

            pipelined(pe, T, [(9, turn_o), (8, numerators), (7, chunk1), (3, project), (6, chunk0), (2, turn_a),
                              (9, project_o)])

        @block.scalar
        def _(act):
            act.wait_ge(const_in, 16 * N_CONST)
            act.copy(w_hi[:], w_raw).then_inc(w_hi_done, 1)

            def split_at(q, u):
                h = q * 2 + u
                act.wait_ge(a_turned, h + 1)
                act.wait_ge(proj_done, h + 1)
                for k in range(K):
                    ins = act.activation(at_hi[:, u, k, :], ps_a[:, k, :], ACT.Copy, scale=scale[:, k:k + 1])
                ins.then_inc(at_hi_done, 1)

            def exp_gate(q, u):
                act.wait_ge(gp_done, q * 2 + (u + 1))
                act.activation(row(eg_all, q, u), gp[:, u], ACT.Exp, scale=-1.0).then_inc(eg_done, 1)

            def exp_rot(q, u):
                h = q * 2 + u
                act.wait_ge(rot_done, h + 3)
                act.activation(er[:, u], rot[:, u], ACT.Exp)
                act.activation(pos_part[:, u], rot[:, u], ACT.Relu).then_inc(er_done, 1)

            def values(q, u):
                act.wait_ge(s1_done, q * 2 + (u + 1))
                act.copy(v1[:, u, :, 0:P], row(v_all, q, u).rearrange("p (k c) -> p k c", k=2)).then_inc(v1_done, 1)

            def copy_qt(q, u):
                h = q * 2 + u
                act.wait_ge(q_turned, h + 1)
                act.wait_ge(num_done, h + 1)
                act.copy(qt[:, u], ps_qt[:]).then_inc(qt_done, 1)

            def copy_ot(q, u):
                h = q * 2 + u
                act.wait_ge(o_turned, h + 1)
                act.wait_ge(wo_done, h + 1)
                act.copy(ot[:].rearrange("p k c -> p (k c)"), ps_o[:, 0, :]).then_inc(ot_done, 1)

            def sum_squares(q, u):
                act.wait_ge(x2_done, q * 2 + (u + 2))
                act.wait_ge(sum_done, q * 2 + (u + 1))
                act.activation(square, row(x2_all, q, u), ACT.Square,
                               accum_out=sums[:, ds(q + u * Q, 1)]).then_inc(sum_done, 1)

            pipelined(act, T, [(9, copy_ot), (6, copy_qt), (10, sum_squares), (5, values), (4, exp_rot), (3, exp_gate),
                               (2, split_at)])

        @block.vector
        def _(dve):
            for sem, free in ((a_done, 2), (at_done, 1), (proj_done, 2), (proj_read, 1), (rot_done, 2), (s1_done, 2),
                              (v1_done, 2), (qt_done, 1), (m1_done, 2), (num_done, 2), (o_done, 1), (x2_done, 1),
                              (wo_done, 1), (sum_done, 1), (total_done, 2), (stored[0], 16), (stored[1], 16)):
                dve.sem_inc(sem, free)
            dve.memset(zeros[:], 0.0)
            dve.memset(v1[:], 1.0).then_inc(set_up, 1)
            dve.wait_ge(const_in, 16 * N_CONST)

            def stat(q, u):
                h = q * 2 + u
                dve.wait_ge(x_in_s[u], q * 16 + 16)
                dve.bn_stats(stats[:, u], row(x_all, q, u)).then_inc(own_aggr, 1)
                wait_apart(dve, own_aggr, h + 1)
                dve.bn_aggr(mv[:, u], stats[:, u]).then_inc(stat_done, 1)

            def norm(q, u):
                h = q * 2 + u
                dve.wait_ge(rs_done, h + 1)
                dve.tensor_scalar(row(x2_all, q, u), row(x_all, q, u), mv[:, u, 0:1], rs[:, u, 1:2], ALU.subtract,
                                  ALU.mult).then_inc(own_xt, 1)
                dve.wait_ge(own_xt, h + 1)
                dve.tensor_scalar(a[:, u], row(x2_all, q, u), rs[:, u, 3:4], None, ALU.mult).then_inc(a_done, 1)

            def split_low(q, u):
                dve.wait_ge(at_hi_done, q * 2 + (u + 1))
                for k in range(K):
                    ins = dve.scalar_tensor_tensor(at_lo[:, u, k, :], ps_a[:, k, :], scale[:, k:k + 1],
                                                   as_f32(at_hi[:, u, k, :]), ALU.mult, ALU.subtract)
                ins.then_inc(at_done, 1)

            def add_bias(q, u):
                h = q * 2 + u
                dve.wait_ge(proj_done, h + 3)
                dve.tensor_tensor(gp[:, u], ps_vg[:, D:2 * D], bias[:, 3 * D:4 * D], ALU.add).then_inc(gp_done, 1)
                dve.tensor_tensor(qk[:, u], ps_qk[:], bias[:, QK], ALU.add).then_inc(own_qk, 1)
                dve.tensor_tensor(row(v_all, q, u), ps_vg[:, 0:D], bias[:, 2 * D:3 * D], ALU.add).then_inc(proj_read, 1)
                dve.wait_ge(own_qk, h + 1)
                dve.tensor_tensor(rot_a[:, u].rearrange("p (h c) -> p h c", c=DK),
                                  qk[:, u].rearrange("p (h c) -> p h c", c=DK),
                                  rope[:, ds(q, 1), 0:2, :].rearrange("p q c j -> p q (c j)")
                                  .to_broadcast([P, 2 * HEADS, DK]), ALU.mult).then_inc(rot_a_done, 1)

            def rotate(q, u):
                h = q * 2 + u
                dve.wait_ge(rot_b_done, h + 1)
                dve.wait_ge(rot_a_done, h + 1)
                dve.tensor_tensor(rot[:, u], rot_a[:, u], rot_b[:, u], ALU.add).then_inc(rot_done, 1)

            def feature(q, u):
                dve.wait_ge(er_done, q * 2 + (u + 1))
                dve.wait_ge(s1_done, q * 2 + (u + 1))
                dve.scalar_tensor_tensor(phi[:, u], er[:, u], 1.0, pos_part[:, u], ALU.min, ALU.add).then_inc(phi_done, 1)

            def copy_state(c, q, u):
                dve.tensor_tensor(state[:, u, c], ps_state[u][:], mask[:].unsqueeze(1).to_broadcast([P, 2, HW]), ALU.mult
                                  ).then_inc((m0_done, m1_done)[c], 1)

            def state0(q, u):
                dve.wait_ge(s0_done, q * 2 + (u + 1))
                dve.wait_ge(num_done, q * 2 + (u + 1))
                copy_state(0, q, u)

            def state1(q, u):
                dve.wait_ge(s1_done, q * 2 + (u + 3))
                copy_state(1, q, u)

            def divide(q, u):
                h = q * 2 + u
                dve.wait_ge(num_done, h + 3)
                dve.wait_ge(eg_done, h + 1)
                dve.tensor_scalar(den[:].rearrange("p (k h) -> p k h", k=2), ps_num[:, :, P:], 1e-6, None, ALU.add
                                  ).then_inc(own_den, 1)
                dve.wait_ge(own_den, h * 2 + 1)
                dve.scalar_tensor_tensor(div[:].rearrange("p (h c) -> p h c", c=DK),
                                         row(eg_all, q, u).rearrange("p (h c) -> p h c", c=DK), 1.0,
                                         den[:].unsqueeze(2).to_broadcast([P, HEADS, DK]), ALU.add, ALU.mult
                                         ).then_inc(own_den, 1)
                dve.wait_ge(own_den, h * 2 + 2)
                dve.reciprocal(div[:], div[:]).then_inc(own_div, 1)
                dve.wait_ge(own_div, h + 1)
                dve.tensor_tensor(o[:, u].rearrange("p (k c) -> p k c", k=2), ps_num[:, :, 0:P],
                                  div[:].rearrange("p (k c) -> p k c", k=2), ALU.mult).then_inc(o_done, 1)

            def add_out(q, u):
                h = q * 2 + u
                dve.wait_ge(wo_done, h + 2)
                dve.wait_ge(xtb_done, h + 1)
                dve.tensor_tensor(row(x2_all, q, u), ps_o[:, 1, :], row(x2_all, q, u), ALU.add).then_inc(x2_done, 1)

            pipelined(dve, T, [(10, add_out), (8, divide), (7, state1), (6, state0), (5, feature), (4, rotate),
                               (3, add_bias), (2, split_low), (1, norm), (0, stat)])


def route(nc, tag, w, consts, x2_all, sums, h_rows, logits, spare):
    with Scope(nc, tag) as s:
        ident, router = s.sb("ident", [P, P]), s.sb("router", [P, K, MOE_E])
        scale, rb = s.sb("scale", [P, D]), s.sb("rb", [P, MOE_E])
        neg_half, root = s.sb("neg_half", [P, T]), s.sb("root", [P, T])
        zeros = s.sb("zeros", [P, D])
        h = s.sb("h", [P, 2, 2, D])
        ht = s.sb("ht", [P, 2, 2, K, P])
        turned = [s.ps(f"turned{b}", (P, 2, K, P)) for b in range(2)]
        scored = [s.ps(f"scored{b}", (P, 2, MOE_E)) for b in range(2)]
        const_in, mean_done, root_done, h_done, turn_done, ht_done, score_done, logit_done = (
            s.sem(n) for n in ("const_in", "mean_done", "root_done", "h_done", "turn_done", "ht_done", "score_done",
                               "logit_done"))
        h_out = [s.sem(f"h_out{b}") for b in range(2)]
        pool_own, zeros_done, spare_out = s.sem("pool_own"), s.sem("zeros_done"), s.sem("spare_out")
        block = s.enter_context(nc.Block())
        R = T // 2

        @block.sync
        def _(sp):
            for dst, src in ((ident[:], consts[:, C_IDENT:C_IDENT + P]), (router[:], w["router"]),
                             (scale[:], w["norm2"].to_broadcast([P, D])), (rb[:], w["router_b"].to_broadcast([P, MOE_E]))):
                sp.dma_start(dst, src).then_inc(const_in, 16)
            with sp.Fori(0, R // 2) as i:
                for b in range(2):
                    r = i * 2 + b
                    sp.wait_ge(h_done, r + 1)
                    sp.dma_start(h_rows[ds(r * (2 * P), 2 * P), :].rearrange("(t p) d -> p t d", p=P), h[:, b]
                                 ).then_inc(h_out[b], 16)
            for b in range(2):
                sp.wait_ge(h_out[b], 16 * (R // 2) + 16)

        @block.gpsimd
        def _(pool):
            pool.memset(zeros[:], 0.0).then_inc(zeros_done, 1)
            pool.memset(neg_half[:], -0.5).then_inc(pool_own, 1)
            pool.wait_ge(pool_own, 1)
            pool.wait_ge(mean_done, 1)
            pool.tensor_tensor(root[:], root[:], neg_half[:], ALU.pow).then_inc(root_done, 1)

        @block.tensor
        def _(pe):
            pe.wait_ge(const_in, 64)
            with pe.Fori(0, R // 2) as i:
                for b in range(2):
                    r = i * 2 + b
                    pe.wait_ge(h_done, r + 1)
                    pe.wait_ge(ht_done, r + 1)
                    for t in range(2):
                        for k in range(K):
                            ins = pe.transpose(turned[b][:, t, k, :], h[:, b, t, k * P:(k + 1) * P], ident[:])
                    ins.then_inc(turn_done, 1)
                    pe.wait_ge(ht_done, r + 3)
                    pe.wait_ge(logit_done, r + 1)
                    for t in range(2):
                        for k in range(K):
                            ins = pe.matmul(scored[b][:, t, :], ht[:, b, t, k, :], router[:, k, :], start=(k == 0),
                                            stop=(k == K - 1))
                    ins.then_inc(score_done, 1)

        @block.scalar
        def _(act):
            act.wait_ge(zeros_done, 1)
            act.dma_start(spare.rearrange("(t p) d -> p t d", p=P),
                          zeros[:].unsqueeze(1).to_broadcast([P, MOE_CAP // P, D])).then_inc(spare_out, 16)
            with act.Fori(0, R // 2) as i:
                for b in range(2):
                    r = i * 2 + b
                    act.wait_ge(turn_done, r + 3)
                    act.wait_ge(score_done, r + 1)
                    act.copy(ht[:, b], turned[b][:]).then_inc(ht_done, 1)
            act.wait_ge(spare_out, 16)

        @block.vector
        def _(dve):
            for sem, free in ((ht_done, 2), (logit_done, 2), (score_done, 2), (turn_done, 2), (h_out[0], 16), (h_out[1], 16)):
                dve.sem_inc(sem, free)
            dve.tensor_scalar(root[:], sums[:], 1.0 / D, None, ALU.mult).then_inc(mean_done, 1)
            dve.wait_ge(const_in, 64)
            dve.wait_ge(root_done, 1)
            with dve.Fori(0, R // 2) as i:
                for b in range(2):
                    r = i * 2 + b
                    dve.wait_ge(h_out[b], i * 16 + 16)
                    dve.wait_ge(turn_done, r + 1)
                    for t in range(2):
                        at = ds(r * 2 + t, 1)
                        ins = dve.scalar_tensor_tensor(h[:, b, t], x2_all[:, at, :].rearrange("p t d -> p (t d)"),
                                                       root[:, at], scale[:], ALU.mult, ALU.mult)
                    ins.then_inc(h_done, 1)
                    dve.wait_ge(score_done, r + 3)
                    dve.tensor_tensor(logits[:, ds(r * 2, 2), :], scored[b][:],
                                      rb[:].unsqueeze(1).to_broadcast([P, 2, MOE_E]), ALU.add).then_inc(logit_done, 1)
            dve.wait_ge(logit_done, R + 2)


def attention_and_moe(nc, tag, x_in, acc, w, consts):
    NT = MOE_CAP // P
    h_rows = nc.dram_tensor(f"{tag}_h", (N, D), F32, kind="Internal").ap()
    with Scope(nc, tag) as s:
        logits = s.sb("logits", [P, T, MOE_E])
        ids, ids2 = s.sb("ids", [P, MOE_E, NT], U32), s.sb("ids2", [P, MOE_E, NT], U32)
        gates = s.sb("gates", [P, MOE_E, NT])
        with Scope(nc, tag) as s2:
            x2_all, sums = s2.sb("x2_all", [P, T, D]), s2.sb("sums", [P, T])
            attention(nc, tag + "a", x_in, acc, w, consts, x2_all, sums)
            route(nc, tag + "r", w, consts, x2_all, sums, h_rows, logits, acc[N:N + MOE_CAP])
        make_lists(nc, tag + "l", MOE_E, NT, consts, logits, None, None, ids, ids2, gates)
        run_experts(nc, tag + "e", MOE_E, NT, False, w["moe_w"], w["moe_b"], w["moe_db"], consts, h_rows, acc,
                    ids, ids2, gates)


def macaron(nc, w, out):
    acc1 = nc.dram_tensor("after_ffn1", (N, D), F32, kind="Internal").ap()
    acc2 = nc.dram_tensor("after_moe", (N + MOE_CAP, D), F32, kind="Internal").ap()
    ffn_w = (w["gate_w"], w["shared_w"], w["ffn_w"], w["ffn_b"], w["ffn_db"], w["consts"])
    ffn(nc, "f1", w["x"], acc1, *ffn_w)
    attention_and_moe(nc, "m", acc1, acc2, w, w["consts"])
    ffn(nc, "f2", acc2, out, *ffn_w)


def constants():
    c = np.zeros((P, C_ALL), np.float32)
    p = np.arange(P)
    c[:, C_IDENT:C_IDENT + P] = np.eye(P)
    c[:, C_TRI:C_TRI + P] = p[:, None] < p[None, :]
    c[:, C_IOTA:C_IOTA + P] = p
    c[:, C_TILE:C_TILE + T] = np.arange(T)
    c[:, C_SLOTHI:C_SLOTHI + 16] = np.arange(16)
    c[:, C_RESET:C_RESET + T] = np.arange(T) > 0
    c[:, C_ROW] = p
    c[:, C_MASK:C_MASK + P] = p[:, None] // DK == p[None, :] // DK
    c[:, C_MASK + P:] = p[:, None] // DK == np.arange(HALF)[None, :]
    return c


def rope_table():
    half = DK // 2
    inv = np.float32(1) / np.float32(10000) ** (np.arange(half, dtype=np.float32) / np.float32(half))
    ang = np.arange(SEQ, dtype=np.float32)[:, None] * inv[None, :]
    sin, cos = np.sin(ang), np.cos(ang)
    table = np.concatenate([cos, cos, -sin, sin], axis=1).astype(np.float32)
    return np.ascontiguousarray(table.reshape(SEQ // P, P, 4 * half).transpose(1, 0, 2))


def k_tiles(w):
    return np.ascontiguousarray(w.reshape(K, P, -1).transpose(1, 0, 2))


def hidden_slices(ins, down):
    E, F = down.shape[:2]
    parts = [w.reshape(E, F // P, P, K, P).transpose(0, 1, 4, 3, 2).reshape(E * F // P, P, D) for w in ins]
    return np.ascontiguousarray(np.concatenate(parts + [down.reshape(E * F // P, P, D)], axis=2))


def lay_out(i):
    a = {k.removeprefix("L0_"): np.asarray(v) for k, v in i.items()}
    by_tile = lambda b: b.reshape(b.shape[0], -1, P).transpose(0, 2, 1)
    o = {"consts": constants(), "x": np.ascontiguousarray(a["attn_x"].reshape(N, D))}
    o["gate_w"] = k_tiles(a["ffn_gate_w"].T)
    o["shared_w"] = hidden_slices([a["ffn_sh_gate_w"][None], a["ffn_sh_up_w"][None]],
                                  a["ffn_sh_down_w"].T[None])
    o["ffn_w"] = hidden_slices([a["ffn_gw"], a["ffn_up_w"]], a["ffn_down_w"].transpose(0, 2, 1))
    o["ffn_b"] = np.ascontiguousarray(np.concatenate([by_tile(a["ffn_gb"]), by_tile(a["ffn_up_b"])], axis=2))
    o["ffn_db"] = a["ffn_down_b"]
    o["moe_w"] = hidden_slices([a["attn_W1"].transpose(0, 2, 1)], a["attn_W2"])
    o["moe_b"], o["moe_db"] = np.ascontiguousarray(by_tile(a["attn_b1"])), a["attn_b2"]
    o["qkvg"] = k_tiles(np.concatenate([a[f"attn_W{c}"] for c in "qkvg"], axis=1))
    o["qkvg_b"] = np.concatenate([a[f"attn_b{c}"] for c in "qkvg"])[None]
    o["wo"], o["bo"] = k_tiles(a["attn_Wo"]), a["attn_bo"][None]
    o["norm1"] = np.ascontiguousarray(a["attn_norm1_scale"].reshape(K, P).T)
    o["norm2"] = a["attn_norm2_scale"][None]
    o["router"], o["router_b"] = k_tiles(a["attn_router_W"]), a["attn_router_b"][None]
    o["rope"] = rope_table()
    return o


def kernel(**inputs):
    import concourse.bacc as bacc
    from concourse.bass_utils import run_bass_kernel_spmd

    arrays = lay_out(inputs)
    nc = bacc.Bacc("TRN2", target_bir_lowering=False, num_devices=1)
    w = {n: nc.dram_tensor(f"in_{n}", a.shape, mybir.dt.from_np(a.dtype), kind="ExternalInput").ap()
         for n, a in arrays.items()}
    out = nc.dram_tensor("out", (N, D), F32, kind="ExternalOutput").ap()
    macaron(nc, w, out)
    r = run_bass_kernel_spmd(nc, [{f"in_{n}": a for n, a in arrays.items()}], core_ids=[0])
    return r.results[0]["out"].reshape(BATCH, SEQ, D)
```

```python
from contextlib import ExitStack

import numpy as np

import concourse.bass as bass
from concourse import mybir

P = 128
ALU = mybir.AluOpType
ACT = mybir.ActivationFunctionType
AX = mybir.AxisListType
F32 = mybir.dt.float32
F32R = mybir.dt.float32r
BF16 = mybir.dt.bfloat16
I32 = mybir.dt.int32
U32 = mybir.dt.uint32
ds = bass.ds

BATCH, SEQ, D = 2, 2048, 256
N = BATCH * SEQ
T = N // P
K = D // P
EPS = 1e-5

FFN_E, FFN_F, FFN_CAP, SHARED_F = 16, 1024, N // 16 * 2, 512
MOE_E, MOE_F, MOE_CAP = 8, 1024, int(1.25 * (8 * 1024 / 8))
HEADS, DK, CHUNK = 16, 16, 64
HALF = P // DK

GT = 4
G = T // GT
W_RING = 4
SEARCH = 4 * G
IDC = 5

C_IDENT, C_TRI, C_IOTA = 0, P, 2 * P
C_TILE = 3 * P
C_SLOTHI = C_TILE + T
C_RESET = C_SLOTHI + 16
C_ROW = C_RESET + T
C_MASK = C_ROW + 1
C_ALL = C_MASK + P + HALF


class Scope(ExitStack):

    def __init__(self, nc, tag):
        super().__init__()
        self.nc, self.tag, self.sems = nc, tag, []
        self.callback(self.clear)

    def sb(self, name, shape, dt=F32):
        return self.enter_context(self.nc.sbuf_tensor(f"{self.tag}_{name}", shape, dt))

    def ps(self, name, shape=(P, 512), dt=F32):
        return self.enter_context(self.nc.psum_tensor(f"{self.tag}_{name}", list(shape), dt))

    def sem(self, name):
        self.sems.append(self.nc.alloc_semaphore(name=f"{self.tag}_{name}"))
        return self.sems[-1]

    def clear(self):
        if self.sems:
            self.nc.clear_and_free_semaphores(self.sems)
            self.nc.all_engine_barrier()


class Chain:

    def __init__(self, eng, sem):
        self.eng, self.sem, self.base, self.n = eng, sem, 0, 0

    def at(self, base):
        self.base, self.n = base, 0

    def step(self, ins, apart=False):
        ins.then_inc(self.sem, 1)
        self.n += 1
        if apart:
            wait_apart(self.eng, self.sem, self.base + self.n)
        else:
            self.eng.wait_ge(self.sem, self.base + self.n)


def wait_apart(eng, sem, value):
    eng.wait_ge(sem, value)
    eng.nop(nofuse=True)


def product(pe, out, left, right, first, last):
    (lh, ll), (rh, rl) = left, right
    pe.matmul(out, lh, rh, start=first, stop=False, skip_group_check=True)
    pe.matmul(out, lh, rl, start=False, stop=False, skip_group_check=True)
    return pe.matmul(out, ll, rh, start=False, stop=last, skip_group_check=True)


def as_f32(ap):
    return ap.bitcast(F32)


def pipelined(eng, tiles, stages):
    deep = -(-max(lag for lag, _ in stages) // 2) * 2
    end = tiles + deep

    def round_(r):
        for lag, step in stages:
            if 0 <= r - lag < tiles:
                step((r - lag) // 2, (r - lag) % 2)

    for r in range(deep):
        round_(r)
    with eng.Fori(0, (tiles - deep) // 2) as i:
        for u in range(2):
            for lag, step in stages:
                step(i + (deep + u - lag) // 2, (u - lag) % 2)
    for r in range(tiles, end):
        round_(r)


def norm_and_score(nc, tag, x_in, gate_w, consts, h_rows, x_all, ht_hi, ht_lo, logits):
    E = gate_w.shape[2]
    with Scope(nc, tag) as s:
        ident = s.sb("ident", [P, P])
        gate = s.sb("gate", [P, K, E])
        neg_half = s.sb("neg_half", [P, GT])
        stats = s.sb("stats", [P, 2, GT, 6])
        mv = s.sb("mv", [P, 2, GT, 2])
        var_eps = s.sb("var_eps", [P, 2, GT])
        rstd = s.sb("rstd", [P, 2, GT])
        h = s.sb("h", [P, 2, GT, D])
        ht = s.sb("ht", [P, 2, K, GT * P])
        turned = [s.ps(f"turned{b}", (P, K, GT * P)) for b in range(2)]
        scored = [s.ps(f"scored{b}", (P, GT, E)) for b in range(2)]
        const_in, x_in_s = s.sem("const_in"), [s.sem(f"x_in{b}") for b in range(2)]
        stat_done, rstd_done, h_done = s.sem("stat_done"), s.sem("rstd_done"), s.sem("h_done")
        h_out = [s.sem(f"h_out{b}") for b in range(2)]
        turn_done, ht_done, hi_done = s.sem("turn_done"), s.sem("ht_done"), s.sem("hi_done")
        lo_done, score_done, logit_done = s.sem("lo_done"), s.sem("score_done"), s.sem("logit_done")
        dve_own, pool_own, half_done = s.sem("dve_own"), s.sem("pool_own"), s.sem("half_done")
        block = s.enter_context(nc.Block())

        def group(arr, q, u):
            return arr[:, ds((q * 2 + u) * GT, GT), :]

        def tile(arr, q, u, t):
            return arr[:, ds((q * 2 + u) * GT + t, 1), :].rearrange("p t d -> p (t d)")

        def columns(q, u):
            return ds((q * 2 + u) * (GT * P), GT * P)

        def rows_of(dram, q, u):
            return dram[columns(q, u), :].rearrange("(t p) d -> p t d", p=P)

        @block.sync
        def _(sp):
            sp.dma_start(ident[:], consts[:, C_IDENT:C_IDENT + P]).then_inc(const_in, 16)
            sp.dma_start(gate[:], gate_w).then_inc(const_in, 16)

            def load(q, u):
                sp.wait_ge(stat_done, q * 2 + (u + 1))
                sp.dma_start(group(x_all, q, u), rows_of(x_in, q, u)).then_inc(x_in_s[u], 16)

            pipelined(sp, G, [(0, load)])

        @block.gpsimd
        def _(pool):
            pool.memset(neg_half[:], -0.5).then_inc(half_done, 1)
            pool.wait_ge(half_done, 1)

            def root(q, u):
                g = q * 2 + u
                wait_apart(pool, stat_done, g + 3)
                wait_apart(pool, h_done, g + 1)
                pool.tensor_scalar(var_eps[:, u], mv[:, u, :, 1], EPS, None, ALU.add).then_inc(pool_own, 1)
                pool.wait_ge(pool_own, g + 1)
                pool.tensor_tensor(rstd[:, u], var_eps[:, u], neg_half[:], ALU.pow).then_inc(rstd_done, 1)

            def low_part(q, u):
                g = q * 2 + u
                pool.wait_ge(ht_done, g + 1)
                pool.wait_ge(hi_done, g + 3)
                for k in range(K):
                    ins = pool.tensor_tensor(ht_lo[:, k, columns(q, u)], ht[:, u, k, :],
                                             as_f32(ht_hi[:, k, columns(q, u)]), ALU.subtract)
                ins.then_inc(lo_done, 1)

            pipelined(pool, G, [(0, root), (2, low_part)])

        @block.tensor
        def _(pe):
            pe.wait_ge(const_in, 32)

            def turn(q, u):
                g = q * 2 + u
                pe.wait_ge(h_done, g + 3)
                pe.wait_ge(hi_done, g + 1)
                for k in range(K):
                    for t in range(GT):
                        ins = pe.transpose(turned[u][:, k, t * P:(t + 1) * P], h[:, u, t, k * P:(k + 1) * P], ident[:])
                ins.then_inc(turn_done, 1)

            def score(q, u):
                g = q * 2 + u
                pe.wait_ge(ht_done, g + 1)
                pe.wait_ge(logit_done, g + 1)
                for t in range(GT):
                    for k in range(K):
                        ins = pe.matmul(scored[u][:, t, :], ht[:, u, k, t * P:(t + 1) * P], gate[:, k, :],
                                        start=(k == 0), stop=(k == K - 1))
                ins.then_inc(score_done, 1)

            pipelined(pe, G, [(2, score), (1, turn)])

        @block.scalar
        def _(act):
            def copy_turned(q, u):
                g = q * 2 + u
                act.wait_ge(turn_done, g + 3)
                act.wait_ge(score_done, g + 1)
                act.wait_ge(lo_done, g + 1)
                for k in range(K):
                    ins = act.copy(ht[:, u, k, :], turned[u][:, k, :])
                ins.then_inc(ht_done, 1)
                for k in range(K):
                    ins = act.copy(ht_hi[:, k, columns(q, u)], turned[u][:, k, :])
                ins.then_inc(hi_done, 1)
                act.wait_ge(h_done, g + 3)
                act.dma_start(rows_of(h_rows, q, u), h[:, u]).then_inc(h_out[u], 16)

            pipelined(act, G, [(1, copy_turned)])
            for u in range(2):
                act.wait_ge(h_out[u], 16 * (G // 2) + 16)

        @block.vector
        def _(dve):
            for sem in (h_done, hi_done, lo_done, turn_done, logit_done, score_done, stat_done):
                dve.sem_inc(sem, 2)
            for u in range(2):
                dve.sem_inc(h_out[u], 16)

            def stat(q, u):
                g = q * 2 + u
                dve.wait_ge(x_in_s[u], q * 16 + 16)
                for t in range(GT):
                    ins = dve.bn_stats(stats[:, u, t], tile(x_all, q, u, t))
                ins.then_inc(dve_own, 1)
                wait_apart(dve, dve_own, g + 1)
                for t in range(GT):
                    ins = dve.bn_aggr(mv[:, u, t], stats[:, u, t])
                ins.then_inc(stat_done, 1)

            def norm(q, u):
                g = q * 2 + u
                dve.wait_ge(rstd_done, g + 1)
                dve.wait_ge(stat_done, g + 3)
                dve.wait_ge(h_out[u], q * 16 + 16)
                dve.wait_ge(turn_done, g + 1)
                for t in range(GT):
                    ins = dve.tensor_scalar(h[:, u, t], tile(x_all, q, u, t), mv[:, u, t, 0:1], rstd[:, u, t:t + 1],
                                            ALU.subtract, ALU.mult)
                ins.then_inc(h_done, 1)

            def keep_logits(q, u):
                dve.wait_ge(score_done, q * 2 + (u + 3))
                dve.tensor_copy(logits[:, :, ds((q * 2 + u) * GT, GT)], scored[u][:].rearrange("p t e -> p e t")
                                ).then_inc(logit_done, 1)

            pipelined(dve, G, [(3, keep_logits), (1, norm), (0, stat)])
            dve.wait_ge(logit_done, G + 2)
            dve.wait_ge(lo_done, G + 2)


def shared_and_search(nc, tag, w_dram, consts, x_all, ht_hi, ht_lo, logits, low, high, acc_out):
    E = FFN_E
    F_T = SHARED_F // P
    W = (2 * K) * P + D
    with Scope(nc, tag) as s:
        raw = s.sb("raw", [P, F_T, W])
        w_hi, w_lo = s.sb("w_hi", [P, F_T, W], F32R), s.sb("w_lo", [P, F_T, W], F32R)
        ones = s.sb("ones", [P, P], BF16)
        at_least = s.sb("at_least", [P, E, T], BF16)
        twice = s.sb("twice", [P, E, T])
        part = s.sb("part", [P, E])
        part_b = s.sb("part_b", [P, E], BF16)
        ends = s.sb("ends", [P, 2, E])
        ends_all = s.sb("ends_all", [P, 2, E])
        size = s.sb("size", [P, E])
        both = s.sb("both", [P, E])
        mid = s.sb("mid", [P, E])
        enough, short = s.sb("enough", [P, E], I32), s.sb("short", [P, E], I32)
        silu = s.sb("silu", [P, 2, 512])
        act_f = s.sb("act_f", [P, 2, 512])
        act_hi, act_lo = s.sb("act_hi", [P, 2, 512], F32R), s.sb("act_lo", [P, 2, 512], F32R)
        out = s.sb("out", [P, 2, GT, D])
        ps_gate = [s.ps(f"gate{b}") for b in range(2)]
        ps_up = [s.ps(f"up{b}") for b in range(2)]
        ps_down = s.ps("down", (P, GT, D))
        ps_count = s.ps("count", (P, E))
        w_in, w_hi_done, w_lo_done = s.sem("w_in"), s.sem("w_hi_done"), s.sem("w_lo_done")
        ones_done, ends_done, ends_all_done = s.sem("ones_done"), s.sem("ends_done"), s.sem("ends_all_done")
        gu_done, silu_done, act_done, down_done = (s.sem(n) for n in ("gu_done", "silu_done", "act_done", "down_done"))
        part_done, count_done, out_done = s.sem("part_done"), s.sem("count_done"), s.sem("out_done")
        act_hi_done = s.sem("act_hi_done")
        out_stored = [s.sem(f"out_stored{b}") for b in range(2)]
        dve_own = s.sem("dve_own")
        block = s.enter_context(nc.Block())

        def groups(eng, one):
            with eng.Fori(0, G // 2 - 1) as i:
                one(i * 2, 0, False)
                one(i * 2 + 1, 1, False)
            one(G - 2, 0, False)
            one(G - 1, 1, True)

        @block.sync
        def _(sp):
            sp.dma_start(raw[:], w_dram.rearrange("f p w -> p f w")).then_inc(w_in, 16)
            with sp.Fori(0, G // 2) as i:
                for b in range(2):
                    g = i * 2 + b
                    sp.wait_ge(out_done, g + 2)
                    sp.dma_start(acc_out[ds(g * (GT * P), GT * P), :].rearrange("(t p) d -> p t d", p=P),
                                 out[:, b]).then_inc(out_stored[b], 16)
            for b in range(2):
                sp.wait_ge(out_stored[b], 16 * (G // 2) + 16)

        @block.gpsimd
        def _(pool):
            pool.wait_ge(w_hi_done, 1)
            for f in range(F_T):
                last = pool.tensor_tensor(w_lo[:, f], raw[:, f], as_f32(w_hi[:, f]), ALU.subtract)
            last.then_inc(w_lo_done, 1)
            pool.wait_ge(ends_done, 1)
            pool.partition_all_reduce(ends_all[:].rearrange("p a e -> p (a e)"),
                                      ends[:].rearrange("p a e -> p (a e)"), P,
                                      bass.bass_isa.ReduceOp.max).then_inc(ends_all_done, 1)

            def low_part(n, f):
                pool.wait_ge(act_hi_done, n + 1)
                pool.tensor_tensor(act_lo[:, f % 2], act_f[:, f % 2], as_f32(act_hi[:, f % 2]),
                                   ALU.subtract).then_inc(act_done, 1)

            with pool.Fori(0, G) as g:
                for f in range(F_T):
                    low_part(g * F_T + f, f)

        @block.tensor
        def _(pe):
            pe.wait_ge(w_lo_done, 1)
            pe.wait_ge(ones_done, 1)

            def down(g, n, f):
                pe.wait_ge(act_done, n + 3)
                if f == 0:
                    pe.wait_ge(out_done, g + 1)
                for t in range(GT):
                    last = product(pe, ps_down[:, t, :],
                                   [a[:, f % 2, t * P:(t + 1) * P] for a in (act_hi, act_lo)],
                                   [w[:, f, 2 * K * P:] for w in (w_hi, w_lo)],
                                   f == 0 and t % 2 == 0, f == F_T - 1)
                last.then_inc(down_done, 1)

            def into(g, f):
                pe.wait_ge(act_done, g * F_T + (f + 1))
                for j, ps in enumerate((ps_gate, ps_up)):
                    for k in range(K):
                        w0 = (j * K + k) * P
                        last = product(pe, ps[f % 2][:], [w[:, f, w0:w0 + P] for w in (w_hi, w_lo)],
                                       [h[:, k, ds(g * (GT * P), GT * P)] for h in (ht_hi, ht_lo)],
                                       k == 0, k == K - 1)
                last.then_inc(gu_done, 1)

            def count(n):
                pe.wait_ge(part_done, n + 1)
                pe.matmul(ps_count[:], ones[:], part_b[:], start=True, stop=True).then_inc(count_done, 1)

            into(0, 0)
            count(0)

            def one(g, b, last):
                for f in range(1, F_T):
                    into(g, f)
                    down(g, g * F_T + (f - 1), f - 1)
                    count(g * F_T + f)
                if not last:
                    into(g + 1, 0)
                down(g, g * F_T + (F_T - 1), F_T - 1)
                if not last:
                    count((g + 1) * F_T)

            groups(pe, one)

        @block.scalar
        def _(act):
            act.wait_ge(w_in, 16)
            for f in range(F_T):
                last = act.copy(w_hi[:, f], raw[:, f])
            last.then_inc(w_hi_done, 1)
            with act.Fori(0, G // 2) as i:
                for b in range(2):
                    for f in range(F_T):
                        n = (i * 2 + b) * F_T + f
                        act.wait_ge(gu_done, n + 1)
                        act.wait_ge(act_done, n + 1)
                        act.activation(silu[:, f % 2], ps_gate[f % 2][:], ACT.Silu).then_inc(silu_done, 1)

        @block.vector
        def _(dve):
            own = Chain(dve, dve_own)
            dve.sem_inc(act_done, 2)
            dve.sem_inc(down_done, 2)
            dve.sem_inc(out_done, 1)
            for b in range(2):
                dve.sem_inc(out_stored[b], 16)
            dve.memset(ones[:], 1.0).then_inc(ones_done, 1)
            own.step(dve.tensor_scalar(twice[:], logits[:], 2.0, None, ALU.mult))
            own.step(dve.tensor_reduce(ends[:, 0], logits[:], AX.X, ALU.max))
            own.step(dve.tensor_reduce(ends[:, 1], logits[:], AX.X, ALU.min))
            dve.tensor_scalar(ends[:, 1], ends[:, 1], -1.0, None, ALU.mult).then_inc(ends_done, 1)
            dve.wait_ge(ends_all_done, 1)
            own.step(dve.tensor_scalar(low[:], ends_all[:, 1], -1.0, None, ALU.mult))
            own.step(dve.scalar_tensor_tensor(size[:], ends_all[:, 0], -1.0, ends_all[:, 0], ALU.mult, ALU.max))
            own.step(dve.tensor_scalar(size[:], size[:], 2.0 ** -10, 1e-30, ALU.mult, ALU.add))
            own.step(dve.tensor_tensor(high[:], ends_all[:, 0], size[:], ALU.add))
            first = own.n

            def compare():
                own.step(dve.tensor_tensor(both[:], low[:], high[:], ALU.add))
                own.step(dve.tensor_tensor(at_least[:], twice[:], both[:].unsqueeze(2).to_broadcast([P, E, T]), ALU.is_ge))
                dve.tensor_scalar(mid[:], both[:], 0.5, None, ALU.mult)
                own.step(dve.tensor_reduce(part[:], at_least[:], AX.X, ALU.add))
                dve.tensor_copy(part_b[:], part[:]).then_inc(part_done, 1)

            def halve(n):
                wait_apart(dve, count_done, n + 1)
                dve.tensor_scalar(enough[:], ps_count[:], float(FFN_CAP) - 0.5, None, ALU.is_ge)
                own.step(dve.tensor_scalar(short[:], ps_count[:], float(FFN_CAP) - 0.5, None, ALU.is_lt), apart=True)
                dve.copy_predicated(low[:], enough[:], mid[:])
                own.step(dve.copy_predicated(high[:], short[:], mid[:]))

            def activate(g, f):
                n = g * F_T + f
                dve.wait_ge(silu_done, n + 1)
                dve.wait_ge(act_done, n + 1)
                own.step(dve.tensor_tensor(act_f[:, f % 2], ps_up[f % 2][:], silu[:, f % 2], ALU.mult))
                dve.wait_ge(down_done, n + 1)
                dve.tensor_copy(act_hi[:, f % 2], act_f[:, f % 2]).then_inc(act_hi_done, 1)

            compare()
            activate(0, 0)
            halve(0)
            compare()
            first = own.n
            STEP = 1 + 2 + 3

            def one(g, b, last):
                own.at(g * (F_T * STEP) + first)
                for f in range(1, F_T):
                    activate(g, f)
                    halve(g * F_T + f)
                    if not (last and f == F_T - 1):
                        compare()
                if not last:
                    activate(g + 1, 0)
                dve.wait_ge(down_done, g * F_T + (F_T + 2))
                dve.wait_ge(out_stored[b], (g - b) * 8 + 16)
                for t in range(0, GT, 2):
                    ins = dve.scalar_tensor_tensor(out[:, b, t:t + 2], ps_down[:, t:t + 2, :], 0.5,
                                                   x_all[:, ds(g * GT + t, 2), :], ALU.mult, ALU.add)
                ins.then_inc(out_done, 1)
                if not last:
                    halve((g + 1) * F_T)
                    compare()

            groups(dve, one)


def make_lists(nc, tag, E, NT, consts, logits, low, high, gather_ids, scatter_ids, gate_cols):
    ET = E * T
    HB = 8
    NB = T // HB
    expert_chooses = low is not None
    with Scope(nc, tag) as s:
        cst = s.sb("cst", [P, C_ALL])
        tri, ones = (s.sb(n, [P, P], BF16) for n in ("tri", "ones"))
        lanes = s.sb("lanes", [P, P, HB], BF16)
        reset, sel, tie, gate, totals, summed, pos, row = (
            s.sb(n, [P, E, T]) for n in ("reset", "sel", "tie", "gate", "totals", "summed", "pos", "row"))
        sel_b, lane_b = s.sb("sel_b", [P, E, T], BF16), s.sb("lane_b", [P, E, T], BF16)
        pos_i, part_i = s.sb("pos_i", [P, E, T], I32), s.sb("part_i", [P, E, T], I32)
        row_hot = s.sb("row_hot", [P, E, T, NT], BF16)
        vals = s.sb("vals", [P, E, T, IDC], BF16)
        moved = s.sb("moved", [P, E, T, NT * IDC], BF16)
        hot = s.sb("hot", [P, 2, P, HB], BF16)
        counts = s.sb("counts", [P, E])
        slots = s.sb("slots", [P, E, NT, IDC])
        idf, tmp = s.sb("idf", [P, E, NT]), s.sb("tmp", [P, E, NT])
        if not expert_chooses:
            slot_no = s.sb("slot_no", [P, E, NT])
            best, best_i = s.sb("best", [P, T, 8]), s.sb("best_i", [P, T, 8], U32)
            best_f = s.sb("best_f", [P, 2, T])
            ratio, share = s.sb("ratio", [P, T]), s.sb("share", [P, 2, T])
        ps_before, ps_total = s.ps("before", (P, E, T)), s.ps("total", (P, E, T))
        PER_BANK = 512 // (NT * IDC)
        n_banks = -(-E // PER_BANK)
        ps_slots = [s.ps(f"slots{i}", (P, PER_BANK, NT * IDC)) for i in range(n_banks)]
        const_in, const_done = s.sem("const_in"), s.sem("const_done")
        sel_done, prefix_done, vals_done = s.sem("sel_done"), s.sem("prefix_done"), s.sem("vals_done")
        hot_done, hot_used = s.sem("hot_done"), s.sem("hot_used")
        gate_asked, gate_ready = s.sem("gate_asked"), s.sem("gate_ready")
        dve_own = s.sem("dve_own")
        block = s.enter_context(nc.Block())
        ROUNDS = 3 if expert_chooses else 1

        @block.sync
        def _(sp):
            sp.dma_start(cst[:], consts).then_inc(const_in, 16)

        @block.scalar
        def _(act):
            if expert_chooses:
                act.activation(gate[:], logits[:], ACT.Sigmoid).then_inc(gate_ready, 1)
            else:
                act.wait_ge(gate_asked, 1)
                act.activation(ratio[:], ratio[:], ACT.Exp).then_inc(gate_ready, 1)

        @block.tensor
        def _(pe):
            pe.wait_ge(const_done, 1)
            flat = sel_b[:].rearrange("p e t -> p (e t)")
            for r in range(ROUNDS):
                pe.wait_ge(sel_done, r + 1)
                pe.matmul(ps_before[:].rearrange("p e t -> p (e t)"), tri[:], flat, start=True, stop=True)
                pe.matmul(ps_total[:].rearrange("p e t -> p (e t)"), ones[:], flat,
                          start=True, stop=True).then_inc(prefix_done, 1)
            pe.wait_ge(vals_done, 1)
            for e in range(E):
                for n in range(NB):
                    m = e * NB + n
                    pe.wait_ge(hot_done, m + 1)
                    for t in range(HB):
                        last = pe.matmul(ps_slots[e // PER_BANK][:, e % PER_BANK, :], hot[:, m % 2, :, t],
                                         moved[:, e, n * HB + t, :], start=(n == 0 and t == 0),
                                         stop=(n == NB - 1 and t == HB - 1))
                    last.then_inc(hot_used, 1)

        @block.vector
        def _(dve):
            own = Chain(dve, dve_own)
            by_expert = [P, E, T]
            dve.wait_ge(const_in, 16)
            dve.tensor_copy(tri[:], cst[:, C_TRI:C_TRI + P])
            dve.memset(ones[:], 1.0)
            dve.tensor_copy(lanes[:], cst[:, C_IOTA:C_IOTA + P].unsqueeze(2).to_broadcast([P, P, HB]))
            dve.tensor_copy(reset[:], cst[:, C_RESET:C_RESET + T].unsqueeze(1).to_broadcast(by_expert)
                            ).then_inc(const_done, 1)
            dve.wait_ge(const_done, 1)
            rounds = [0]

            def prefix(chosen):
                rounds[0] += 1
                dve.tensor_copy(sel_b[:], chosen[:]).then_inc(sel_done, 1)
                dve.wait_ge(prefix_done, rounds[0])
                own.step(dve.tensor_copy(totals[:], ps_total[:]))
                own.step(dve.tensor_tensor_scan(summed[:].rearrange("p e t -> p (e t)"),
                                                reset[:].rearrange("p e t -> p (e t)"),
                                                totals[:].rearrange("p e t -> p (e t)"), 0.0, ALU.mult, ALU.add))
                own.step(dve.tensor_tensor(pos[:], summed[:], totals[:], ALU.subtract))
                own.step(dve.tensor_tensor(pos[:], ps_before[:], pos[:], ALU.add))

            if expert_chooses:
                own.step(dve.tensor_tensor(sel[:], logits[:], high[:].unsqueeze(2).to_broadcast(by_expert), ALU.is_ge))
                own.step(dve.tensor_tensor(tie[:], logits[:], low[:].unsqueeze(2).to_broadcast(by_expert), ALU.is_ge))
                own.step(dve.tensor_tensor(tie[:], tie[:], sel[:], ALU.subtract))
                prefix(sel)
                own.step(dve.tensor_scalar(counts[:], summed[:, :, T - 1], -1.0, float(FFN_CAP), ALU.mult, ALU.add))
                prefix(tie)
                own.step(dve.tensor_tensor(pos[:], pos[:], counts[:].unsqueeze(2).to_broadcast(by_expert), ALU.is_lt))
                own.step(dve.tensor_tensor(tie[:], tie[:], pos[:], ALU.mult))
                own.step(dve.tensor_tensor(sel[:], sel[:], tie[:], ALU.add))
                prefix(sel)
                dve.wait_ge(gate_ready, 1)
            else:
                for t in range(T):
                    last = dve.max(best[:, t, :], logits[:, t, :])
                own.step(last)
                for t in range(T):
                    last = dve.max_index(best_i[:, t, :], best[:, t, :], logits[:, t, :])
                own.step(last)
                own.step(dve.tensor_copy(best_f[:], best_i[:, :, 0:2].rearrange("p t c -> p c t")))
                dve.tensor_tensor(ratio[:], best[:, :, 1], best[:, :, 0], ALU.subtract).then_inc(gate_asked, 1)
                dve.wait_ge(gate_ready, 1)
                own.step(dve.tensor_scalar(share[:, 1], ratio[:], 1.0, None, ALU.add))
                own.step(dve.reciprocal(share[:, 0], share[:, 1]))
                own.step(dve.tensor_tensor(share[:, 1], share[:, 0], ratio[:], ALU.mult))
                expert_no = cst[:, C_SLOTHI:C_SLOTHI + E].unsqueeze(2).to_broadcast(by_expert)
                for c, (hot_c, gated) in enumerate(((sel, gate), (tie, row))):
                    own.step(dve.tensor_tensor(hot_c[:], expert_no,
                                               best_f[:, c, :].unsqueeze(1).to_broadcast(by_expert), ALU.is_equal))
                    own.step(dve.tensor_tensor(gated[:], hot_c[:],
                                               share[:, c, :].unsqueeze(1).to_broadcast(by_expert), ALU.mult))
                own.step(dve.tensor_tensor(sel[:], sel[:], tie[:], ALU.add))
                own.step(dve.tensor_tensor(gate[:], gate[:], row[:], ALU.add))
                prefix(sel)
                own.step(dve.tensor_scalar(tie[:], pos[:], float(MOE_CAP) - 0.5, None, ALU.is_lt))
                own.step(dve.tensor_tensor(sel[:], sel[:], tie[:], ALU.mult))
                own.step(dve.tensor_scalar(counts[:], summed[:, :, T - 1], float(MOE_CAP), None, ALU.min))
            own.step(dve.tensor_scalar(pos[:], pos[:], 1.0, None, ALU.add))
            own.step(dve.tensor_tensor(pos[:], pos[:], sel[:], ALU.mult))
            own.step(dve.tensor_scalar(pos_i[:], pos[:], -1.0, None, ALU.add))
            own.step(dve.tensor_scalar(part_i[:], pos_i[:], P - 1, None, ALU.bitwise_and))
            own.step(dve.tensor_copy(lane_b[:], part_i[:]))
            own.step(dve.tensor_scalar(part_i[:], pos_i[:], P.bit_length() - 1, None, ALU.arith_shift_right))
            own.step(dve.tensor_copy(row[:], part_i[:]))
            own.step(dve.tensor_copy(vals[:, :, :, 0], cst[:, C_TILE:C_TILE + T].unsqueeze(1).to_broadcast(by_expert)))
            own.step(dve.tensor_copy(vals[:, :, :, 1], cst[:, C_ROW:C_ROW + 1].unsqueeze(2).to_broadcast(by_expert)))
            for c in range(3):
                own.step(dve.tensor_copy(vals[:, :, :, 2 + c], gate[:]))
                if c < 2:
                    own.step(dve.tensor_tensor(gate[:], gate[:], vals[:, :, :, 2 + c], ALU.subtract))
            for j in range(NT):
                last = dve.tensor_scalar(row_hot[:, :, :, j], row[:], float(j), None, ALU.is_equal)
            own.step(last)
            for j in range(NT):
                last = dve.tensor_tensor(moved[:, :, :, j * IDC:(j + 1) * IDC].rearrange("p e t c -> p (e t) c"),
                                         vals[:].rearrange("p e t c -> p (e t) c"),
                                         row_hot[:, :, :, j].rearrange("p e t -> p (e t)").unsqueeze(2)
                                         .to_broadcast([P, ET, IDC]), ALU.mult)
            last.then_inc(vals_done, 1)
            for e in range(E):
                for n in range(NB):
                    m = e * NB + n
                    if m >= 2:
                        dve.wait_ge(hot_used, m - 1)
                    dve.tensor_tensor(hot[:, m % 2], lanes[:],
                                      lane_b[:, e, n * HB:(n + 1) * HB].unsqueeze(1).to_broadcast([P, P, HB]),
                                      ALU.is_equal).then_inc(hot_done, 1)
            dve.wait_ge(hot_used, E * NB)
            for i in range(n_banks):
                e0, e1 = i * PER_BANK, min(E, (i + 1) * PER_BANK)
                last = dve.tensor_copy(slots[:, e0:e1].rearrange("p e j c -> p e (j c)"), ps_slots[i][:, 0:e1 - e0])
            own.step(last)
            own.step(dve.scalar_tensor_tensor(idf[:], slots[:, :, :, 0], float(P), slots[:, :, :, 1], ALU.mult, ALU.add))
            own.step(dve.tensor_copy(gather_ids[:], idf[:]))
            own.step(dve.tensor_tensor(tmp[:], slots[:, :, :, 2], slots[:, :, :, 3], ALU.add))
            own.step(dve.tensor_tensor(gate_cols[:], tmp[:], slots[:, :, :, 4], ALU.add))
            if expert_chooses:
                own.step(dve.tensor_scalar(gate_cols[:], gate_cols[:], 0.5, None, ALU.mult))
            else:
                slot_tiles = cst[:, C_SLOTHI:C_SLOTHI + NT].unsqueeze(1).to_broadcast([P, E, NT])
                own.step(dve.tensor_scalar(slot_no[:], slot_tiles, float(P), cst[:, C_ROW:C_ROW + 1], ALU.mult, ALU.add))
                own.step(dve.tensor_tensor(tmp[:], slot_no[:], counts[:].unsqueeze(2).to_broadcast([P, E, NT]), ALU.is_ge))
                own.step(dve.scalar_tensor_tensor(tmp[:], slot_no[:], float(N), tmp[:], ALU.add, ALU.mult))
                own.step(dve.tensor_tensor(idf[:], idf[:], tmp[:], ALU.add))
            own.step(dve.tensor_copy(scatter_ids[:], idf[:]))


def run_experts(nc, tag, E, NT, gated, w_dram, bias_dram, down_bias, consts, h_rows, acc,
                gather_ids, scatter_ids, gate_cols):
    F_T = FFN_F // P
    CH = [(c, min(c + 4, NT)) for c in range(0, NT, 4)]
    S = F_T * len(CH)
    IN = (2 if gated else 1)
    W = IN * K * P + D
    NI = NT // 2
    NMISC = 2 if gated else 1
    ITEM_AT = {4: 0, 6: 1} if gated else {13: 0, 15: 1, 17: 2, 19: 3, 21: 4}
    AHEAD = 3
    LOW_AHEAD = 5
    assert len(ITEM_AT) == NI and S % 2 == 0 and F_T % W_RING == 0 and NI % NMISC == 0
    with Scope(nc, tag) as s:
        ident = s.sb("ident", [P, P])
        raw = s.sb("raw", [P, W_RING, W])
        w_hi, w_lo = s.sb("w_hi", [P, W_RING, W], F32R), s.sb("w_lo", [P, W_RING, W], F32R)
        bias = s.sb("bias", [P, 2, IN * F_T])
        db = s.sb("db", [P, 2, D])
        rows = s.sb("rows", [P, NT, D])
        xt_hi = s.sb("xt_hi", [P, 2, K, NT * P], F32R)
        xt_lo = s.sb("xt_lo", [P, 2, K, NT * P], F32R)
        silu = s.sb("silu", [P, 2, 512])
        act_f = s.sb("act_f", [P, 2, 512])
        act_hi, act_lo = s.sb("act_hi", [P, 2, 512], F32R), s.sb("act_lo", [P, 2, 512], F32R)
        out = s.sb("out", [P, 2, NT, D])
        gcol = s.sb("gcol", [P, 2, NT])
        gid, sid = s.sb("gid", [P, NT], U32), s.sb("sid", [P, NT], U32)
        ps_in = [[s.ps(f"in{j}{b}") for j in range(IN)] for b in range(2)]
        ps_down = s.ps("down", (P, NT, D))
        ps_turn = [s.ps(f"turn{m}", (P, K, 2 * P)) for m in range(NMISC)]
        const_in = s.sem("const_in")
        raw_in = [s.sem(f"raw_in{r}") for r in range(W_RING)]
        bias_in = [s.sem(f"bias_in{b}") for b in range(2)]
        raw_hi, raw_lo = s.sem("raw_hi"), s.sem("raw_lo")
        rows_in, turned, xt_done = s.sem("rows_in"), s.sem("turned"), s.sem("xt_done")
        in_done, silu_done, act_done, down_done = (s.sem(n) for n in ("in_done", "silu_done", "act_done", "down_done"))
        read_out, out_done, scattered = s.sem("read_out"), s.sem("out_done"), s.sem("scattered")
        landed, gates_set = s.sem("landed"), s.sem("gates_set")
        dve_own, pool_own = s.sem("dve_own"), s.sem("pool_own")
        block = s.enter_context(nc.Block())
        ACT0, DOWN0, RAW0, XT0, READ0, OUT0 = 2, 4 * len(CH), W_RING, NMISC, len(CH), 2

        def experts(eng, one):
            with eng.Fori(0, E // 2 - 1) as i:
                one(i * 2, 0, 2)
                one(i * 2 + 1, 1, 2)
            one(E - 2, 0, 1)
            one(E - 1, 1, 0)

        @block.sync
        def _(sp):
            sp.dma_start(ident[:], consts[:, C_IDENT:C_IDENT + P]).then_inc(const_in, 16)

            def one(e, b, left):
                sp.wait_ge(out_done, e + 1)
                sp.dma_start(bias[:, b], bias_dram[ds(e, 1)].rearrange("e p c -> (e p) c")).then_inc(bias_in[b], 16)
                sp.dma_start(db[:, b], down_bias[ds(e, 1)].to_broadcast([P, D])).then_inc(bias_in[b], 16)
                for f in range(F_T):
                    sp.wait_ge(raw_hi, e * F_T + (f + 1))
                    sp.wait_ge(raw_lo, e * F_T + (f + 1))
                    sp.dma_start(raw[:, f % W_RING], w_dram[ds(e * F_T + f, 1)].rearrange("s p w -> (s p) w")
                                 ).then_inc(raw_in[f % W_RING], 16)

            experts(sp, one)

        @block.gpsimd
        def _(pool):
            own = Chain(pool, pool_own)
            PER = 2

            def gather(e):
                own.step(pool.tensor_copy(gid[:], gather_ids[:, ds(e, 1), :].rearrange("p e j -> p (e j)")), apart=True)
                for j in range(NT):
                    pool.indirect_dma_start(out=rows[:, j, :], out_offset=None, in_=h_rows,
                                            in_offset=bass.IndirectOffsetOnAxis(ap=gid[:, j:j + 1], axis=0)
                                            ).then_inc(rows_in, 16)

            def gather_after(e):
                pool.wait_ge(turned, e * NI + NI)
                wait_apart(pool, rows_in, e * (16 * NT) + 16 * NT)
                gather(e + 1)

            def low_part(e, f):
                n = e * F_T + f
                pool.wait_ge(raw_hi, n + (RAW0 + 1))
                r = f % W_RING
                pool.tensor_tensor(w_lo[:, r], raw[:, r], as_f32(w_hi[:, r]), ALU.subtract).then_inc(raw_lo, 1)

            gather(0)
            for f in range(AHEAD):
                low_part(0, f)
            gather_after(0)
            for f in range(AHEAD, LOW_AHEAD):
                low_part(0, f)

            def one(e, b, left):
                own.at(e * PER + (2 if left else 1))
                for f in range(LOW_AHEAD, F_T):
                    low_part(e, f)
                for f in range(LOW_AHEAD if left else 0):
                    low_part(e + 1, f)
                    if f == 0 and left > 1:
                        gather_after(e + 1)
                own.step(pool.tensor_copy(sid[:], scatter_ids[:, ds(e, 1), :].rearrange("p e j -> p (e j)")))
                wait_apart(pool, out_done, e + (OUT0 + 1))
                for j in range(NT):
                    pool.indirect_dma_start(out=acc, out_offset=bass.IndirectOffsetOnAxis(ap=sid[:, j:j + 1], axis=0),
                                            in_=out[:, b, j, :], in_offset=None, compute_op=ALU.add
                                            ).then_inc(scattered, 16)
                pool.wait_ge(scattered, e * (16 * NT) + 16 * NT)
                pool.nop().then_inc(landed, 1)

            experts(pool, one)

        @block.tensor
        def _(pe):
            pe.wait_ge(const_in, 16)

            def turn(e, i):
                if i == 0:
                    pe.wait_ge(rows_in, e * (16 * NT) + 16 * NT)
                pe.wait_ge(xt_done, e * NI + (i + 1))
                for k in range(K):
                    for t in range(2):
                        last = pe.transpose(ps_turn[i % NMISC][:, k, t * P:(t + 1) * P],
                                            rows[:, 2 * i + t, k * P:(k + 1) * P], ident[:])
                last.then_inc(turned, 1)

            def down(e, st):
                f, (t0, t1) = st // len(CH), CH[st % len(CH)]
                pe.wait_ge(act_done, e * S + (st + 1 + ACT0))
                if f == 0:
                    pe.wait_ge(read_out, e * len(CH) + (st + 1))
                for t in range(t0, t1):
                    at = slice((t - t0) * P, (t - t0 + 1) * P)
                    last = product(pe, ps_down[:, t, :], [a[:, st % 2, at] for a in (act_hi, act_lo)],
                                   [w[:, f % W_RING, IN * K * P:] for w in (w_hi, w_lo)],
                                   f == 0 and t % 2 == 0, f == F_T - 1)
                last.then_inc(down_done, 1)

            def into(e, st, b):
                f, (t0, t1) = st // len(CH), CH[st % len(CH)]
                if st == 0:
                    pe.wait_ge(xt_done, e * NI + (NI + XT0))
                if st % len(CH) == 0:
                    pe.wait_ge(raw_lo, e * F_T + (f + 1 + RAW0))
                pe.wait_ge(act_done, e * S + (st + 1))
                for j in range(IN):
                    for k in range(K):
                        w0 = (j * K + k) * P
                        last = product(pe, ps_in[st % 2][j][:, 0:(t1 - t0) * P],
                                       [w[:, f % W_RING, w0:w0 + P] for w in (w_hi, w_lo)],
                                       [x[:, b, k, t0 * P:t1 * P] for x in (xt_hi, xt_lo)],
                                       k == 0, k == K - 1)
                last.then_inc(in_done, 1)

            for i in range(NI):
                turn(0, i)
            into(0, 0, 0)

            def one(e, b, left):
                for st in range(1, S):
                    into(e, st, b)
                    if st in ITEM_AT and left:
                        turn(e + 1, ITEM_AT[st])
                    down(e, st - 1)
                if left:
                    into(e + 1, 0, 1 - b)
                down(e, S - 1)

            experts(pe, one)

        @block.scalar
        def _(act):
            def high_part(e, f):
                n = e * F_T + f
                act.wait_ge(raw_in[f % W_RING], (e * (F_T // W_RING) + (f // W_RING + 1)) * 16)
                act.wait_ge(down_done, (n + 1) * len(CH))
                act.copy(w_hi[:, f % W_RING], raw[:, f % W_RING]).then_inc(raw_hi, 1)

            def hidden(e, st, b):
                f, (t0, t1) = st // len(CH), CH[st % len(CH)]
                n = (t1 - t0) * P
                if st == 0:
                    act.wait_ge(bias_in[b], (e - b) * 16 + 32)
                act.wait_ge(in_done, e * S + (st + 1))
                act.wait_ge(act_done, e * S + (st + 1))
                dst, func = (silu, ACT.Silu) if gated else (act_f, ACT.Gelu)
                act.activation(dst[:, st % 2, 0:n], ps_in[st % 2][0][:, 0:n], func,
                               bias=bias[:, b, f:f + 1]).then_inc(silu_done, 1)

            def next_slice(e, st, left):
                if st % len(CH) == 0:
                    f = st // len(CH)
                    if f + AHEAD < F_T:
                        high_part(e, f + AHEAD)
                    elif left:
                        high_part(e + 1, f + AHEAD - F_T)

            def read_sums(e, st, b):
                t0, t1 = CH[st % len(CH)]
                if st == S - len(CH):
                    act.wait_ge(landed, e + 1)
                act.wait_ge(down_done, e * S + (st + 1 + DOWN0))
                act.wait_ge(gates_set, e + 1)
                for t in range(t0, t1):
                    ins = act.activation(out[:, b, t, :], ps_down[:, t, :], ACT.Copy, scale=gcol[:, b, t:t + 1])
                ins.then_inc(read_out, 1)

            for f in range(AHEAD):
                high_part(0, f)
            hidden(0, 0, 0)
            next_slice(0, 0, 1)

            def one(e, b, left):
                for st in range(1, S):
                    hidden(e, st, b)
                    if st > S - len(CH):
                        read_sums(e, st - 1, b)
                    next_slice(e, st, left)
                if left:
                    hidden(e + 1, 0, 1 - b)
                read_sums(e, S - 1, b)
                if left:
                    next_slice(e + 1, 0, left - 1)

            experts(act, one)

        @block.vector
        def _(dve):
            own = Chain(dve, dve_own)
            dve.sem_inc(act_done, ACT0)
            dve.sem_inc(down_done, DOWN0)
            dve.sem_inc(raw_hi, RAW0)
            dve.sem_inc(raw_lo, RAW0)
            dve.sem_inc(xt_done, XT0)
            dve.sem_inc(read_out, READ0)
            dve.sem_inc(out_done, OUT0)
            dve.sem_inc(landed, 2)

            def split_rows(e, i, b):
                dve.wait_ge(turned, e * NI + (i + 1))
                at = slice(2 * i * P, (2 * i + 2) * P)
                own.step(dve.tensor_copy(xt_hi[:, b, :, at], ps_turn[i % NMISC][:]))
                dve.tensor_tensor(xt_lo[:, b, :, at], ps_turn[i % NMISC][:], as_f32(xt_hi[:, b, :, at]),
                                  ALU.subtract).then_inc(xt_done, 1)

            def activate(e, st, b):
                f, (t0, t1) = st // len(CH), CH[st % len(CH)]
                n = (t1 - t0) * P
                act_n, hi_n, lo_n = (a[:, st % 2, 0:n] for a in (act_f, act_hi, act_lo))
                if st == 0:
                    dve.wait_ge(bias_in[b], (e - b) * 16 + 32)
                dve.wait_ge(silu_done, e * S + (st + 1))
                dve.wait_ge(down_done, e * S + (st + DOWN0 - 1))
                if gated:
                    own.step(dve.scalar_tensor_tensor(act_n, ps_in[st % 2][1][:, 0:n],
                                                      bias[:, b, F_T + f:F_T + f + 1], silu[:, st % 2, 0:n],
                                                      ALU.add, ALU.mult))
                own.step(dve.tensor_copy(hi_n, act_n))
                dve.tensor_tensor(lo_n, act_n, as_f32(hi_n), ALU.subtract).then_inc(act_done, 1)

            for i in range(NI):
                split_rows(0, i, 0)
            activate(0, 0, 0)
            first = own.n
            PER = NI + S * (2 if gated else 1)

            def gates(e, b):
                dve.tensor_copy(gcol[:, b], gate_cols[:, ds(e, 1), :].rearrange("p e j -> p (e j)")).then_inc(gates_set, 1)

            def add_bias(e, st, b):
                c = st % len(CH)
                dve.wait_ge(gates_set, e + 1)
                dve.wait_ge(read_out, e * len(CH) + (c + 1 + READ0))
                for j in range(*CH[c]):
                    ins = dve.scalar_tensor_tensor(out[:, b, j, :], db[:, b], gcol[:, b, j:j + 1], out[:, b, j, :],
                                                   ALU.mult, ALU.add)
                if st == S - 1:
                    ins.then_inc(out_done, 1)

            def one(e, b, left):
                own.at(e * PER + first)
                gates(e, b)
                for st in range(1, S):
                    activate(e, st, b)
                    if st > S - len(CH):
                        add_bias(e, st - 1, b)
                    if st in ITEM_AT and left:
                        split_rows(e + 1, ITEM_AT[st], 1 - b)
                if left:
                    activate(e + 1, 0, 1 - b)
                add_bias(e, S - 1, b)

            experts(dve, one)


def ffn(nc, tag, x_in, acc, gate_w, shared_w, ffn_w, ffn_b, ffn_db, consts):
    NT = FFN_CAP // P
    h_rows = nc.dram_tensor(f"{tag}_h", (N, D), F32, kind="Internal").ap()
    with Scope(nc, tag) as s:
        logits = s.sb("logits", [P, FFN_E, T])
        low, high = s.sb("low", [P, FFN_E]), s.sb("high", [P, FFN_E])
        ids = s.sb("ids", [P, FFN_E, NT], U32)
        ids2 = s.sb("ids2", [P, FFN_E, NT], U32)
        gates = s.sb("gates", [P, FFN_E, NT])
        with Scope(nc, tag) as s2:
            x_all = s2.sb("x_all", [P, T, D])
            ht_hi, ht_lo = s2.sb("ht_hi", [P, K, N], F32R), s2.sb("ht_lo", [P, K, N], F32R)
            norm_and_score(nc, tag + "n", x_in, gate_w, consts, h_rows, x_all, ht_hi, ht_lo, logits)
            shared_and_search(nc, tag + "s", shared_w, consts, x_all, ht_hi, ht_lo, logits, low, high, acc)
        make_lists(nc, tag + "l", FFN_E, NT, consts, logits, low, high, ids, ids2, gates)
        run_experts(nc, tag + "e", FFN_E, NT, True, ffn_w, ffn_b, ffn_db, consts, h_rows, acc, ids, ids2, gates)


def attention(nc, tag, x_in, acc, w, consts, x2_all, sums):
    Q = T // BATCH
    QK, VG = slice(0, 2 * D), slice(2 * D, 4 * D)
    HW = P + HALF
    with Scope(nc, tag) as s:
        ident, mask = s.sb("ident", [P, P]), s.sb("mask", [P, HW])
        w_hi, w_lo = s.sb("w_hi", [P, K, 4 * D], F32R), s.sb("w_lo", [P, K, 4 * D], F32R)
        wo, scale = s.sb("wo", [P, K, D]), s.sb("scale", [P, K])
        bias, bo, rope = s.sb("bias", [P, 4 * D]), s.sb("bo", [P, D]), s.sb("rope", [P, Q, 4, DK // 2])
        zeros = s.sb("zeros", [P, K * HW])
        x_all, v_all, eg_all = (s.sb(n, [P, T, D]) for n in ("x_all", "v_all", "eg_all"))
        w_raw = v_all[:, 0:4 * K, :].rearrange("p (k t) d -> p k (t d)", k=K)
        neg_half = s.sb("neg_half", [P, 1])
        stats, mv = s.sb("stats", [P, 2, 6]), s.sb("mv", [P, 2, 2])
        rs = s.sb("rs", [P, 2, 4])
        a = s.sb("a", [P, 2, D])
        at_hi, at_lo = s.sb("at_hi", [P, 2, K, P], F32R), s.sb("at_lo", [P, 2, K, P], F32R)
        qk, rot_a, rot_b, rot, er, pos_part, phi = (
            s.sb(n, [P, 2, 2 * D]) for n in ("qk", "rot_a", "rot_b", "rot", "er", "pos_part", "phi"))
        gp = s.sb("gp", [P, 2, D])
        v1 = s.sb("v1", [P, 2, 2, HW])
        qt = s.sb("qt", [P, 2, K, P])
        state = s.sb("state", [P, 2, 2, 2, HW])
        den, div, o = s.sb("den", [P, HEADS]), s.sb("div", [P, D]), s.sb("o", [P, 2, D])
        ot = s.sb("ot", [P, K, P])
        square = zeros[:, 0:D]
        total = s.sb("total", [P, 2, D])
        ps_a, ps_qt = s.ps("ps_a", (P, K, P)), s.ps("ps_qt", (P, K, P))
        ps_qk, ps_vg = s.ps("ps_qk"), s.ps("ps_vg")
        ps_state = [s.ps(f"state{u}", (P, 2, HW)) for u in range(2)]
        ps_num, ps_o = s.ps("ps_num", (P, 2, HW)), s.ps("ps_o", (P, 2, D))
        const_in, w_hi_done, w_lo_done, set_up = (s.sem(n) for n in ("const_in", "w_hi_done", "w_lo_done", "set_up"))
        x_in_s = [s.sem(f"x_in{u}") for u in range(2)]
        stored = [s.sem(f"stored{u}") for u in range(2)]
        (stat_done, rs_done, a_done, xtb_done, a_turned, at_hi_done, at_done, proj_done, proj_read, gp_done, eg_done,
         rot_a_done, rot_b_done, rot_done, er_done, phi_done, v1_done, q_turned, qt_done, s0_done, m0_done, s1_done,
         m1_done, num_done, o_done, o_turned, ot_done, wo_done, x2_done, sum_done, total_done) = (
            s.sem(n) for n in (
                "stat_done", "rs_done", "a_done", "xtb_done", "a_turned", "at_hi_done", "at_done", "proj_done",
                "proj_read", "gp_done", "eg_done", "rot_a_done", "rot_b_done", "rot_done", "er_done", "phi_done",
                "v1_done", "q_turned", "qt_done", "s0_done", "m0_done", "s1_done", "m1_done", "num_done", "o_done",
                "o_turned", "ot_done", "wo_done", "x2_done", "sum_done", "total_done"))
        own_aggr, own_xt, own_qk, own_den, own_div, own_rs, own_var, own_sq, own_ratio = (
            s.sem(n) for n in ("own_aggr", "own_xt", "own_qk", "own_den", "own_div", "own_rs", "own_var", "own_sq",
                               "own_ratio"))
        own_inv = s.sem("own_inv")
        block = s.enter_context(nc.Block())
        N_CONST = 8

        def row(arr, q, u):
            return arr[:, ds(q + u * Q, 1), :].rearrange("p t d -> p (t d)")

        def rows_of(dram, q, u):
            return dram[ds(q * P + u * SEQ, P), :]

        @block.sync
        def _(sp):
            for dst, src in ((ident[:], consts[:, C_IDENT:C_IDENT + P]), (mask[:], consts[:, C_MASK:C_MASK + HW]),
                             (w_raw, w["qkvg"]), (wo[:], w["wo"]), (scale[:], w["norm1"]),
                             (bias[:], w["qkvg_b"].to_broadcast([P, 4 * D])), (bo[:], w["bo"].to_broadcast([P, D])),
                             (rope[:].rearrange("p q c j -> p q (c j)"), w["rope"])):
                sp.dma_start(dst, src).then_inc(const_in, 16)

            def load(q, u):
                sp.wait_ge(a_done, q * 2 + (u + 1))
                sp.dma_start(row(x_all, q, u), rows_of(x_in, q, u)).then_inc(x_in_s[u], 16)

            def store(q, u):
                sp.wait_ge(total_done, q * 2 + (u + 3))
                sp.dma_start(rows_of(acc, q, u), total[:, u]).then_inc(stored[u], 16)

            pipelined(sp, T, [(10, store), (0, load)])
            for u in range(2):
                sp.wait_ge(stored[u], 16 * Q + 16)

        @block.gpsimd
        def _(pool):
            pool.memset(neg_half[:], -0.5).then_inc(own_rs, 1)
            pool.wait_ge(own_rs, 1)
            pool.wait_ge(const_in, 16 * N_CONST)
            pool.wait_ge(w_hi_done, 1)
            pool.tensor_tensor(w_lo[:], w_raw, as_f32(w_hi[:]), ALU.subtract).then_inc(w_lo_done, 1)

            def root(q, u):
                h = q * 2 + u
                wait_apart(pool, a_done, h + 1)
                wait_apart(pool, stat_done, h + 1)
                var = mv[:, u, 1:2]
                pool.tensor_scalar(rs[:, u, 0:1], var, EPS, None, ALU.add).then_inc(own_var, 1)
                pool.wait_ge(own_var, h + 1)
                pool.tensor_tensor(rs[:, u, 1:2], rs[:, u, 0:1], neg_half[:], ALU.pow).then_inc(own_inv, 1)
                pool.wait_ge(own_inv, h + 1)
                pool.tensor_tensor(rs[:, u, 2:3], rs[:, u, 1:2], rs[:, u, 1:2], ALU.mult).then_inc(own_sq, 1)
                pool.wait_ge(own_sq, h + 1)
                pool.tensor_tensor(rs[:, u, 2:3], rs[:, u, 2:3], var, ALU.mult).then_inc(own_ratio, 1)
                pool.wait_ge(own_ratio, h + 1)
                pool.tensor_tensor(rs[:, u, 3:4], rs[:, u, 2:3], neg_half[:], ALU.pow).then_inc(rs_done, 1)

            def add_bo(q, u):
                wait_apart(pool, a_done, q * 2 + (u + 3))
                pool.tensor_tensor(row(x2_all, q, u), row(x2_all, q, u), bo[:], ALU.add).then_inc(xtb_done, 1)

            def rotate(q, u):
                h = q * 2 + u
                pool.wait_ge(rot_done, h + 1)
                pool.wait_ge(er_done, h + 1)
                wait_apart(pool, rot_a_done, h + 1)
                src = qk[:, u].rearrange("p (h c j) -> p h c j", c=2, j=DK // 2)
                dst = rot_b[:, u].rearrange("p (h c j) -> p h c j", c=2, j=DK // 2)
                for c in range(2):
                    ins = pool.tensor_tensor(dst[:, :, c, :], src[:, :, 1 - c, :],
                                             rope[:, ds(q, 1), 2 + c, :].to_broadcast([P, 2 * HEADS, DK // 2]), ALU.mult)
                ins.then_inc(rot_b_done, 1)
                pool.wait_ge(rot_b_done, h + 1)
                pool.tensor_tensor(rot[:, u], rot_a[:, u], rot_b[:, u], ALU.add).then_inc(rot_done, 1)

            def residual(q, u):
                h = q * 2 + u
                pool.wait_ge(x2_done, h + 2)
                wait_apart(pool, stored[u], q * 16 + 16)
                pool.tensor_tensor(total[:, u], row(x_all, q, u), row(x2_all, q, u), ALU.add).then_inc(total_done, 1)

            pipelined(pool, T, [(10, residual), (4, rotate), (0, root), (1, add_bo)])

        @block.tensor
        def _(pe):
            pe.wait_ge(w_lo_done, 1)
            pe.wait_ge(set_up, 1)
            for u in range(2):
                pe.matmul(ps_state[u][:].rearrange("p k c -> p (k c)"), zeros[:, 0:P], zeros[:], start=True, stop=False,
                          skip_group_check=True)

            def turn_a(q, u):
                h = q * 2 + u
                pe.wait_ge(a_done, h + 3)
                pe.wait_ge(at_done, h + 1)
                for k in range(K):
                    ins = pe.transpose(ps_a[:, k, :], a[:, u, k * P:(k + 1) * P], ident[:])
                ins.then_inc(a_turned, 1)

            def project(q, u):
                h = q * 2 + u
                pe.wait_ge(at_done, h + 2)
                pe.wait_ge(proj_read, h + 1)
                for ps, cols in ((ps_qk, QK), (ps_vg, VG)):
                    for k in range(K):
                        ins = product(pe, ps[:], [x[:, u, k, :] for x in (at_hi, at_lo)],
                                      [x[:, k, cols] for x in (w_hi, w_lo)], k == 0, k == K - 1)
                ins.then_inc(proj_done, 1)

            def add_chunk(c, u):
                at = slice(c * CHUNK, (c + 1) * CHUNK)
                for k in range(2):
                    ins = pe.matmul(ps_state[u][:, k, :], phi[at, u, D + k * P:D + (k + 1) * P], v1[at, u, k, :],
                                    start=False, stop=True, skip_group_check=True)
                return ins

            def chunk0(q, u):
                h = q * 2 + u
                pe.wait_ge(phi_done, h + 1)
                pe.wait_ge(v1_done, h + 3)
                pe.wait_ge(qt_done, h + 1)
                for k in range(K):
                    ins = pe.transpose(ps_qt[:, k, :], phi[:, u, k * P:(k + 1) * P], ident[:])
                ins.then_inc(q_turned, 1)
                pe.wait_ge(m1_done, h + 1)
                add_chunk(0, u).then_inc(s0_done, 1)

            def chunk1(q, u):
                pe.wait_ge(m0_done, q * 2 + (u + 1))
                add_chunk(1, u).then_inc(s1_done, 1)

            def numerators(q, u):
                h = q * 2 + u
                pe.wait_ge(m1_done, h + 3)
                pe.wait_ge(qt_done, h + 2)
                pe.wait_ge(o_done, h + 1)
                for c in range(2):
                    at = slice(c * CHUNK, (c + 1) * CHUNK)
                    for k in range(2):
                        ins = pe.matmul(ps_num[at, k, :], qt[:, u, k, at], state[:, u, c, k, :], start=(k == 0), stop=True,
                                        skip_group_check=True)
                ins.then_inc(num_done, 1)

            def turn_o(q, u):
                h = q * 2 + u
                pe.wait_ge(o_done, h + 2)
                pe.wait_ge(x2_done, h + 1)
                for k in range(K):
                    ins = pe.transpose(ps_o[:, 0, k * P:(k + 1) * P], o[:, u, k * P:(k + 1) * P], ident[:])
                ins.then_inc(o_turned, 1)

            def project_o(q, u):
                pe.wait_ge(ot_done, q * 2 + (u + 1))
                for k in range(K):
                    ins = pe.matmul(ps_o[:, 1, :], ot[:, k, :], wo[:, k, :], start=(k == 0), stop=(k == K - 1))
                ins.then_inc(wo_done, 1)

            pipelined(pe, T, [(7, chunk1), (6, chunk0), (8, numerators), (2, turn_a), (3, project), (9, turn_o),
                              (9, project_o)])

        @block.scalar
        def _(act):
            act.wait_ge(const_in, 16 * N_CONST)
            act.copy(w_hi[:], w_raw).then_inc(w_hi_done, 1)

            def split_at(q, u):
                h = q * 2 + u
                act.wait_ge(a_turned, h + 1)
                act.wait_ge(proj_done, h + 1)
                for k in range(K):
                    ins = act.activation(at_hi[:, u, k, :], ps_a[:, k, :], ACT.Copy, scale=scale[:, k:k + 1])
                ins.then_inc(at_hi_done, 1)

            def exp_gate(q, u):
                act.wait_ge(gp_done, q * 2 + (u + 1))
                act.activation(row(eg_all, q, u), gp[:, u], ACT.Exp, scale=-1.0).then_inc(eg_done, 1)

            def exp_rot(q, u):
                h = q * 2 + u
                act.wait_ge(rot_done, h + 3)
                act.activation(er[:, u], rot[:, u], ACT.Exp)
                act.activation(pos_part[:, u], rot[:, u], ACT.Relu).then_inc(er_done, 1)

            def values(q, u):
                act.wait_ge(s1_done, q * 2 + (u + 1))
                act.copy(v1[:, u, :, 0:P], row(v_all, q, u).rearrange("p (k c) -> p k c", k=2)).then_inc(v1_done, 1)

            def copy_qt(q, u):
                h = q * 2 + u
                act.wait_ge(q_turned, h + 1)
                act.wait_ge(num_done, h + 1)
                act.copy(qt[:, u], ps_qt[:]).then_inc(qt_done, 1)

            def copy_ot(q, u):
                h = q * 2 + u
                act.wait_ge(o_turned, h + 1)
                act.wait_ge(wo_done, h + 1)
                act.copy(ot[:].rearrange("p k c -> p (k c)"), ps_o[:, 0, :]).then_inc(ot_done, 1)

            def sum_squares(q, u):
                act.wait_ge(x2_done, q * 2 + (u + 2))
                act.wait_ge(sum_done, q * 2 + (u + 1))
                act.activation(square, row(x2_all, q, u), ACT.Square,
                               accum_out=sums[:, ds(q + u * Q, 1)]).then_inc(sum_done, 1)

            pipelined(act, T, [(5, exp_rot), (6, copy_qt), (9, copy_ot), (5, values), (2, split_at), (4, exp_gate),
                               (10, sum_squares)])

        @block.vector
        def _(dve):
            for sem, free in ((a_done, 2), (at_done, 1), (proj_done, 2), (proj_read, 1), (rot_done, 2), (er_done, 2), (s1_done, 2),
                              (v1_done, 2), (qt_done, 1), (m1_done, 2), (num_done, 2), (o_done, 1), (x2_done, 1),
                              (wo_done, 1), (sum_done, 1), (total_done, 2), (stored[0], 16), (stored[1], 16)):
                dve.sem_inc(sem, free)
            dve.memset(zeros[:], 0.0)
            dve.memset(v1[:], 1.0).then_inc(set_up, 1)
            dve.wait_ge(const_in, 16 * N_CONST)

            def stat(q, u):
                h = q * 2 + u
                dve.wait_ge(x_in_s[u], q * 16 + 16)
                dve.bn_stats(stats[:, u], row(x_all, q, u)).then_inc(own_aggr, 1)
                wait_apart(dve, own_aggr, h + 1)
                dve.bn_aggr(mv[:, u], stats[:, u]).then_inc(stat_done, 1)

            def norm(q, u):
                h = q * 2 + u
                dve.wait_ge(rs_done, h + 1)
                dve.tensor_scalar(row(x2_all, q, u), row(x_all, q, u), mv[:, u, 0:1], rs[:, u, 1:2], ALU.subtract,
                                  ALU.mult).then_inc(own_xt, 1)
                dve.wait_ge(own_xt, h + 1)
                dve.tensor_scalar(a[:, u], row(x2_all, q, u), rs[:, u, 3:4], None, ALU.mult).then_inc(a_done, 1)

            def split_low(q, u):
                dve.wait_ge(at_hi_done, q * 2 + (u + 1))
                for k in range(K):
                    ins = dve.scalar_tensor_tensor(at_lo[:, u, k, :], ps_a[:, k, :], scale[:, k:k + 1],
                                                   as_f32(at_hi[:, u, k, :]), ALU.mult, ALU.subtract)
                ins.then_inc(at_done, 1)

            def add_bias(q, u):
                h = q * 2 + u
                dve.wait_ge(proj_done, h + 3)
                dve.tensor_tensor(gp[:, u], ps_vg[:, D:2 * D], bias[:, 3 * D:4 * D], ALU.add).then_inc(gp_done, 1)
                dve.wait_ge(rot_done, h + 1)
                dve.tensor_tensor(qk[:, u], ps_qk[:], bias[:, QK], ALU.add).then_inc(own_qk, 1)
                dve.tensor_tensor(row(v_all, q, u), ps_vg[:, 0:D], bias[:, 2 * D:3 * D], ALU.add).then_inc(proj_read, 1)
                dve.wait_ge(own_qk, h + 1)
                dve.tensor_tensor(rot_a[:, u].rearrange("p (h c) -> p h c", c=DK),
                                  qk[:, u].rearrange("p (h c) -> p h c", c=DK),
                                  rope[:, ds(q, 1), 0:2, :].rearrange("p q c j -> p q (c j)")
                                  .to_broadcast([P, 2 * HEADS, DK]), ALU.mult).then_inc(rot_a_done, 1)

            def feature(q, u):
                dve.wait_ge(er_done, q * 2 + (u + 3))
                dve.wait_ge(s1_done, q * 2 + (u + 1))
                dve.scalar_tensor_tensor(phi[:, u], er[:, u], 1.0, pos_part[:, u], ALU.min, ALU.add).then_inc(phi_done, 1)

            def copy_state(c, q, u):
                dve.tensor_tensor(state[:, u, c], ps_state[u][:], mask[:].unsqueeze(1).to_broadcast([P, 2, HW]), ALU.mult
                                  ).then_inc((m0_done, m1_done)[c], 1)

            def state0(q, u):
                dve.wait_ge(s0_done, q * 2 + (u + 1))
                dve.wait_ge(num_done, q * 2 + (u + 1))
                copy_state(0, q, u)

            def state1(q, u):
                dve.wait_ge(s1_done, q * 2 + (u + 3))
                copy_state(1, q, u)

            def divide(q, u):
                h = q * 2 + u
                dve.wait_ge(num_done, h + 3)
                dve.wait_ge(eg_done, h + 1)
                dve.tensor_scalar(den[:].rearrange("p (k h) -> p k h", k=2), ps_num[:, :, P:], 1e-6, None, ALU.add
                                  ).then_inc(own_den, 1)
                dve.wait_ge(own_den, h * 2 + 1)
                dve.scalar_tensor_tensor(div[:].rearrange("p (h c) -> p h c", c=DK),
                                         row(eg_all, q, u).rearrange("p (h c) -> p h c", c=DK), 1.0,
                                         den[:].unsqueeze(2).to_broadcast([P, HEADS, DK]), ALU.add, ALU.mult
                                         ).then_inc(own_den, 1)
                dve.wait_ge(own_den, h * 2 + 2)
                dve.reciprocal(div[:], div[:]).then_inc(own_div, 1)
                dve.wait_ge(own_div, h + 1)
                dve.tensor_tensor(o[:, u].rearrange("p (k c) -> p k c", k=2), ps_num[:, :, 0:P],
                                  div[:].rearrange("p (k c) -> p k c", k=2), ALU.mult).then_inc(o_done, 1)

            def add_out(q, u):
                h = q * 2 + u
                dve.wait_ge(wo_done, h + 2)
                dve.wait_ge(xtb_done, h + 1)
                dve.tensor_tensor(row(x2_all, q, u), ps_o[:, 1, :], row(x2_all, q, u), ALU.add).then_inc(x2_done, 1)

            pipelined(dve, T, [(4, add_bias), (7, state1), (10, add_out), (6, state0), (8, divide), (5, feature),
                               (1, norm), (0, stat), (2, split_low)])


def route(nc, tag, w, consts, x2_all, sums, h_rows, logits, spare):
    with Scope(nc, tag) as s:
        ident, router = s.sb("ident", [P, P]), s.sb("router", [P, K, MOE_E])
        scale, rb = s.sb("scale", [P, D]), s.sb("rb", [P, MOE_E])
        neg_half, root = s.sb("neg_half", [P, T]), s.sb("root", [P, T])
        zeros = s.sb("zeros", [P, D])
        h = s.sb("h", [P, 2, 2, D])
        ht = s.sb("ht", [P, 2, 2, K, P])
        turned = [s.ps(f"turned{b}", (P, 2, K, P)) for b in range(2)]
        scored = [s.ps(f"scored{b}", (P, 2, MOE_E)) for b in range(2)]
        const_in, mean_done, root_done, h_done, turn_done, ht_done, score_done, logit_done = (
            s.sem(n) for n in ("const_in", "mean_done", "root_done", "h_done", "turn_done", "ht_done", "score_done",
                               "logit_done"))
        h_out = [s.sem(f"h_out{b}") for b in range(2)]
        pool_own, zeros_done, spare_out = s.sem("pool_own"), s.sem("zeros_done"), s.sem("spare_out")
        block = s.enter_context(nc.Block())
        R = T // 2

        @block.sync
        def _(sp):
            for dst, src in ((ident[:], consts[:, C_IDENT:C_IDENT + P]), (router[:], w["router"]),
                             (scale[:], w["norm2"].to_broadcast([P, D])), (rb[:], w["router_b"].to_broadcast([P, MOE_E]))):
                sp.dma_start(dst, src).then_inc(const_in, 16)

            def store(q, u):
                sp.wait_ge(h_done, q * 2 + (u + 3))
                sp.dma_start(h_rows[ds((q * 2 + u) * (2 * P), 2 * P), :].rearrange("(t p) d -> p t d", p=P), h[:, u]
                             ).then_inc(h_out[u], 16)

            pipelined(sp, R, [(0, store)])
            for b in range(2):
                sp.wait_ge(h_out[b], 16 * (R // 2) + 16)

        @block.gpsimd
        def _(pool):
            pool.memset(zeros[:], 0.0).then_inc(zeros_done, 1)
            pool.memset(neg_half[:], -0.5).then_inc(pool_own, 1)
            pool.wait_ge(pool_own, 1)
            pool.wait_ge(mean_done, 1)
            pool.tensor_tensor(root[:], root[:], neg_half[:], ALU.pow).then_inc(root_done, 1)

        @block.tensor
        def _(pe):
            pe.wait_ge(const_in, 64)

            def turn(q, u):
                r = q * 2 + u
                pe.wait_ge(h_done, r + 3)
                pe.wait_ge(ht_done, r + 1)
                for t in range(2):
                    for k in range(K):
                        ins = pe.transpose(turned[u][:, t, k, :], h[:, u, t, k * P:(k + 1) * P], ident[:])
                ins.then_inc(turn_done, 1)

            def score(q, u):
                r = q * 2 + u
                pe.wait_ge(ht_done, r + 3)
                pe.wait_ge(logit_done, r + 1)
                for t in range(2):
                    for k in range(K):
                        ins = pe.matmul(scored[u][:, t, :], ht[:, u, t, k, :], router[:, k, :], start=(k == 0),
                                        stop=(k == K - 1))
                ins.then_inc(score_done, 1)

            pipelined(pe, R, [(0, turn), (1, score)])

        @block.scalar
        def _(act):
            act.wait_ge(zeros_done, 1)
            act.dma_start(spare.rearrange("(t p) d -> p t d", p=P),
                          zeros[:].unsqueeze(1).to_broadcast([P, MOE_CAP // P, D])).then_inc(spare_out, 16)

            def copy_turned(q, u):
                r = q * 2 + u
                act.wait_ge(turn_done, r + 3)
                act.wait_ge(score_done, r + 1)
                act.copy(ht[:, u], turned[u][:]).then_inc(ht_done, 1)

            pipelined(act, R, [(0, copy_turned)])
            act.wait_ge(spare_out, 16)

        @block.vector
        def _(dve):
            for sem, free in ((h_done, 2), (ht_done, 2), (logit_done, 2), (score_done, 2), (turn_done, 2), (h_out[0], 16), (h_out[1], 16)):
                dve.sem_inc(sem, free)
            dve.tensor_scalar(root[:], sums[:], 1.0 / D, None, ALU.mult).then_inc(mean_done, 1)
            dve.wait_ge(const_in, 64)
            dve.wait_ge(root_done, 1)

            def norm(q, u):
                r = q * 2 + u
                dve.wait_ge(h_out[u], q * 16 + 16)
                dve.wait_ge(turn_done, r + 1)
                for t in range(2):
                    at = ds(r * 2 + t, 1)
                    ins = dve.scalar_tensor_tensor(h[:, u, t], x2_all[:, at, :].rearrange("p t d -> p (t d)"),
                                                   root[:, at], scale[:], ALU.mult, ALU.mult)
                ins.then_inc(h_done, 1)

            def keep_logits(q, u):
                r = q * 2 + u
                dve.wait_ge(score_done, r + 3)
                dve.tensor_tensor(logits[:, ds(r * 2, 2), :], scored[u][:],
                                  rb[:].unsqueeze(1).to_broadcast([P, 2, MOE_E]), ALU.add).then_inc(logit_done, 1)

            pipelined(dve, R, [(0, norm), (2, keep_logits)])
            dve.wait_ge(logit_done, R + 2)


def attention_and_moe(nc, tag, x_in, acc, w, consts):
    NT = MOE_CAP // P
    h_rows = nc.dram_tensor(f"{tag}_h", (N, D), F32, kind="Internal").ap()
    with Scope(nc, tag) as s:
        logits = s.sb("logits", [P, T, MOE_E])
        ids, ids2 = s.sb("ids", [P, MOE_E, NT], U32), s.sb("ids2", [P, MOE_E, NT], U32)
        gates = s.sb("gates", [P, MOE_E, NT])
        with Scope(nc, tag) as s2:
            x2_all, sums = s2.sb("x2_all", [P, T, D]), s2.sb("sums", [P, T])
            attention(nc, tag + "a", x_in, acc, w, consts, x2_all, sums)
            route(nc, tag + "r", w, consts, x2_all, sums, h_rows, logits, acc[N:N + MOE_CAP])
        make_lists(nc, tag + "l", MOE_E, NT, consts, logits, None, None, ids, ids2, gates)
        run_experts(nc, tag + "e", MOE_E, NT, False, w["moe_w"], w["moe_b"], w["moe_db"], consts, h_rows, acc,
                    ids, ids2, gates)


def macaron(nc, w, out):
    acc1 = nc.dram_tensor("after_ffn1", (N, D), F32, kind="Internal").ap()
    acc2 = nc.dram_tensor("after_moe", (N + MOE_CAP, D), F32, kind="Internal").ap()
    ffn_w = (w["gate_w"], w["shared_w"], w["ffn_w"], w["ffn_b"], w["ffn_db"], w["consts"])
    ffn(nc, "f1", w["x"], acc1, *ffn_w)
    attention_and_moe(nc, "m", acc1, acc2, w, w["consts"])
    ffn(nc, "f2", acc2, out, *ffn_w)


def constants():
    c = np.zeros((P, C_ALL), np.float32)
    p = np.arange(P)
    c[:, C_IDENT:C_IDENT + P] = np.eye(P)
    c[:, C_TRI:C_TRI + P] = p[:, None] < p[None, :]
    c[:, C_IOTA:C_IOTA + P] = p
    c[:, C_TILE:C_TILE + T] = np.arange(T)
    c[:, C_SLOTHI:C_SLOTHI + 16] = np.arange(16)
    c[:, C_RESET:C_RESET + T] = np.arange(T) > 0
    c[:, C_ROW] = p
    c[:, C_MASK:C_MASK + P] = p[:, None] // DK == p[None, :] // DK
    c[:, C_MASK + P:] = p[:, None] // DK == np.arange(HALF)[None, :]
    return c


def rope_table():
    half = DK // 2
    inv = np.float32(1) / np.float32(10000) ** (np.arange(half, dtype=np.float32) / np.float32(half))
    ang = np.arange(SEQ, dtype=np.float32)[:, None] * inv[None, :]
    sin, cos = np.sin(ang), np.cos(ang)
    table = np.concatenate([cos, cos, -sin, sin], axis=1).astype(np.float32)
    return np.ascontiguousarray(table.reshape(SEQ // P, P, 4 * half).transpose(1, 0, 2))


def k_tiles(w):
    return np.ascontiguousarray(w.reshape(K, P, -1).transpose(1, 0, 2))


def hidden_slices(ins, down):
    E, F = down.shape[:2]
    parts = [w.reshape(E, F // P, P, K, P).transpose(0, 1, 4, 3, 2).reshape(E * F // P, P, D) for w in ins]
    return np.ascontiguousarray(np.concatenate(parts + [down.reshape(E * F // P, P, D)], axis=2))


def lay_out(i):
    a = {k.removeprefix("L0_"): np.asarray(v) for k, v in i.items()}
    by_tile = lambda b: b.reshape(b.shape[0], -1, P).transpose(0, 2, 1)
    o = {"consts": constants(), "x": np.ascontiguousarray(a["attn_x"].reshape(N, D))}
    o["gate_w"] = k_tiles(a["ffn_gate_w"].T)
    o["shared_w"] = hidden_slices([a["ffn_sh_gate_w"][None], a["ffn_sh_up_w"][None]],
                                  a["ffn_sh_down_w"].T[None])
    o["ffn_w"] = hidden_slices([a["ffn_gw"], a["ffn_up_w"]], a["ffn_down_w"].transpose(0, 2, 1))
    o["ffn_b"] = np.ascontiguousarray(np.concatenate([by_tile(a["ffn_gb"]), by_tile(a["ffn_up_b"])], axis=2))
    o["ffn_db"] = a["ffn_down_b"]
    o["moe_w"] = hidden_slices([a["attn_W1"].transpose(0, 2, 1)], a["attn_W2"])
    o["moe_b"], o["moe_db"] = np.ascontiguousarray(by_tile(a["attn_b1"])), a["attn_b2"]
    o["qkvg"] = k_tiles(np.concatenate([a[f"attn_W{c}"] for c in "qkvg"], axis=1))
    o["qkvg_b"] = np.concatenate([a[f"attn_b{c}"] for c in "qkvg"])[None]
    o["wo"], o["bo"] = k_tiles(a["attn_Wo"]), a["attn_bo"][None]
    o["norm1"] = np.ascontiguousarray(a["attn_norm1_scale"].reshape(K, P).T)
    o["norm2"] = a["attn_norm2_scale"][None]
    o["router"], o["router_b"] = k_tiles(a["attn_router_W"]), a["attn_router_b"][None]
    o["rope"] = rope_table()
    return o


def kernel(**inputs):
    import concourse.bacc as bacc
    from concourse.bass_utils import run_bass_kernel_spmd

    arrays = lay_out(inputs)
    nc = bacc.Bacc("TRN2", target_bir_lowering=False, num_devices=1)
    w = {n: nc.dram_tensor(f"in_{n}", a.shape, mybir.dt.from_np(a.dtype), kind="ExternalInput").ap()
         for n, a in arrays.items()}
    out = nc.dram_tensor("out", (N, D), F32, kind="ExternalOutput").ap()
    macaron(nc, w, out)
    r = run_bass_kernel_spmd(nc, [{f"in_{n}": a for n, a in arrays.items()}], core_ids=[0])
    return r.results[0]["out"].reshape(BATCH, SEQ, D)
```

```python
from contextlib import ExitStack

import numpy as np

import concourse.bass as bass
from concourse import mybir

P = 128
ALU = mybir.AluOpType
ACT = mybir.ActivationFunctionType
AX = mybir.AxisListType
F32 = mybir.dt.float32
F32R = mybir.dt.float32r
BF16 = mybir.dt.bfloat16
I32 = mybir.dt.int32
U32 = mybir.dt.uint32
ds = bass.ds

BATCH, SEQ, D = 2, 2048, 256
N = BATCH * SEQ
T = N // P
K = D // P
EPS = 1e-5

FFN_E, FFN_F, FFN_CAP, SHARED_F = 16, 1024, N // 16 * 2, 512
MOE_E, MOE_F, MOE_CAP = 8, 1024, int(1.25 * (8 * 1024 / 8))
HEADS, DK, CHUNK = 16, 16, 64
HALF = P // DK

GT = 4
G = T // GT
W_RING = 4
IDC = 5

C_IDENT, C_TRI, C_IOTA = 0, P, 2 * P
C_TILE = 3 * P
C_SLOTHI = C_TILE + T
C_RESET = C_SLOTHI + 16
C_ROW = C_RESET + T
C_MASK = C_ROW + 1
C_ALL = C_MASK + P + HALF


class Scope(ExitStack):

    def __init__(self, nc, tag):
        super().__init__()
        self.nc, self.tag, self.sems = nc, tag, []
        self.callback(self.clear)

    def sb(self, name, shape, dt=F32):
        return self.enter_context(self.nc.sbuf_tensor(f"{self.tag}_{name}", shape, dt))

    def ps(self, name, shape=(P, 512), dt=F32):
        return self.enter_context(self.nc.psum_tensor(f"{self.tag}_{name}", list(shape), dt))

    def sem(self, name):
        self.sems.append(self.nc.alloc_semaphore(name=f"{self.tag}_{name}"))
        return self.sems[-1]

    def clear(self):
        if self.sems:
            self.nc.clear_and_free_semaphores(self.sems)
            self.nc.all_engine_barrier()


class Chain:

    def __init__(self, eng, sem):
        self.eng, self.sem, self.base, self.n = eng, sem, 0, 0

    def at(self, base):
        self.base, self.n = base, 0

    def step(self, ins, apart=False):
        ins.then_inc(self.sem, 1)
        self.n += 1
        if apart:
            wait_apart(self.eng, self.sem, self.base + self.n)
        else:
            self.eng.wait_ge(self.sem, self.base + self.n)


def wait_apart(eng, sem, value):
    eng.wait_ge(sem, value)
    eng.nop(nofuse=True)


def product(pe, out, left, right, first, last):
    (lh, ll), (rh, rl) = left, right
    pe.matmul(out, lh, rh, start=first, stop=False, skip_group_check=True)
    pe.matmul(out, lh, rl, start=False, stop=False, skip_group_check=True)
    return pe.matmul(out, ll, rh, start=False, stop=last, skip_group_check=True)


def as_f32(ap):
    return ap.bitcast(F32)


def pipelined(eng, tiles, stages):
    deep = -(-max(lag for lag, _ in stages) // 2) * 2
    end = tiles + deep

    def round_(r):
        for lag, step in stages:
            if 0 <= r - lag < tiles:
                step((r - lag) // 2, (r - lag) % 2)

    for r in range(deep):
        round_(r)
    with eng.Fori(0, (tiles - deep) // 2) as i:
        for u in range(2):
            for lag, step in stages:
                step(i + (deep + u - lag) // 2, (u - lag) % 2)
    for r in range(tiles, end):
        round_(r)


def norm_and_score(nc, tag, x_in, gate_w, consts, h_rows, x_all, ht_hi, ht_lo, logits, w_dram, w_hi, w_lo):
    E = gate_w.shape[2]
    with Scope(nc, tag) as s:
        ident = s.sb("ident", [P, P])
        gate = s.sb("gate", [P, K, E])
        neg_half = s.sb("neg_half", [P, GT])
        stats = s.sb("stats", [P, 2, GT, 6])
        mv = s.sb("mv", [P, 2, GT, 2])
        var_eps = s.sb("var_eps", [P, 2, GT])
        rstd = s.sb("rstd", [P, 2, GT])
        raw = s.sb("raw", [P, w_hi.shape[1] * w_hi.shape[2]])
        PIECE = raw.shape[1] // G
        h = s.sb("h", [P, 2, GT, D])
        ht = s.sb("ht", [P, 2, K, GT * P])
        turned = [s.ps(f"turned{b}", (P, K, GT * P)) for b in range(2)]
        scored = [s.ps(f"scored{b}", (P, GT, E)) for b in range(2)]
        const_in, x_in_s = s.sem("const_in"), [s.sem(f"x_in{b}") for b in range(2)]
        w_in, w_hi_done, w_lo_done = s.sem("w_in"), s.sem("w_hi_done"), s.sem("w_lo_done")
        stat_done, rstd_done, h_done = s.sem("stat_done"), s.sem("rstd_done"), s.sem("h_done")
        h_out = [s.sem(f"h_out{b}") for b in range(2)]
        turn_done, ht_done, hi_done = s.sem("turn_done"), s.sem("ht_done"), s.sem("hi_done")
        lo_done, score_done, logit_done = s.sem("lo_done"), s.sem("score_done"), s.sem("logit_done")
        dve_own, pool_own, half_done = s.sem("dve_own"), s.sem("pool_own"), s.sem("half_done")
        block = s.enter_context(nc.Block())

        def group(arr, q, u):
            return arr[:, ds((q * 2 + u) * GT, GT), :]

        def tile(arr, q, u, t):
            return arr[:, ds((q * 2 + u) * GT + t, 1), :].rearrange("p t d -> p (t d)")

        def columns(q, u):
            return ds((q * 2 + u) * (GT * P), GT * P)

        def rows_of(dram, q, u):
            return dram[columns(q, u), :].rearrange("(t p) d -> p t d", p=P)

        @block.sync
        def _(sp):
            sp.dma_start(ident[:], consts[:, C_IDENT:C_IDENT + P]).then_inc(const_in, 16)
            sp.dma_start(gate[:], gate_w).then_inc(const_in, 16)

            def load(q, u):
                sp.wait_ge(stat_done, q * 2 + (u + 1))
                sp.dma_start(group(x_all, q, u), rows_of(x_in, q, u)).then_inc(x_in_s[u], 16)

            def store(q, u):
                sp.wait_ge(h_done, q * 2 + (u + 3))
                sp.dma_start(rows_of(h_rows, q, u), h[:, u]).then_inc(h_out[u], 16)

            pipelined(sp, G, [(0, load), (1, store)])
            for u in range(2):
                sp.wait_ge(h_out[u], 16 * (G // 2) + 16)

        @block.gpsimd
        def _(pool):
            pool.memset(neg_half[:], -0.5).then_inc(half_done, 1)
            pool.wait_ge(half_done, 1)

            def root(q, u):
                g = q * 2 + u
                wait_apart(pool, stat_done, g + 3)
                wait_apart(pool, h_done, g + 1)
                pool.tensor_scalar(var_eps[:, u], mv[:, u, :, 1], EPS, None, ALU.add).then_inc(pool_own, 1)
                pool.wait_ge(pool_own, g + 1)
                pool.tensor_tensor(rstd[:, u], var_eps[:, u], neg_half[:], ALU.pow).then_inc(rstd_done, 1)

            def weights_low_part(q, u):
                wait_apart(pool, w_hi_done, 1)
                at = ds((q * 2 + u) * PIECE, PIECE)
                pool.tensor_tensor(w_lo[:].rearrange("p f w -> p (f w)")[:, at], raw[:, at],
                                   as_f32(w_hi[:].rearrange("p f w -> p (f w)")[:, at]), ALU.subtract
                                   ).then_inc(w_lo_done, 1)

            pipelined(pool, G, [(0, root), (3, weights_low_part)])
            pool.wait_ge(w_lo_done, G)

        @block.tensor
        def _(pe):
            pe.wait_ge(const_in, 32)

            def turn(q, u):
                g = q * 2 + u
                pe.wait_ge(h_done, g + 3)
                pe.wait_ge(hi_done, g + 1)
                for k in range(K):
                    for t in range(GT):
                        ins = pe.transpose(turned[u][:, k, t * P:(t + 1) * P], h[:, u, t, k * P:(k + 1) * P], ident[:])
                ins.then_inc(turn_done, 1)

            def score(q, u):
                g = q * 2 + u
                pe.wait_ge(ht_done, g + 1)
                pe.wait_ge(logit_done, g + 1)
                for t in range(GT):
                    for k in range(K):
                        ins = pe.matmul(scored[u][:, t, :], ht[:, u, k, t * P:(t + 1) * P], gate[:, k, :],
                                        start=(k == 0), stop=(k == K - 1))
                ins.then_inc(score_done, 1)

            pipelined(pe, G, [(1, turn), (2, score)])

        @block.scalar
        def _(act):
            act.dma_start(raw[:].rearrange("p (f w) -> p f w", f=w_hi.shape[1]),
                          w_dram.rearrange("f p w -> p f w")).then_inc(w_in, 16)
            act.wait_ge(w_in, 16)
            act.copy(w_hi[:].rearrange("p f w -> p (f w)"), raw[:]).then_inc(w_hi_done, 1)

            def copy_turned(q, u):
                g = q * 2 + u
                act.wait_ge(turn_done, g + 3)
                act.wait_ge(score_done, g + 1)
                act.wait_ge(lo_done, g + 1)
                for k in range(K):
                    ins = act.copy(ht[:, u, k, :], turned[u][:, k, :])
                ins.then_inc(ht_done, 1)
                for k in range(K):
                    ins = act.copy(ht_hi[:, k, columns(q, u)], turned[u][:, k, :])
                ins.then_inc(hi_done, 1)

            pipelined(act, G, [(1, copy_turned)])

        @block.vector
        def _(dve):
            for sem in (h_done, hi_done, lo_done, turn_done, logit_done, score_done, stat_done):
                dve.sem_inc(sem, 2)
            for u in range(2):
                dve.sem_inc(h_out[u], 16)

            def stat(q, u):
                g = q * 2 + u
                dve.wait_ge(x_in_s[u], q * 16 + 16)
                for t in range(GT):
                    ins = dve.bn_stats(stats[:, u, t], tile(x_all, q, u, t))
                ins.then_inc(dve_own, 1)
                wait_apart(dve, dve_own, g + 1)
                for t in range(GT):
                    ins = dve.bn_aggr(mv[:, u, t], stats[:, u, t])
                ins.then_inc(stat_done, 1)

            def norm(q, u):
                g = q * 2 + u
                dve.wait_ge(rstd_done, g + 1)
                dve.wait_ge(stat_done, g + 3)
                dve.wait_ge(h_out[u], q * 16 + 16)
                dve.wait_ge(turn_done, g + 1)
                for t in range(GT):
                    ins = dve.tensor_scalar(h[:, u, t], tile(x_all, q, u, t), mv[:, u, t, 0:1], rstd[:, u, t:t + 1],
                                            ALU.subtract, ALU.mult)
                ins.then_inc(h_done, 1)

            def keep_logits(q, u):
                dve.wait_ge(score_done, q * 2 + (u + 3))
                dve.tensor_copy(logits[:, :, ds((q * 2 + u) * GT, GT)], scored[u][:].rearrange("p t e -> p e t")
                                ).then_inc(logit_done, 1)

            def low_part(q, u):
                g = q * 2 + u
                dve.wait_ge(ht_done, g + 1)
                dve.wait_ge(hi_done, g + 3)
                for k in range(K):
                    ins = dve.tensor_tensor(ht_lo[:, k, columns(q, u)], ht[:, u, k, :],
                                             as_f32(ht_hi[:, k, columns(q, u)]), ALU.subtract)
                ins.then_inc(lo_done, 1)

            pipelined(dve, G, [(1, norm), (0, stat), (2, low_part), (3, keep_logits)])
            dve.wait_ge(logit_done, G + 2)
            dve.wait_ge(lo_done, G + 2)


def shared_and_search(nc, tag, w_hi, w_lo, x_all, ht_hi, ht_lo, logits, low, high, acc_out):
    E = FFN_E
    F_T = SHARED_F // P
    with Scope(nc, tag) as s:
        ones = s.sb("ones", [P, P], BF16)
        at_least = s.sb("at_least", [P, E, T], BF16)
        twice = s.sb("twice", [P, E, T])
        part = s.sb("part", [P, E])
        part_b = s.sb("part_b", [P, E], BF16)
        ends = s.sb("ends", [P, 2, E])
        ends_all = s.sb("ends_all", [P, 2, E])
        size = s.sb("size", [P, E])
        both = s.sb("both", [P, E])
        mid = s.sb("mid", [P, E])
        enough, short = s.sb("enough", [P, E], I32), s.sb("short", [P, E], I32)
        silu = s.sb("silu", [P, 2, 512])
        act_f = s.sb("act_f", [P, 2, 512])
        act_hi, act_lo = s.sb("act_hi", [P, 2, 512], F32R), s.sb("act_lo", [P, 2, 512], F32R)
        out = s.sb("out", [P, 2, GT, D])
        ps_gate = [s.ps(f"gate{b}") for b in range(2)]
        ps_up = [s.ps(f"up{b}") for b in range(2)]
        ps_down = s.ps("down", (P, GT, D))
        ps_count = s.ps("count", (P, E))
        ones_done, ends_done, ends_all_done = s.sem("ones_done"), s.sem("ends_done"), s.sem("ends_all_done")
        gu_done, silu_done, act_done, down_done = (s.sem(n) for n in ("gu_done", "silu_done", "act_done", "down_done"))
        part_done, count_done, out_done = s.sem("part_done"), s.sem("count_done"), s.sem("out_done")
        act_hi_done = s.sem("act_hi_done")
        out_stored = [s.sem(f"out_stored{b}") for b in range(2)]
        dve_own = s.sem("dve_own")
        block = s.enter_context(nc.Block())

        def groups(eng, one):
            with eng.Fori(0, G // 2 - 1) as i:
                one(i * 2, 0, False)
                one(i * 2 + 1, 1, False)
            one(G - 2, 0, False)
            one(G - 1, 1, True)

        @block.sync
        def _(sp):
            with sp.Fori(0, G // 2) as i:
                for b in range(2):
                    g = i * 2 + b
                    sp.wait_ge(out_done, g + 2)
                    sp.dma_start(acc_out[ds(g * (GT * P), GT * P), :].rearrange("(t p) d -> p t d", p=P),
                                 out[:, b]).then_inc(out_stored[b], 16)
            for b in range(2):
                sp.wait_ge(out_stored[b], 16 * (G // 2) + 16)

        @block.gpsimd
        def _(pool):
            pool.wait_ge(ends_done, 1)
            pool.partition_all_reduce(ends_all[:].rearrange("p a e -> p (a e)"),
                                      ends[:].rearrange("p a e -> p (a e)"), P,
                                      bass.bass_isa.ReduceOp.max).then_inc(ends_all_done, 1)

            def low_part(n, f):
                pool.wait_ge(act_hi_done, n + 1)
                pool.tensor_tensor(act_lo[:, f % 2], act_f[:, f % 2], as_f32(act_hi[:, f % 2]),
                                   ALU.subtract).then_inc(act_done, 1)

            with pool.Fori(0, G) as g:
                for f in range(F_T):
                    low_part(g * F_T + f, f)

        @block.tensor
        def _(pe):
            pe.wait_ge(ones_done, 1)

            def down(g, n, f):
                pe.wait_ge(act_done, n + 3)
                if f == 0:
                    pe.wait_ge(out_done, g + 1)
                for t in range(GT):
                    last = product(pe, ps_down[:, t, :],
                                   [a[:, f % 2, t * P:(t + 1) * P] for a in (act_hi, act_lo)],
                                   [w[:, f, 2 * K * P:] for w in (w_hi, w_lo)],
                                   f == 0 and t % 2 == 0, f == F_T - 1)
                last.then_inc(down_done, 1)

            def into(g, f):
                pe.wait_ge(act_done, g * F_T + (f + 1))
                for j, ps in enumerate((ps_gate, ps_up)):
                    for k in range(K):
                        w0 = (j * K + k) * P
                        last = product(pe, ps[f % 2][:], [w[:, f, w0:w0 + P] for w in (w_hi, w_lo)],
                                       [h[:, k, ds(g * (GT * P), GT * P)] for h in (ht_hi, ht_lo)],
                                       k == 0, k == K - 1)
                last.then_inc(gu_done, 1)

            def count(n):
                pe.wait_ge(part_done, n + 1)
                pe.matmul(ps_count[:], ones[:], part_b[:], start=True, stop=True).then_inc(count_done, 1)

            into(0, 0)
            count(0)

            def one(g, b, last):
                for f in range(1, F_T):
                    into(g, f)
                    down(g, g * F_T + (f - 1), f - 1)
                    count(g * F_T + f)
                if not last:
                    into(g + 1, 0)
                down(g, g * F_T + (F_T - 1), F_T - 1)
                if not last:
                    count((g + 1) * F_T)

            groups(pe, one)

        @block.scalar
        def _(act):
            with act.Fori(0, G // 2) as i:
                for b in range(2):
                    for f in range(F_T):
                        n = (i * 2 + b) * F_T + f
                        act.wait_ge(gu_done, n + 1)
                        act.wait_ge(act_done, n + 1)
                        act.activation(silu[:, f % 2], ps_gate[f % 2][:], ACT.Silu).then_inc(silu_done, 1)

        @block.vector
        def _(dve):
            own = Chain(dve, dve_own)
            dve.sem_inc(act_done, 2)
            dve.sem_inc(down_done, 2)
            dve.sem_inc(out_done, 1)
            for b in range(2):
                dve.sem_inc(out_stored[b], 16)
            dve.memset(ones[:], 1.0).then_inc(ones_done, 1)
            own.step(dve.tensor_scalar(twice[:], logits[:], 2.0, None, ALU.mult))
            own.step(dve.tensor_reduce(ends[:, 0], logits[:], AX.X, ALU.max))
            own.step(dve.tensor_reduce(ends[:, 1], logits[:], AX.X, ALU.min))
            dve.tensor_scalar(ends[:, 1], ends[:, 1], -1.0, None, ALU.mult).then_inc(ends_done, 1)
            dve.wait_ge(ends_all_done, 1)
            own.step(dve.tensor_scalar(low[:], ends_all[:, 1], -1.0, None, ALU.mult))
            own.step(dve.scalar_tensor_tensor(size[:], ends_all[:, 0], -1.0, ends_all[:, 0], ALU.mult, ALU.max))
            own.step(dve.tensor_scalar(size[:], size[:], 2.0 ** -10, 1e-30, ALU.mult, ALU.add))
            own.step(dve.tensor_tensor(high[:], ends_all[:, 0], size[:], ALU.add))
            first = own.n

            def compare():
                own.step(dve.tensor_tensor(both[:], low[:], high[:], ALU.add))
                own.step(dve.tensor_tensor(at_least[:], twice[:], both[:].unsqueeze(2).to_broadcast([P, E, T]),
                                           ALU.is_ge))
                dve.tensor_scalar(mid[:], both[:], 0.5, None, ALU.mult)
                own.step(dve.tensor_reduce(part[:], at_least[:], AX.X, ALU.add))
                dve.tensor_copy(part_b[:], part[:]).then_inc(part_done, 1)

            def halve(n):
                wait_apart(dve, count_done, n + 1)
                dve.tensor_scalar(enough[:], ps_count[:], float(FFN_CAP) - 0.5, None, ALU.is_ge)
                own.step(dve.tensor_scalar(short[:], ps_count[:], float(FFN_CAP) - 0.5, None, ALU.is_lt), apart=True)
                dve.copy_predicated(low[:], enough[:], mid[:])
                own.step(dve.copy_predicated(high[:], short[:], mid[:]))

            def activate(g, f):
                n = g * F_T + f
                dve.wait_ge(silu_done, n + 1)
                dve.wait_ge(act_done, n + 1)
                own.step(dve.tensor_tensor(act_f[:, f % 2], ps_up[f % 2][:], silu[:, f % 2], ALU.mult))
                dve.wait_ge(down_done, n + 1)
                dve.tensor_copy(act_hi[:, f % 2], act_f[:, f % 2]).then_inc(act_hi_done, 1)

            compare()
            activate(0, 0)
            halve(0)
            compare()
            first = own.n
            STEP = 1 + 2 + 3

            def one(g, b, last):
                own.at(g * (F_T * STEP) + first)
                for f in range(1, F_T):
                    activate(g, f)
                    halve(g * F_T + f)
                    if not (last and f == F_T - 1):
                        compare()
                if not last:
                    activate(g + 1, 0)
                dve.wait_ge(down_done, g * F_T + (F_T + 2))
                dve.wait_ge(out_stored[b], (g - b) * 8 + 16)
                for t in range(0, GT, 2):
                    ins = dve.scalar_tensor_tensor(out[:, b, t:t + 2], ps_down[:, t:t + 2, :], 0.5,
                                                   x_all[:, ds(g * GT + t, 2), :], ALU.mult, ALU.add)
                ins.then_inc(out_done, 1)
                if not last:
                    halve((g + 1) * F_T)
                    compare()

            groups(dve, one)


def make_lists(nc, tag, E, NT, consts, logits, bracket, largest, gather_ids, scatter_ids, gate_cols):
    HB = 8
    NB = T // HB
    HOTS = 8
    expert_chooses = bracket is not None
    if expert_chooses:
        low, high = bracket
    else:
        best, best_i = largest
    with Scope(nc, tag) as s:
        cst = s.sb("cst", [P, C_ALL])
        tri, ones = (s.sb(n, [P, P], BF16) for n in ("tri", "ones"))
        lanes = s.sb("lanes", [P, P, HB], BF16)
        reset, sel, tie, gate, summed, pos, row, tie_pos, part = (
            s.sb(n, [P, E, T]) for n in ("reset", "sel", "tie", "gate", "summed", "pos", "row", "tie_pos", "part"))
        sel_b, lane_b = s.sb("sel_b", [P, 2, E, T], BF16), s.sb("lane_b", [P, E, T], BF16)
        pos_i, part_i = s.sb("pos_i", [P, E, T], I32), s.sb("part_i", [P, E, T], I32)
        row_hot = s.sb("row_hot", [P, E, T, NT], BF16)
        vals = s.sb("vals", [P, E, T, IDC], BF16)
        moved = s.sb("moved", [P, E, T, NT * IDC], BF16)
        hot = s.sb("hot", [P, HOTS, P, HB], BF16)
        counts = s.sb("counts", [P, E])
        slots = s.sb("slots", [P, E, NT, IDC])
        idf, tmp = s.sb("idf", [P, E, NT]), s.sb("tmp", [P, E, NT])
        if not expert_chooses:
            slot_no = s.sb("slot_no", [P, E, NT])
            best_f = s.sb("best_f", [P, 2, T])
            ratio, share = s.sb("ratio", [P, T]), s.sb("share", [P, 2, T])
        ROUNDS = 2 if expert_chooses else 1
        ps_before = [s.ps(f"before{r}", (P, E, T)) for r in range(ROUNDS)]
        ps_total = [s.ps(f"total{r}", (P, E, T)) for r in range(ROUNDS)]
        PER_BANK = 512 // (NT * IDC)
        n_banks = -(-E // PER_BANK)
        ps_slots = [s.ps(f"slots{i}", (P, PER_BANK, NT * IDC)) for i in range(n_banks)]
        const_in, const_done = s.sem("const_in"), s.sem("const_done")
        sel_done, prefix_done, row_done = s.sem("sel_done"), s.sem("prefix_done"), s.sem("row_done")
        hot_done, hot_used = s.sem("hot_done"), s.sem("hot_used")
        pool_moved, dve_moved, row_hot_done = s.sem("pool_moved"), s.sem("dve_moved"), s.sem("row_hot_done")
        gate_asked, gate_ready, gate_made = s.sem("gate_asked"), s.sem("gate_ready"), s.sem("gate_made")
        vals_done, dve_own, pool_own = s.sem("vals_done"), s.sem("dve_own"), s.sem("pool_own")
        block = s.enter_context(nc.Block())
        by_expert = [P, E, T]

        def by_dve(e):
            return NT > 4 and e % 2 == 1

        def move(eng, e):
            return eng.tensor_tensor(moved[:, e].rearrange("p t (j c) -> p t j c", c=IDC),
                                     vals[:, e].unsqueeze(2).to_broadcast([P, T, NT, IDC]),
                                     row_hot[:, e].unsqueeze(3).to_broadcast([P, T, NT, IDC]), ALU.mult)

        @block.sync
        def _(sp):
            sp.dma_start(cst[:], consts).then_inc(const_in, 16)

        @block.scalar
        def _(act):
            if expert_chooses:
                act.activation(gate[:], logits[:], ACT.Sigmoid).then_inc(gate_ready, 1)
            else:
                act.wait_ge(gate_asked, 1)
                act.activation(ratio[:], ratio[:], ACT.Exp).then_inc(gate_ready, 1)

        @block.gpsimd
        def _(pool):
            own = Chain(pool, pool_own)
            pool.wait_ge(const_in, 16)
            own.step(pool.tensor_copy(vals[:, :, :, 0], cst[:, C_TILE:C_TILE + T].unsqueeze(1).to_broadcast(by_expert)))
            own.step(pool.tensor_copy(vals[:, :, :, 1], cst[:, C_ROW:C_ROW + 1].unsqueeze(2).to_broadcast(by_expert)))
            pool.wait_ge(gate_ready if expert_chooses else gate_made, 1)
            for c in range(2):
                own.step(pool.tensor_copy(vals[:, :, :, 2 + c], gate[:]))
                own.step(pool.tensor_tensor(gate[:], gate[:], vals[:, :, :, 2 + c], ALU.subtract))
            pool.tensor_copy(vals[:, :, :, 4], gate[:]).then_inc(vals_done, 1)
            pool.wait_ge(vals_done, 1)
            pool.wait_ge(row_hot_done, 1)
            for e in range(E):
                if not by_dve(e):
                    move(pool, e).then_inc(pool_moved, 1)

        @block.tensor
        def _(pe):
            pe.wait_ge(const_done, 1)
            for r in range(ROUNDS):
                flat = sel_b[:, r].rearrange("p e t -> p (e t)")
                pe.wait_ge(sel_done, r + 1)
                pe.matmul(ps_before[r][:].rearrange("p e t -> p (e t)"), tri[:], flat, start=True, stop=True)
                pe.matmul(ps_total[r][:].rearrange("p e t -> p (e t)"), ones[:], flat,
                          start=True, stop=True).then_inc(prefix_done, 1)
            for e in range(E):
                made = sum(by_dve(i) == by_dve(e) for i in range(e + 1))
                pe.wait_ge(dve_moved if by_dve(e) else pool_moved, made)
                for n in range(NB):
                    m = e * NB + n
                    pe.wait_ge(hot_done, m + 1)
                    for t in range(HB):
                        last = pe.matmul(ps_slots[e // PER_BANK][:, e % PER_BANK, :], hot[:, m % HOTS, :, t],
                                         moved[:, e, n * HB + t, :], start=(n == 0 and t == 0),
                                         stop=(n == NB - 1 and t == HB - 1))
                    last.then_inc(hot_used, 1)

        @block.vector
        def _(dve):
            own = Chain(dve, dve_own)
            dve.wait_ge(const_in, 16)
            dve.tensor_copy(tri[:], cst[:, C_TRI:C_TRI + P])
            dve.memset(ones[:], 1.0)
            dve.tensor_copy(lanes[:], cst[:, C_IOTA:C_IOTA + P].unsqueeze(2).to_broadcast([P, P, HB]))
            dve.tensor_copy(reset[:], cst[:, C_RESET:C_RESET + T].unsqueeze(1).to_broadcast(by_expert)
                            ).then_inc(const_done, 1)
            dve.wait_ge(const_done, 1)

            def ask(r, chosen):
                dve.tensor_copy(sel_b[:, r], chosen[:]).then_inc(sel_done, 1)

            def prefix(r, before):
                dve.wait_ge(prefix_done, r + 1)
                own.step(dve.tensor_copy(part[:], ps_total[r][:]))
                own.step(dve.tensor_tensor_scan(summed[:].rearrange("p e t -> p (e t)"),
                                                reset[:].rearrange("p e t -> p (e t)"),
                                                part[:].rearrange("p e t -> p (e t)"), 0.0, ALU.mult, ALU.add))
                own.step(dve.tensor_tensor(before[:], summed[:], part[:], ALU.subtract))
                own.step(dve.tensor_tensor(before[:], ps_before[r][:], before[:], ALU.add))

            if expert_chooses:
                own.step(dve.tensor_tensor(sel[:], logits[:], high[:].unsqueeze(2).to_broadcast(by_expert), ALU.is_ge))
                ask(0, sel)
                own.step(dve.tensor_tensor(tie[:], logits[:], low[:].unsqueeze(2).to_broadcast(by_expert), ALU.is_ge))
                own.step(dve.tensor_tensor(tie[:], tie[:], sel[:], ALU.subtract))
                ask(1, tie)
                prefix(0, pos)
                own.step(dve.tensor_scalar(counts[:], summed[:, :, T - 1], -1.0, float(FFN_CAP), ALU.mult, ALU.add))
                prefix(1, tie_pos)
                left = counts[:].unsqueeze(2).to_broadcast(by_expert)
                own.step(dve.tensor_tensor(part[:], tie_pos[:], left, ALU.is_lt))
                own.step(dve.tensor_tensor(tie[:], tie[:], part[:], ALU.mult))
                own.step(dve.tensor_tensor(sel[:], sel[:], tie[:], ALU.add))
                own.step(dve.tensor_tensor(part[:], tie_pos[:], left, ALU.min))
                own.step(dve.tensor_tensor(pos[:], pos[:], part[:], ALU.add))
            else:
                dve.tensor_tensor(ratio[:], best[:, :, 1], best[:, :, 0], ALU.subtract).then_inc(gate_asked, 1)
                own.step(dve.tensor_copy(best_f[:], best_i[:, :, 0:2].rearrange("p t c -> p c t")))
                expert_no = cst[:, C_SLOTHI:C_SLOTHI + E].unsqueeze(2).to_broadcast(by_expert)
                for c, hot_c in enumerate((gate, tie)):
                    own.step(dve.tensor_tensor(hot_c[:], expert_no,
                                               best_f[:, c, :].unsqueeze(1).to_broadcast(by_expert), ALU.is_equal))
                own.step(dve.tensor_tensor(sel[:], gate[:], tie[:], ALU.add))
                ask(0, sel)
                dve.wait_ge(gate_ready, 1)
                own.step(dve.tensor_scalar(share[:, 1], ratio[:], 1.0, None, ALU.add))
                own.step(dve.reciprocal(share[:, 0], share[:, 1]))
                own.step(dve.tensor_tensor(share[:, 1], share[:, 0], ratio[:], ALU.mult))
                for c, hot_c in enumerate((gate, tie)):
                    own.step(dve.tensor_tensor(hot_c[:], hot_c[:],
                                               share[:, c, :].unsqueeze(1).to_broadcast(by_expert), ALU.mult))
                dve.tensor_tensor(gate[:], gate[:], tie[:], ALU.add).then_inc(gate_made, 1)
                prefix(0, pos)
                own.step(dve.scalar_tensor_tensor(sel[:], pos[:], float(MOE_CAP) - 0.5, sel[:], ALU.is_lt, ALU.mult))
                own.step(dve.tensor_scalar(counts[:], summed[:, :, T - 1], float(MOE_CAP), None, ALU.min))
            own.step(dve.scalar_tensor_tensor(pos[:], pos[:], 1.0, sel[:], ALU.add, ALU.mult))
            own.step(dve.tensor_scalar(pos_i[:], pos[:], -1.0, None, ALU.add))
            own.step(dve.tensor_scalar(part_i[:], pos_i[:], P.bit_length() - 1, None, ALU.arith_shift_right))
            dve.tensor_copy(row[:], part_i[:]).then_inc(row_done, 1)
            dve.wait_ge(row_done, 1)
            for j in range(NT):
                ins = dve.tensor_scalar(row_hot[:, :, :, j], row[:], float(j), None, ALU.is_equal)
            ins.then_inc(row_hot_done, 1)
            own.step(dve.tensor_scalar(part_i[:], pos_i[:], P - 1, None, ALU.bitwise_and))
            own.step(dve.tensor_copy(lane_b[:], part_i[:]))
            for e in range(E):
                for n in range(NB):
                    m = e * NB + n
                    if m >= HOTS:
                        dve.wait_ge(hot_used, m - HOTS + 1)
                    dve.tensor_tensor(hot[:, m % HOTS], lanes[:],
                                      lane_b[:, e, n * HB:(n + 1) * HB].unsqueeze(1).to_broadcast([P, P, HB]),
                                      ALU.is_equal).then_inc(hot_done, 1)
                if e + 1 < E and by_dve(e + 1):
                    dve.wait_ge(vals_done, 1)
                    dve.wait_ge(row_hot_done, 1)
                    move(dve, e + 1).then_inc(dve_moved, 1)
            dve.wait_ge(hot_used, E * NB)
            for i in range(n_banks):
                e0, e1 = i * PER_BANK, min(E, (i + 1) * PER_BANK)
                last = dve.tensor_copy(slots[:, e0:e1].rearrange("p e j c -> p e (j c)"), ps_slots[i][:, 0:e1 - e0])
            own.step(last)
            own.step(dve.scalar_tensor_tensor(idf[:], slots[:, :, :, 0], float(P), slots[:, :, :, 1], ALU.mult,
                                              ALU.add))
            own.step(dve.tensor_copy(gather_ids[:], idf[:]))
            own.step(dve.tensor_tensor(tmp[:], slots[:, :, :, 2], slots[:, :, :, 3], ALU.add))
            own.step(dve.tensor_tensor(gate_cols[:], tmp[:], slots[:, :, :, 4], ALU.add))
            if expert_chooses:
                own.step(dve.tensor_scalar(gate_cols[:], gate_cols[:], 0.5, None, ALU.mult))
            else:
                slot_tiles = cst[:, C_SLOTHI:C_SLOTHI + NT].unsqueeze(1).to_broadcast([P, E, NT])
                own.step(dve.tensor_scalar(slot_no[:], slot_tiles, float(P), cst[:, C_ROW:C_ROW + 1], ALU.mult,
                                           ALU.add))
                own.step(dve.tensor_tensor(tmp[:], slot_no[:], counts[:].unsqueeze(2).to_broadcast([P, E, NT]),
                                           ALU.is_ge))
                own.step(dve.scalar_tensor_tensor(tmp[:], slot_no[:], float(N), tmp[:], ALU.add, ALU.mult))
                own.step(dve.tensor_tensor(idf[:], idf[:], tmp[:], ALU.add))
            own.step(dve.tensor_copy(scatter_ids[:], idf[:]))


def run_experts(nc, tag, E, NT, gated, w_dram, bias_dram, down_bias, consts, h_rows, acc,
                gather_ids, scatter_ids, gate_cols):
    F_T = FFN_F // P
    CH = [(c, min(c + 4, NT)) for c in range(0, NT, 4)]
    S = F_T * len(CH)
    IN = (2 if gated else 1)
    W = IN * K * P + D
    NI = NT // 2
    NMISC = 2 if gated else 1
    ITEM_AT = {4: 0, 6: 1} if gated else {13: 0, 15: 1, 17: 2, 19: 3, 21: 4}
    AHEAD = 3
    LOW_AHEAD = 5
    assert len(ITEM_AT) == NI and S % 2 == 0 and F_T % W_RING == 0 and NI % NMISC == 0
    with Scope(nc, tag) as s:
        ident = s.sb("ident", [P, P])
        raw = s.sb("raw", [P, W_RING, W])
        w_hi, w_lo = s.sb("w_hi", [P, W_RING, W], F32R), s.sb("w_lo", [P, W_RING, W], F32R)
        bias = s.sb("bias", [P, 2, IN * F_T])
        db = s.sb("db", [P, 2, D])
        rows = s.sb("rows", [P, NT, D])
        xt_hi = s.sb("xt_hi", [P, 2, K, NT * P], F32R)
        xt_lo = s.sb("xt_lo", [P, 2, K, NT * P], F32R)
        silu = s.sb("silu", [P, 2, 512])
        act_f = s.sb("act_f", [P, 2, 512])
        act_hi, act_lo = s.sb("act_hi", [P, 2, 512], F32R), s.sb("act_lo", [P, 2, 512], F32R)
        out = s.sb("out", [P, 2, NT, D])
        gcol = s.sb("gcol", [P, 2, NT])
        gid, sid = s.sb("gid", [P, NT], U32), s.sb("sid", [P, NT], U32)
        ps_in = [[s.ps(f"in{j}{b}") for j in range(IN)] for b in range(2)]
        ps_down = s.ps("down", (P, NT, D))
        ps_turn = [s.ps(f"turn{m}", (P, K, 2 * P)) for m in range(NMISC)]
        const_in = s.sem("const_in")
        raw_in = [s.sem(f"raw_in{r}") for r in range(W_RING)]
        bias_in = [s.sem(f"bias_in{b}") for b in range(2)]
        raw_hi, raw_lo = s.sem("raw_hi"), s.sem("raw_lo")
        rows_in, turned, xt_done = s.sem("rows_in"), s.sem("turned"), s.sem("xt_done")
        in_done, silu_done, act_done, down_done = (s.sem(n) for n in ("in_done", "silu_done", "act_done", "down_done"))
        read_out, out_done, scattered = s.sem("read_out"), s.sem("out_done"), s.sem("scattered")
        landed, gates_set = s.sem("landed"), s.sem("gates_set")
        dve_own, pool_own = s.sem("dve_own"), s.sem("pool_own")
        block = s.enter_context(nc.Block())
        ACT0, DOWN0, RAW0, XT0, READ0, OUT0 = 2, 4 * len(CH), W_RING, NMISC, len(CH), 2

        def experts(eng, one):
            with eng.Fori(0, E // 2 - 1) as i:
                one(i * 2, 0, 2)
                one(i * 2 + 1, 1, 2)
            one(E - 2, 0, 1)
            one(E - 1, 1, 0)

        @block.sync
        def _(sp):
            sp.dma_start(ident[:], consts[:, C_IDENT:C_IDENT + P]).then_inc(const_in, 16)

            def one(e, b, left):
                sp.wait_ge(out_done, e + 1)
                sp.dma_start(bias[:, b], bias_dram[ds(e, 1)].rearrange("e p c -> (e p) c")).then_inc(bias_in[b], 16)
                sp.dma_start(db[:, b], down_bias[ds(e, 1)].to_broadcast([P, D])).then_inc(bias_in[b], 16)
                for f in range(F_T):
                    sp.wait_ge(raw_hi, e * F_T + (f + 1))
                    sp.wait_ge(raw_lo, e * F_T + (f + 1))
                    sp.dma_start(raw[:, f % W_RING], w_dram[ds(e * F_T + f, 1)].rearrange("s p w -> (s p) w")
                                 ).then_inc(raw_in[f % W_RING], 16)

            experts(sp, one)

        @block.gpsimd
        def _(pool):
            own = Chain(pool, pool_own)
            PER = 2

            def gather(e):
                own.step(pool.tensor_copy(gid[:], gather_ids[:, ds(e, 1), :].rearrange("p e j -> p (e j)")), apart=True)
                for j in range(NT):
                    pool.indirect_dma_start(out=rows[:, j, :], out_offset=None, in_=h_rows,
                                            in_offset=bass.IndirectOffsetOnAxis(ap=gid[:, j:j + 1], axis=0)
                                            ).then_inc(rows_in, 16)

            def gather_after(e):
                pool.wait_ge(turned, e * NI + NI)
                wait_apart(pool, rows_in, e * (16 * NT) + 16 * NT)
                gather(e + 1)

            def low_part(e, f):
                n = e * F_T + f
                pool.wait_ge(raw_hi, n + (RAW0 + 1))
                r = f % W_RING
                pool.tensor_tensor(w_lo[:, r], raw[:, r], as_f32(w_hi[:, r]), ALU.subtract).then_inc(raw_lo, 1)

            gather(0)
            for f in range(AHEAD):
                low_part(0, f)
            gather_after(0)
            for f in range(AHEAD, LOW_AHEAD):
                low_part(0, f)

            def one(e, b, left):
                own.at(e * PER + (2 if left else 1))
                for f in range(LOW_AHEAD, F_T):
                    low_part(e, f)
                for f in range(LOW_AHEAD if left else 0):
                    low_part(e + 1, f)
                    if f == 0 and left > 1:
                        gather_after(e + 1)
                own.step(pool.tensor_copy(sid[:], scatter_ids[:, ds(e, 1), :].rearrange("p e j -> p (e j)")))
                wait_apart(pool, out_done, e + (OUT0 + 1))
                for j in range(NT):
                    pool.indirect_dma_start(out=acc, out_offset=bass.IndirectOffsetOnAxis(ap=sid[:, j:j + 1], axis=0),
                                            in_=out[:, b, j, :], in_offset=None, compute_op=ALU.add
                                            ).then_inc(scattered, 16)
                pool.wait_ge(scattered, e * (16 * NT) + 16 * NT)
                pool.nop().then_inc(landed, 1)

            experts(pool, one)

        @block.tensor
        def _(pe):
            pe.wait_ge(const_in, 16)

            def turn(e, i):
                if i == 0:
                    pe.wait_ge(rows_in, e * (16 * NT) + 16 * NT)
                pe.wait_ge(xt_done, e * NI + (i + 1))
                for k in range(K):
                    for t in range(2):
                        last = pe.transpose(ps_turn[i % NMISC][:, k, t * P:(t + 1) * P],
                                            rows[:, 2 * i + t, k * P:(k + 1) * P], ident[:])
                last.then_inc(turned, 1)

            def down(e, st):
                f, (t0, t1) = st // len(CH), CH[st % len(CH)]
                pe.wait_ge(act_done, e * S + (st + 1 + ACT0))
                if f == 0:
                    pe.wait_ge(read_out, e * len(CH) + (st + 1))
                for t in range(t0, t1):
                    at = slice((t - t0) * P, (t - t0 + 1) * P)
                    last = product(pe, ps_down[:, t, :], [a[:, st % 2, at] for a in (act_hi, act_lo)],
                                   [w[:, f % W_RING, IN * K * P:] for w in (w_hi, w_lo)],
                                   f == 0 and t % 2 == 0, f == F_T - 1)
                last.then_inc(down_done, 1)

            def into(e, st, b):
                f, (t0, t1) = st // len(CH), CH[st % len(CH)]
                if st == 0:
                    pe.wait_ge(xt_done, e * NI + (NI + XT0))
                if st % len(CH) == 0:
                    pe.wait_ge(raw_lo, e * F_T + (f + 1 + RAW0))
                pe.wait_ge(act_done, e * S + (st + 1))
                for j in range(IN):
                    for k in range(K):
                        w0 = (j * K + k) * P
                        last = product(pe, ps_in[st % 2][j][:, 0:(t1 - t0) * P],
                                       [w[:, f % W_RING, w0:w0 + P] for w in (w_hi, w_lo)],
                                       [x[:, b, k, t0 * P:t1 * P] for x in (xt_hi, xt_lo)],
                                       k == 0, k == K - 1)
                last.then_inc(in_done, 1)

            for i in range(NI):
                turn(0, i)
            into(0, 0, 0)

            def one(e, b, left):
                for st in range(1, S):
                    into(e, st, b)
                    if st in ITEM_AT and left:
                        turn(e + 1, ITEM_AT[st])
                    down(e, st - 1)
                if left:
                    into(e + 1, 0, 1 - b)
                down(e, S - 1)

            experts(pe, one)

        @block.scalar
        def _(act):
            def high_part(e, f):
                n = e * F_T + f
                act.wait_ge(raw_in[f % W_RING], (e * (F_T // W_RING) + (f // W_RING + 1)) * 16)
                act.wait_ge(down_done, (n + 1) * len(CH))
                act.copy(w_hi[:, f % W_RING], raw[:, f % W_RING]).then_inc(raw_hi, 1)

            def hidden(e, st, b):
                f, (t0, t1) = st // len(CH), CH[st % len(CH)]
                n = (t1 - t0) * P
                if st == 0:
                    act.wait_ge(bias_in[b], (e - b) * 16 + 32)
                act.wait_ge(in_done, e * S + (st + 1))
                act.wait_ge(act_done, e * S + (st + 1))
                dst, func = (silu, ACT.Silu) if gated else (act_f, ACT.Gelu)
                act.activation(dst[:, st % 2, 0:n], ps_in[st % 2][0][:, 0:n], func,
                               bias=bias[:, b, f:f + 1]).then_inc(silu_done, 1)

            def next_slice(e, st, left):
                if st % len(CH) == 0:
                    f = st // len(CH)
                    if f + AHEAD < F_T:
                        high_part(e, f + AHEAD)
                    elif left:
                        high_part(e + 1, f + AHEAD - F_T)

            def read_sums(e, st, b):
                t0, t1 = CH[st % len(CH)]
                if st == S - len(CH):
                    act.wait_ge(landed, e + 1)
                act.wait_ge(down_done, e * S + (st + 1 + DOWN0))
                act.wait_ge(gates_set, e + 1)
                for t in range(t0, t1):
                    ins = act.activation(out[:, b, t, :], ps_down[:, t, :], ACT.Copy, scale=gcol[:, b, t:t + 1])
                ins.then_inc(read_out, 1)

            for f in range(AHEAD):
                high_part(0, f)
            hidden(0, 0, 0)
            next_slice(0, 0, 1)

            def one(e, b, left):
                for st in range(1, S):
                    hidden(e, st, b)
                    if st > S - len(CH):
                        read_sums(e, st - 1, b)
                    next_slice(e, st, left)
                if left:
                    hidden(e + 1, 0, 1 - b)
                read_sums(e, S - 1, b)
                if left:
                    next_slice(e + 1, 0, left - 1)

            experts(act, one)

        @block.vector
        def _(dve):
            own = Chain(dve, dve_own)
            dve.sem_inc(act_done, ACT0)
            dve.sem_inc(down_done, DOWN0)
            dve.sem_inc(raw_hi, RAW0)
            dve.sem_inc(raw_lo, RAW0)
            dve.sem_inc(xt_done, XT0)
            dve.sem_inc(read_out, READ0)
            dve.sem_inc(out_done, OUT0)
            dve.sem_inc(landed, 2)

            def split_rows(e, i, b):
                dve.wait_ge(turned, e * NI + (i + 1))
                at = slice(2 * i * P, (2 * i + 2) * P)
                own.step(dve.tensor_copy(xt_hi[:, b, :, at], ps_turn[i % NMISC][:]))
                dve.tensor_tensor(xt_lo[:, b, :, at], ps_turn[i % NMISC][:], as_f32(xt_hi[:, b, :, at]),
                                  ALU.subtract).then_inc(xt_done, 1)

            def activate(e, st, b):
                f, (t0, t1) = st // len(CH), CH[st % len(CH)]
                n = (t1 - t0) * P
                act_n, hi_n, lo_n = (a[:, st % 2, 0:n] for a in (act_f, act_hi, act_lo))
                if st == 0:
                    dve.wait_ge(bias_in[b], (e - b) * 16 + 32)
                dve.wait_ge(silu_done, e * S + (st + 1))
                dve.wait_ge(down_done, e * S + (st + DOWN0 - 1))
                if gated:
                    own.step(dve.scalar_tensor_tensor(act_n, ps_in[st % 2][1][:, 0:n],
                                                      bias[:, b, F_T + f:F_T + f + 1], silu[:, st % 2, 0:n],
                                                      ALU.add, ALU.mult))
                own.step(dve.tensor_copy(hi_n, act_n))
                dve.tensor_tensor(lo_n, act_n, as_f32(hi_n), ALU.subtract).then_inc(act_done, 1)

            for i in range(NI):
                split_rows(0, i, 0)
            activate(0, 0, 0)
            first = own.n
            PER = NI + S * (2 if gated else 1)

            def gates(e, b):
                dve.tensor_copy(gcol[:, b], gate_cols[:, ds(e, 1), :].rearrange("p e j -> p (e j)")
                                ).then_inc(gates_set, 1)

            def add_bias(e, st, b):
                c = st % len(CH)
                dve.wait_ge(gates_set, e + 1)
                dve.wait_ge(read_out, e * len(CH) + (c + 1 + READ0))
                for j in range(*CH[c]):
                    ins = dve.scalar_tensor_tensor(out[:, b, j, :], db[:, b], gcol[:, b, j:j + 1], out[:, b, j, :],
                                                   ALU.mult, ALU.add)
                if st == S - 1:
                    ins.then_inc(out_done, 1)

            def one(e, b, left):
                own.at(e * PER + first)
                gates(e, b)
                for st in range(1, S):
                    activate(e, st, b)
                    if st > S - len(CH):
                        add_bias(e, st - 1, b)
                    if st in ITEM_AT and left:
                        split_rows(e + 1, ITEM_AT[st], 1 - b)
                if left:
                    activate(e + 1, 0, 1 - b)
                add_bias(e, S - 1, b)

            experts(dve, one)


def ffn(nc, tag, x_in, acc, gate_w, shared_w, ffn_w, ffn_b, ffn_db, consts):
    NT = FFN_CAP // P
    h_rows = nc.dram_tensor(f"{tag}_h", (N, D), F32, kind="Internal").ap()
    with Scope(nc, tag) as s:
        logits = s.sb("logits", [P, FFN_E, T])
        low, high = s.sb("low", [P, FFN_E]), s.sb("high", [P, FFN_E])
        ids = s.sb("ids", [P, FFN_E, NT], U32)
        ids2 = s.sb("ids2", [P, FFN_E, NT], U32)
        gates = s.sb("gates", [P, FFN_E, NT])
        with Scope(nc, tag) as s2:
            x_all = s2.sb("x_all", [P, T, D])
            ht_hi, ht_lo = s2.sb("ht_hi", [P, K, N], F32R), s2.sb("ht_lo", [P, K, N], F32R)
            w_hi, w_lo = (s2.sb(n, [P, SHARED_F // P, 2 * K * P + D], F32R) for n in ("w_hi", "w_lo"))
            norm_and_score(nc, tag + "n", x_in, gate_w, consts, h_rows, x_all, ht_hi, ht_lo, logits, shared_w, w_hi,
                           w_lo)
            shared_and_search(nc, tag + "s", w_hi, w_lo, x_all, ht_hi, ht_lo, logits, low, high, acc)
        make_lists(nc, tag + "l", FFN_E, NT, consts, logits, (low, high), None, ids, ids2, gates)
        run_experts(nc, tag + "e", FFN_E, NT, True, ffn_w, ffn_b, ffn_db, consts, h_rows, acc, ids, ids2, gates)


def attention(nc, tag, x_in, acc, w, consts, x2_all, sums):
    Q = T // BATCH
    QK, VG = slice(0, 2 * D), slice(2 * D, 4 * D)
    HW = P + HALF
    with Scope(nc, tag) as s:
        ident, mask = s.sb("ident", [P, P]), s.sb("mask", [P, HW])
        w_hi, w_lo = s.sb("w_hi", [P, K, 4 * D], F32R), s.sb("w_lo", [P, K, 4 * D], F32R)
        wo, scale = s.sb("wo", [P, K, D]), s.sb("scale", [P, K])
        bias, bo, rope = s.sb("bias", [P, 4 * D]), s.sb("bo", [P, D]), s.sb("rope", [P, Q, 4, DK // 2])
        zeros = s.sb("zeros", [P, K * HW])
        x_all, v_all, tanh_all = (s.sb(n, [P, T, D]) for n in ("x_all", "v_all", "tanh_all"))
        w_raw = v_all[:, 0:4 * K, :].rearrange("p (k t) d -> p k (t d)", k=K)
        neg_half = s.sb("neg_half", [P, 1])
        stats, mv = s.sb("stats", [P, 2, 6]), s.sb("mv", [P, 2, 2])
        rs = s.sb("rs", [P, 2, 4])
        a = s.sb("a", [P, 2, D])
        at_hi, at_lo = s.sb("at_hi", [P, 2, K, P], F32R), s.sb("at_lo", [P, 2, K, P], F32R)
        qk, rot_a, rot_b, rot, er, pos_part, phi = (
            s.sb(n, [P, 2, 2 * D]) for n in ("qk", "rot_a", "rot_b", "rot", "er", "pos_part", "phi"))
        gp = s.sb("gp", [P, 2, D])
        v1 = s.sb("v1", [P, 2, 2, HW])
        qt = s.sb("qt", [P, 2, K, P])
        state = s.sb("state", [P, 2, 2, 2, HW])
        den, div, o = s.sb("den", [P, HEADS]), s.sb("div", [P, D]), s.sb("o", [P, 2, D])
        ot = s.sb("ot", [P, K, P])
        square = zeros[:, 0:D]
        ps_a, ps_qt = s.ps("ps_a", (P, K, P)), s.ps("ps_qt", (P, K, P))
        ps_qk, ps_vg = s.ps("ps_qk"), s.ps("ps_vg")
        ps_state = [s.ps(f"state{u}", (P, 2, HW)) for u in range(2)]
        ps_num, ps_o = s.ps("ps_num", (P, 2, HW)), s.ps("ps_o", (P, 2, D))
        const_in, w_hi_done, w_lo_done, set_up = (s.sem(n) for n in ("const_in", "w_hi_done", "w_lo_done", "set_up"))
        x_in_s = [s.sem(f"x_in{u}") for u in range(2)]
        stored = [s.sem(f"stored{u}") for u in range(2)]
        (stat_done, rs_done, a_done, xtb_done, a_turned, at_hi_done, at_done, proj_done, proj_read, gp_done, tanh_done,
         rot_a_done, rot_b_done, rot_done, er_done, phi_done, v1_done, q_turned, qt_done, s0_done, m0_done, s1_done,
         m1_done, num_done, o_done, o_turned, ot_done, wo_done, x2_done, sum_done, total_done) = (
            s.sem(n) for n in (
                "stat_done", "rs_done", "a_done", "xtb_done", "a_turned", "at_hi_done", "at_done", "proj_done",
                "proj_read", "gp_done", "tanh_done", "rot_a_done", "rot_b_done", "rot_done", "er_done", "phi_done",
                "v1_done", "q_turned", "qt_done", "s0_done", "m0_done", "s1_done", "m1_done", "num_done", "o_done",
                "o_turned", "ot_done", "wo_done", "x2_done", "sum_done", "total_done"))
        own_aggr, own_xt, own_qk, own_den, own_div, own_rs, own_var, own_sq, own_ratio = (
            s.sem(n) for n in ("own_aggr", "own_xt", "own_qk", "own_den", "own_div", "own_rs", "own_var", "own_sq",
                               "own_ratio"))
        own_inv = s.sem("own_inv")
        block = s.enter_context(nc.Block())
        N_CONST = 8

        def row(arr, q, u):
            return arr[:, ds(q + u * Q, 1), :].rearrange("p t d -> p (t d)")

        def rows_of(dram, q, u):
            return dram[ds(q * P + u * SEQ, P), :]

        @block.sync
        def _(sp):
            def load(q, u):
                sp.wait_ge(a_done, q * 2 + (u + 1))
                sp.dma_start(row(x_all, q, u), rows_of(x_in, q, u)).then_inc(x_in_s[u], 16)

            def store(q, u):
                sp.wait_ge(total_done, q * 2 + (u + 1))
                sp.dma_start(rows_of(acc, q, u), row(x_all, q, u)).then_inc(stored[u], 16)

            pipelined(sp, T, [(10, store), (0, load)])
            for u in range(2):
                sp.wait_ge(stored[u], 16 * Q)

        @block.gpsimd
        def _(pool):
            pool.memset(neg_half[:], -0.5).then_inc(own_rs, 1)
            pool.wait_ge(own_rs, 1)
            pool.wait_ge(const_in, 16 * N_CONST)

            def root(q, u):
                h = q * 2 + u
                wait_apart(pool, a_done, h + 1)
                wait_apart(pool, stat_done, h + 1)
                var = mv[:, u, 1:2]
                pool.tensor_scalar(rs[:, u, 0:1], var, EPS, None, ALU.add).then_inc(own_var, 1)
                pool.wait_ge(own_var, h + 1)
                pool.tensor_tensor(rs[:, u, 1:2], rs[:, u, 0:1], neg_half[:], ALU.pow).then_inc(own_inv, 1)
                pool.wait_ge(own_inv, h + 1)
                pool.tensor_tensor(rs[:, u, 2:3], rs[:, u, 1:2], rs[:, u, 1:2], ALU.mult).then_inc(own_sq, 1)
                pool.wait_ge(own_sq, h + 1)
                pool.tensor_tensor(rs[:, u, 2:3], rs[:, u, 2:3], var, ALU.mult).then_inc(own_ratio, 1)
                pool.wait_ge(own_ratio, h + 1)
                pool.tensor_tensor(rs[:, u, 3:4], rs[:, u, 2:3], neg_half[:], ALU.pow).then_inc(rs_done, 1)

            def add_bo(q, u):
                wait_apart(pool, a_done, q * 2 + (u + 3))
                pool.tensor_tensor(row(x2_all, q, u), row(x2_all, q, u), bo[:], ALU.add).then_inc(xtb_done, 1)

            def rotate(q, u):
                h = q * 2 + u
                pool.wait_ge(rot_done, h + 1)
                pool.wait_ge(er_done, h + 1)
                wait_apart(pool, rot_a_done, h + 1)
                src = qk[:, u].rearrange("p (h c j) -> p h c j", c=2, j=DK // 2)
                dst = rot_b[:, u].rearrange("p (h c j) -> p h c j", c=2, j=DK // 2)
                for c in range(2):
                    ins = pool.tensor_tensor(dst[:, :, c, :], src[:, :, 1 - c, :],
                                             rope[:, ds(q, 1), 2 + c, :].to_broadcast([P, 2 * HEADS, DK // 2]), ALU.mult)
                ins.then_inc(rot_b_done, 1)
                pool.wait_ge(rot_b_done, h + 1)
                pool.tensor_tensor(rot[:, u], rot_a[:, u], rot_b[:, u], ALU.add).then_inc(rot_done, 1)

            def residual(q, u):
                wait_apart(pool, x2_done, q * 2 + (u + 2))
                pool.tensor_tensor(row(x_all, q, u), row(x_all, q, u), row(x2_all, q, u), ALU.add
                                   ).then_inc(total_done, 1)

            pipelined(pool, T, [(10, residual), (4, rotate), (1, add_bo), (0, root)])

        @block.tensor
        def _(pe):
            pe.wait_ge(w_lo_done, K)
            pe.wait_ge(set_up, 1)
            for u in range(2):
                pe.matmul(ps_state[u][:].rearrange("p k c -> p (k c)"), zeros[:, 0:P], zeros[:], start=True, stop=False,
                          skip_group_check=True)

            def turn_a(q, u):
                h = q * 2 + u
                pe.wait_ge(a_done, h + 3)
                pe.wait_ge(at_done, h + 1)
                for k in range(K):
                    ins = pe.transpose(ps_a[:, k, :], a[:, u, k * P:(k + 1) * P], ident[:])
                ins.then_inc(a_turned, 1)

            def project(q, u):
                h = q * 2 + u
                pe.wait_ge(at_done, h + 2)
                pe.wait_ge(proj_read, h + 1)
                for ps, cols in ((ps_qk, QK), (ps_vg, VG)):
                    for k in range(K):
                        ins = product(pe, ps[:], [x[:, u, k, :] for x in (at_hi, at_lo)],
                                      [x[:, k, cols] for x in (w_hi, w_lo)], k == 0, k == K - 1)
                ins.then_inc(proj_done, 1)

            def add_chunk(c, u):
                at = slice(c * CHUNK, (c + 1) * CHUNK)
                for k in range(2):
                    ins = pe.matmul(ps_state[u][:, k, :], phi[at, u, D + k * P:D + (k + 1) * P], v1[at, u, k, :],
                                    start=False, stop=True, skip_group_check=True)
                return ins

            def chunk0(q, u):
                h = q * 2 + u
                pe.wait_ge(phi_done, h + 1)
                pe.wait_ge(v1_done, h + 3)
                pe.wait_ge(qt_done, h + 1)
                for k in range(K):
                    ins = pe.transpose(ps_qt[:, k, :], phi[:, u, k * P:(k + 1) * P], ident[:])
                ins.then_inc(q_turned, 1)
                pe.wait_ge(m1_done, h + 1)
                add_chunk(0, u).then_inc(s0_done, 1)

            def chunk1(q, u):
                pe.wait_ge(m0_done, q * 2 + (u + 1))
                add_chunk(1, u).then_inc(s1_done, 1)

            def numerators(q, u):
                h = q * 2 + u
                pe.wait_ge(m1_done, h + 3)
                pe.wait_ge(qt_done, h + 2)
                pe.wait_ge(o_done, h + 1)
                for c in range(2):
                    at = slice(c * CHUNK, (c + 1) * CHUNK)
                    for k in range(2):
                        ins = pe.matmul(ps_num[at, k, :], qt[:, u, k, at], state[:, u, c, k, :], start=(k == 0), stop=True,
                                        skip_group_check=True)
                ins.then_inc(num_done, 1)

            def turn_o(q, u):
                h = q * 2 + u
                pe.wait_ge(o_done, h + 2)
                pe.wait_ge(x2_done, h + 1)
                for k in range(K):
                    ins = pe.transpose(ps_o[:, 0, k * P:(k + 1) * P], o[:, u, k * P:(k + 1) * P], ident[:])
                ins.then_inc(o_turned, 1)

            def project_o(q, u):
                pe.wait_ge(ot_done, q * 2 + (u + 1))
                for k in range(K):
                    ins = pe.matmul(ps_o[:, 1, :], ot[:, k, :], wo[:, k, :], start=(k == 0), stop=(k == K - 1))
                ins.then_inc(wo_done, 1)

            pipelined(pe, T, [(6, chunk0), (2, turn_a), (7, chunk1), (8, numerators), (9, turn_o), (3, project),
                              (9, project_o)])

        @block.scalar
        def _(act):
            for dst, src in ((w_raw, w["qkvg"]), (ident[:], consts[:, C_IDENT:C_IDENT + P]),
                             (mask[:], consts[:, C_MASK:C_MASK + HW]), (wo[:], w["wo"]), (scale[:], w["norm1"]),
                             (bias[:], w["qkvg_b"].to_broadcast([P, 4 * D])), (bo[:], w["bo"].to_broadcast([P, D])),
                             (rope[:].rearrange("p q c j -> p q (c j)"), w["rope"])):
                act.dma_start(dst, src).then_inc(const_in, 16)
            act.wait_ge(const_in, 16 * N_CONST)
            for k in range(K):
                act.copy(w_hi[:, k], w_raw[:, k]).then_inc(w_hi_done, 1)

            def split_at(q, u):
                h = q * 2 + u
                act.wait_ge(a_turned, h + 1)
                act.wait_ge(proj_done, h + 1)
                for k in range(K):
                    ins = act.activation(at_hi[:, u, k, :], ps_a[:, k, :], ACT.Copy, scale=scale[:, k:k + 1])
                ins.then_inc(at_hi_done, 1)

            def half_tanh(q, u):
                act.wait_ge(gp_done, q * 2 + (u + 1))
                act.activation(row(tanh_all, q, u), gp[:, u], ACT.Tanh, scale=0.5).then_inc(tanh_done, 1)

            def exp_rot(q, u):
                h = q * 2 + u
                act.wait_ge(rot_done, h + 3)
                act.activation(er[:, u], rot[:, u], ACT.Exp)
                act.activation(pos_part[:, u], rot[:, u], ACT.Relu).then_inc(er_done, 1)

            def values(q, u):
                act.wait_ge(s1_done, q * 2 + (u + 1))
                act.copy(v1[:, u, :, 0:P], row(v_all, q, u).rearrange("p (k c) -> p k c", k=2)).then_inc(v1_done, 1)

            def copy_qt(q, u):
                h = q * 2 + u
                act.wait_ge(q_turned, h + 1)
                act.wait_ge(num_done, h + 1)
                act.copy(qt[:, u], ps_qt[:]).then_inc(qt_done, 1)

            def copy_ot(q, u):
                h = q * 2 + u
                act.wait_ge(o_turned, h + 1)
                act.wait_ge(wo_done, h + 1)
                act.copy(ot[:].rearrange("p k c -> p (k c)"), ps_o[:, 0, :]).then_inc(ot_done, 1)

            def sum_squares(q, u):
                act.wait_ge(x2_done, q * 2 + (u + 2))
                act.wait_ge(sum_done, q * 2 + (u + 1))
                act.activation(square, row(x2_all, q, u), ACT.Square,
                               accum_out=sums[:, ds(q + u * Q, 1)]).then_inc(sum_done, 1)

            pipelined(act, T, [(2, split_at), (5, exp_rot), (4, half_tanh), (6, copy_qt), (5, values), (9, copy_ot),
                               (10, sum_squares)])

        @block.vector
        def _(dve):
            for sem, free in ((a_done, 2), (at_done, 1), (proj_done, 2), (proj_read, 1), (rot_done, 2), (er_done, 2),
                              (s1_done, 2),
                              (v1_done, 2), (qt_done, 1), (m1_done, 2), (num_done, 2), (o_done, 1), (x2_done, 1),
                              (wo_done, 1), (sum_done, 1)):
                dve.sem_inc(sem, free)
            dve.memset(zeros[:], 0.0)
            dve.memset(v1[:], 1.0).then_inc(set_up, 1)
            dve.wait_ge(const_in, 16 * N_CONST)
            for k in range(K):
                dve.wait_ge(w_hi_done, k + 1)
                dve.tensor_tensor(w_lo[:, k], w_raw[:, k], as_f32(w_hi[:, k]), ALU.subtract).then_inc(w_lo_done, 1)

            def stat(q, u):
                h = q * 2 + u
                dve.wait_ge(x_in_s[u], q * 16 + 16)
                dve.bn_stats(stats[:, u], row(x_all, q, u)).then_inc(own_aggr, 1)
                wait_apart(dve, own_aggr, h + 1)
                dve.bn_aggr(mv[:, u], stats[:, u]).then_inc(stat_done, 1)

            def norm(q, u):
                h = q * 2 + u
                dve.wait_ge(rs_done, h + 1)
                dve.tensor_scalar(row(x2_all, q, u), row(x_all, q, u), mv[:, u, 0:1], rs[:, u, 1:2], ALU.subtract,
                                  ALU.mult).then_inc(own_xt, 1)
                dve.wait_ge(own_xt, h + 1)
                dve.tensor_scalar(a[:, u], row(x2_all, q, u), rs[:, u, 3:4], None, ALU.mult).then_inc(a_done, 1)

            def split_low(q, u):
                dve.wait_ge(at_hi_done, q * 2 + (u + 1))
                for k in range(K):
                    ins = dve.scalar_tensor_tensor(at_lo[:, u, k, :], ps_a[:, k, :], scale[:, k:k + 1],
                                                   as_f32(at_hi[:, u, k, :]), ALU.mult, ALU.subtract)
                ins.then_inc(at_done, 1)

            def add_bias(q, u):
                h = q * 2 + u
                dve.wait_ge(proj_done, h + 3)
                dve.tensor_tensor(gp[:, u], ps_vg[:, D:2 * D], bias[:, 3 * D:4 * D], ALU.add).then_inc(gp_done, 1)
                dve.wait_ge(rot_done, h + 1)
                dve.tensor_tensor(qk[:, u], ps_qk[:], bias[:, QK], ALU.add).then_inc(own_qk, 1)
                dve.tensor_tensor(row(v_all, q, u), ps_vg[:, 0:D], bias[:, 2 * D:3 * D], ALU.add).then_inc(proj_read, 1)
                dve.wait_ge(own_qk, h + 1)
                dve.tensor_tensor(rot_a[:, u].rearrange("p (h c) -> p h c", c=DK),
                                  qk[:, u].rearrange("p (h c) -> p h c", c=DK),
                                  rope[:, ds(q, 1), 0:2, :].rearrange("p q c j -> p q (c j)")
                                  .to_broadcast([P, 2 * HEADS, DK]), ALU.mult).then_inc(rot_a_done, 1)

            def feature(q, u):
                dve.wait_ge(er_done, q * 2 + (u + 3))
                dve.wait_ge(s1_done, q * 2 + (u + 1))
                dve.scalar_tensor_tensor(phi[:, u], er[:, u], 1.0, pos_part[:, u], ALU.min, ALU.add).then_inc(phi_done, 1)

            def copy_state(c, q, u):
                dve.tensor_tensor(state[:, u, c], ps_state[u][:], mask[:].unsqueeze(1).to_broadcast([P, 2, HW]), ALU.mult
                                  ).then_inc((m0_done, m1_done)[c], 1)

            def state0(q, u):
                dve.wait_ge(s0_done, q * 2 + (u + 1))
                dve.wait_ge(num_done, q * 2 + (u + 1))
                copy_state(0, q, u)

            def state1(q, u):
                dve.wait_ge(s1_done, q * 2 + (u + 3))
                copy_state(1, q, u)

            def divide(q, u):
                h = q * 2 + u
                dve.wait_ge(num_done, h + 3)
                dve.wait_ge(tanh_done, h + 1)
                dve.tensor_scalar(den[:].rearrange("p (k h) -> p k h", k=2), ps_num[:, :, P:], 1e-6, 2.0, ALU.add, ALU.mult
                                  ).then_inc(own_den, 1)
                dve.wait_ge(own_den, h * 2 + 1)
                dve.reciprocal(den[:], den[:]).then_inc(own_den, 1)
                dve.wait_ge(own_den, h * 2 + 2)
                dve.scalar_tensor_tensor(div[:].rearrange("p (h c) -> p h c", c=DK),
                                         row(tanh_all, q, u).rearrange("p (h c) -> p h c", c=DK), 1.0,
                                         den[:].unsqueeze(2).to_broadcast([P, HEADS, DK]), ALU.add, ALU.mult
                                         ).then_inc(own_div, 1)
                dve.wait_ge(own_div, h + 1)
                dve.tensor_tensor(o[:, u].rearrange("p (k c) -> p k c", k=2), ps_num[:, :, 0:P],
                                  div[:].rearrange("p (k c) -> p k c", k=2), ALU.mult).then_inc(o_done, 1)

            def add_out(q, u):
                h = q * 2 + u
                dve.wait_ge(wo_done, h + 2)
                dve.wait_ge(xtb_done, h + 1)
                dve.tensor_tensor(row(x2_all, q, u), ps_o[:, 1, :], row(x2_all, q, u), ALU.add).then_inc(x2_done, 1)

            pipelined(dve, T, [(10, add_out), (4, add_bias), (2, split_low), (6, state0), (7, state1), (5, feature),
                               (1, norm), (8, divide), (0, stat)])


def route(nc, tag, w, consts, x2_all, sums, h_rows, best, best_i, spare):
    with Scope(nc, tag) as s:
        ident, router = s.sb("ident", [P, P]), s.sb("router", [P, K, MOE_E])
        scale, rb = s.sb("scale", [P, D]), s.sb("rb", [P, MOE_E])
        neg_half, root = s.sb("neg_half", [P, T]), s.sb("root", [P, T])
        zeros = s.sb("zeros", [P, D])
        h = s.sb("h", [P, 2, 2, D])
        logits, top = s.sb("logits", [P, 2, 2, MOE_E]), s.sb("top", [P, 2, 2, 8])
        top_i = s.sb("top_i", [P, 2, 2, 8], U32)
        ht = s.sb("ht", [P, 2, 2, K, P])
        turned = [s.ps(f"turned{b}", (P, 2, K, P)) for b in range(2)]
        scored = [s.ps(f"scored{b}", (P, 2, MOE_E)) for b in range(2)]
        const_in, mean_done, root_done, h_done, turn_done, ht_done, score_done, logit_done = (
            s.sem(n) for n in ("const_in", "mean_done", "root_done", "h_done", "turn_done", "ht_done", "score_done",
                               "logit_done"))
        h_out = [s.sem(f"h_out{b}") for b in range(2)]
        pool_own, zeros_done, spare_out = s.sem("pool_own"), s.sem("zeros_done"), s.sem("spare_out")
        best_done, index_done, kept = s.sem("best_done"), s.sem("index_done"), s.sem("kept")
        block = s.enter_context(nc.Block())
        R = T // 2

        @block.sync
        def _(sp):
            for dst, src in ((ident[:], consts[:, C_IDENT:C_IDENT + P]), (router[:], w["router"]),
                             (scale[:], w["norm2"].to_broadcast([P, D])), (rb[:], w["router_b"].to_broadcast([P, MOE_E]))):
                sp.dma_start(dst, src).then_inc(const_in, 16)

            def store(q, u):
                sp.wait_ge(h_done, q * 2 + (u + 3))
                sp.dma_start(h_rows[ds((q * 2 + u) * (2 * P), 2 * P), :].rearrange("(t p) d -> p t d", p=P), h[:, u]
                             ).then_inc(h_out[u], 16)

            pipelined(sp, R, [(0, store)])
            for b in range(2):
                sp.wait_ge(h_out[b], 16 * (R // 2) + 16)

        @block.gpsimd
        def _(pool):
            pool.memset(zeros[:], 0.0).then_inc(zeros_done, 1)
            pool.memset(neg_half[:], -0.5).then_inc(pool_own, 1)
            pool.wait_ge(pool_own, 1)
            pool.wait_ge(mean_done, 1)
            for r in range(R):
                at = slice(2 * r, 2 * r + 2)
                pool.tensor_tensor(root[:, at], root[:, at], neg_half[:, at], ALU.pow).then_inc(root_done, 1)

        @block.tensor
        def _(pe):
            pe.wait_ge(const_in, 64)

            def turn(q, u):
                r = q * 2 + u
                pe.wait_ge(h_done, r + 3)
                pe.wait_ge(ht_done, r + 1)
                for t in range(2):
                    for k in range(K):
                        ins = pe.transpose(turned[u][:, t, k, :], h[:, u, t, k * P:(k + 1) * P], ident[:])
                ins.then_inc(turn_done, 1)

            def score(q, u):
                r = q * 2 + u
                pe.wait_ge(ht_done, r + 3)
                pe.wait_ge(logit_done, r + 1)
                for t in range(2):
                    for k in range(K):
                        ins = pe.matmul(scored[u][:, t, :], ht[:, u, t, k, :], router[:, k, :], start=(k == 0),
                                        stop=(k == K - 1))
                ins.then_inc(score_done, 1)

            pipelined(pe, R, [(0, turn), (1, score)])

        @block.scalar
        def _(act):
            act.wait_ge(zeros_done, 1)
            act.dma_start(spare.rearrange("(t p) d -> p t d", p=P),
                          zeros[:].unsqueeze(1).to_broadcast([P, MOE_CAP // P, D])).then_inc(spare_out, 16)

            def copy_turned(q, u):
                r = q * 2 + u
                act.wait_ge(turn_done, r + 3)
                act.wait_ge(score_done, r + 1)
                act.copy(ht[:, u], turned[u][:]).then_inc(ht_done, 1)

            pipelined(act, R, [(0, copy_turned)])
            act.wait_ge(spare_out, 16)

        @block.vector
        def _(dve):
            for sem, free in ((h_done, 2), (ht_done, 2), (logit_done, 2), (score_done, 2), (turn_done, 2),
                              (h_out[0], 16), (h_out[1], 16)):
                dve.sem_inc(sem, free)
            dve.tensor_scalar(root[:], sums[:], 1.0 / D, None, ALU.mult).then_inc(mean_done, 1)
            dve.wait_ge(const_in, 64)

            def norm(q, u):
                r = q * 2 + u
                dve.wait_ge(root_done, r + 1)
                dve.wait_ge(h_out[u], q * 16 + 16)
                dve.wait_ge(turn_done, r + 1)
                for t in range(2):
                    at = ds(r * 2 + t, 1)
                    ins = dve.scalar_tensor_tensor(h[:, u, t], x2_all[:, at, :].rearrange("p t d -> p (t d)"),
                                                   root[:, at], scale[:], ALU.mult, ALU.mult)
                ins.then_inc(h_done, 1)

            def keep_logits(q, u):
                r = q * 2 + u
                dve.wait_ge(score_done, r + 3)
                dve.tensor_tensor(logits[:, u], scored[u][:],
                                  rb[:].unsqueeze(1).to_broadcast([P, 2, MOE_E]), ALU.add).then_inc(logit_done, 1)

            def largest(q, u):
                r = q * 2 + u
                wait_apart(dve, logit_done, r + 3)
                for t in range(2):
                    ins = dve.max(top[:, u, t], logits[:, u, t])
                ins.then_inc(best_done, 1)
                wait_apart(dve, best_done, r + 1)
                for t in range(2):
                    ins = dve.max_index(top_i[:, u, t], top[:, u, t], logits[:, u, t])
                ins.then_inc(index_done, 1)
                dve.wait_ge(index_done, r + 1)
                dve.tensor_copy(best[:, ds(r * 2, 2), :], top[:, u])
                dve.tensor_copy(best_i[:, ds(r * 2, 2), :], top_i[:, u]).then_inc(kept, 1)
                dve.wait_ge(kept, r + 1)

            pipelined(dve, R, [(0, norm), (3, largest), (2, keep_logits)])
            dve.wait_ge(logit_done, R + 2)


def attention_and_moe(nc, tag, x_in, acc, w, consts):
    NT = MOE_CAP // P
    h_rows = nc.dram_tensor(f"{tag}_h", (N, D), F32, kind="Internal").ap()
    with Scope(nc, tag) as s:
        best, best_i = s.sb("best", [P, T, 8]), s.sb("best_i", [P, T, 8], U32)
        ids, ids2 = s.sb("ids", [P, MOE_E, NT], U32), s.sb("ids2", [P, MOE_E, NT], U32)
        gates = s.sb("gates", [P, MOE_E, NT])
        with Scope(nc, tag) as s2:
            x2_all, sums = s2.sb("x2_all", [P, T, D]), s2.sb("sums", [P, T])
            attention(nc, tag + "a", x_in, acc, w, consts, x2_all, sums)
            route(nc, tag + "r", w, consts, x2_all, sums, h_rows, best, best_i, acc[N:N + MOE_CAP])
        make_lists(nc, tag + "l", MOE_E, NT, consts, None, None, (best, best_i), ids, ids2, gates)
        run_experts(nc, tag + "e", MOE_E, NT, False, w["moe_w"], w["moe_b"], w["moe_db"], consts, h_rows, acc,
                    ids, ids2, gates)


def macaron(nc, w, out):
    acc1 = nc.dram_tensor("after_ffn1", (N, D), F32, kind="Internal").ap()
    acc2 = nc.dram_tensor("after_moe", (N + MOE_CAP, D), F32, kind="Internal").ap()
    ffn_w = (w["gate_w"], w["shared_w"], w["ffn_w"], w["ffn_b"], w["ffn_db"], w["consts"])
    ffn(nc, "f1", w["x"], acc1, *ffn_w)
    attention_and_moe(nc, "m", acc1, acc2, w, w["consts"])
    ffn(nc, "f2", acc2, out, *ffn_w)


def constants():
    c = np.zeros((P, C_ALL), np.float32)
    p = np.arange(P)
    c[:, C_IDENT:C_IDENT + P] = np.eye(P)
    c[:, C_TRI:C_TRI + P] = p[:, None] < p[None, :]
    c[:, C_IOTA:C_IOTA + P] = p
    c[:, C_TILE:C_TILE + T] = np.arange(T)
    c[:, C_SLOTHI:C_SLOTHI + 16] = np.arange(16)
    c[:, C_RESET:C_RESET + T] = np.arange(T) > 0
    c[:, C_ROW] = p
    c[:, C_MASK:C_MASK + P] = p[:, None] // DK == p[None, :] // DK
    c[:, C_MASK + P:] = p[:, None] // DK == np.arange(HALF)[None, :]
    return c


def rope_table():
    half = DK // 2
    inv = np.float32(1) / np.float32(10000) ** (np.arange(half, dtype=np.float32) / np.float32(half))
    ang = np.arange(SEQ, dtype=np.float32)[:, None] * inv[None, :]
    sin, cos = np.sin(ang), np.cos(ang)
    table = np.concatenate([cos, cos, -sin, sin], axis=1).astype(np.float32)
    return np.ascontiguousarray(table.reshape(SEQ // P, P, 4 * half).transpose(1, 0, 2))


def k_tiles(w):
    return np.ascontiguousarray(w.reshape(K, P, -1).transpose(1, 0, 2))


def hidden_slices(ins, down):
    E, F = down.shape[:2]
    parts = [w.reshape(E, F // P, P, K, P).transpose(0, 1, 4, 3, 2).reshape(E * F // P, P, D) for w in ins]
    return np.ascontiguousarray(np.concatenate(parts + [down.reshape(E * F // P, P, D)], axis=2))


def lay_out(i):
    a = {k.removeprefix("L0_"): np.asarray(v) for k, v in i.items()}
    by_tile = lambda b: b.reshape(b.shape[0], -1, P).transpose(0, 2, 1)
    o = {"consts": constants(), "x": np.ascontiguousarray(a["attn_x"].reshape(N, D))}
    o["gate_w"] = k_tiles(a["ffn_gate_w"].T)
    o["shared_w"] = hidden_slices([a["ffn_sh_gate_w"][None], a["ffn_sh_up_w"][None]],
                                  a["ffn_sh_down_w"].T[None])
    o["ffn_w"] = hidden_slices([a["ffn_gw"], a["ffn_up_w"]], a["ffn_down_w"].transpose(0, 2, 1))
    o["ffn_b"] = np.ascontiguousarray(np.concatenate([by_tile(a["ffn_gb"]), by_tile(a["ffn_up_b"])], axis=2))
    o["ffn_db"] = a["ffn_down_b"]
    o["moe_w"] = hidden_slices([a["attn_W1"].transpose(0, 2, 1)], a["attn_W2"])
    o["moe_b"], o["moe_db"] = np.ascontiguousarray(by_tile(a["attn_b1"])), a["attn_b2"]
    o["qkvg"] = k_tiles(np.concatenate([a[f"attn_W{c}"] for c in "qkvg"], axis=1))
    o["qkvg_b"] = np.concatenate([a[f"attn_b{c}"] for c in "qkvg"])[None]
    o["wo"], o["bo"] = k_tiles(a["attn_Wo"]), a["attn_bo"][None]
    o["norm1"] = np.ascontiguousarray(a["attn_norm1_scale"].reshape(K, P).T)
    o["norm2"] = a["attn_norm2_scale"][None]
    o["router"], o["router_b"] = k_tiles(a["attn_router_W"]), a["attn_router_b"][None]
    o["rope"] = rope_table()
    return o


def kernel(**inputs):
    import concourse.bacc as bacc
    from concourse.bass_utils import run_bass_kernel_spmd

    arrays = lay_out(inputs)
    nc = bacc.Bacc("TRN2", target_bir_lowering=False, num_devices=1)
    w = {n: nc.dram_tensor(f"in_{n}", a.shape, mybir.dt.from_np(a.dtype), kind="ExternalInput").ap()
         for n, a in arrays.items()}
    out = nc.dram_tensor("out", (N, D), F32, kind="ExternalOutput").ap()
    macaron(nc, w, out)
    r = run_bass_kernel_spmd(nc, [{f"in_{n}": a for n, a in arrays.items()}], core_ids=[0])
    return r.results[0]["out"].reshape(BATCH, SEQ, D)
```
